# Optimizing a Trainium2 kernel written in Bass

```python
import numpy as np
import jax
import jax.numpy as jnp

def _softmax(x, axis=-1):
    return jax.nn.softmax(x, axis=axis)

def _gelu(x):
    return jax.nn.gelu(x, approximate=True)

def _silu(x):
    return jax.nn.silu(x)

def _sigmoid(x):
    return jax.nn.sigmoid(x)

def _layernorm(x, axis=-1, eps=1e-05):
    m = jnp.mean(x, axis=axis, keepdims=True)
    v = jnp.var(x, axis=axis, keepdims=True)
    return (x - m) / jnp.sqrt(v + eps)

def _scatter_add(tgt, idx, src, axis=0):
    return tgt.at[idx].add(src)

def _segment_sum(src, seg, n):
    return jax.ops.segment_sum(src, seg, n)
kernel_name = 'mk_perceiver_d1_seqx_r8_c9f770'

def setup_inputs(seed: int=0):
    np.random.seed(seed)
    _w = jnp.asarray

    def _rec_inputs():
        import jax
        import jax.numpy as jnp
        _rk = jax.random.key(seed)
        x = -0.0005207 + 1.001 * jax.random.normal(jax.random.fold_in(_rk, 1), (4, 128, 128), jnp.float32)
        _lenS = 128 - jax.random.randint(jax.random.fold_in(_rk, 7), (4,), 0, max(1, 128 // 4) + 1, jnp.int32)
        _lenS2 = 2048 - jax.random.randint(jax.random.fold_in(_rk, 8), (4,), 0, max(1, 2048 // 4) + 1, jnp.int32)
        _ctx_1024P = jax.random.normal(jax.random.fold_in(_rk, 11), (4, 16, 128), jnp.float32)
        _ctx_1024c = jax.random.dirichlet(jax.random.fold_in(_rk, 511), 0.3 * jnp.ones((16,), jnp.float32), (4, 2048))
        _ctx_1024t = jnp.einsum('bsk,bkd->bsd', _ctx_1024c, _ctx_1024P)
        _ctx_1024t = _ctx_1024t * jax.lax.rsqrt(jnp.mean(jnp.square(_ctx_1024t)) + 1e-12) * 0.953939
        ctx_1024 = -0.000514642 + 1.00011 * (_ctx_1024t + 0.3 * jax.random.normal(jax.random.fold_in(_rk, 611), (4, 2048, 128), jnp.float32))
        return (x, ctx_1024)
    x, ctx_1024 = _rec_inputs()

    def _L0_xattn_setup():
        import math
        import jax, jax.numpy as jnp
        import numpy as np
        L, D, H, DH = (6, 128, 16, 64)
        INNER = 4 * D
        ROT = 32
        SCALE = 16.0
        NUM_BUCKETS, MAX_DIST = (32, 128)
        EPS = 1e-05

        def layernorm(x, g, stable=False):
            if stable:
                x = x / jax.lax.stop_gradient(jnp.max(x, axis=-1, keepdims=True))
            mean = jnp.mean(x, axis=-1, keepdims=True)
            var = jnp.var(x, axis=-1, keepdims=True)
            return (x - mean) * jax.lax.rsqrt(var + EPS) * g

        def l2norm(x):
            return x / jnp.clip(jnp.linalg.norm(x, axis=-1, keepdims=True), 1e-12)

        def rel_pos_bias(n_q, n_k, emb):
            rel = jnp.arange(n_k)[None, :] - jnp.arange(n_q)[:, None]
            neg = jnp.maximum(-rel, 0)
            max_exact = NUM_BUCKETS // 2
            is_small = neg < max_exact
            safe = jnp.maximum(neg, 1).astype(jnp.float32)
            val_large = max_exact + (jnp.log(safe / max_exact) / math.log(MAX_DIST / max_exact) * (NUM_BUCKETS - max_exact)).astype(jnp.int32)
            val_large = jnp.minimum(val_large, NUM_BUCKETS - 1)
            bucket = jnp.where(is_small, neg, val_large)
            return jnp.transpose(emb[bucket], (2, 0, 1))

        def rotary_freqs(n):
            inv_freq = 1.0 / 10000.0 ** (jnp.arange(0, ROT, 2, dtype=jnp.float32) / ROT)
            f = jnp.arange(n, dtype=jnp.float32)[:, None] * inv_freq[None, :]
            return jnp.repeat(f, 2, axis=-1)

        def rotate_half(x):
            shape = x.shape
            x = x.reshape(shape[:-1] + (-1, 2))
            x1, x2 = (x[..., 0], x[..., 1])
            return jnp.stack((-x2, x1), axis=-1).reshape(shape)

        def apply_rotary(t, freqs):
            t_rot, t_pass = (t[..., :ROT], t[..., ROT:])
            t_rot = t_rot * jnp.cos(freqs) + rotate_half(t_rot) * jnp.sin(freqs)
            return jnp.concatenate((t_rot, t_pass), axis=-1)

        def attention(x, kv_inp, g, wq, wkv, wo, out_g, null_kv, causal, attn_bias, freqs):
            b, n, _ = x.shape
            xn = layernorm(x, g)
            kv = xn if kv_inp is None else kv_inp
            q = (xn @ wq).reshape(b, n, H, DH).transpose(0, 2, 1, 3) * SCALE
            k, v = jnp.split(kv @ wkv, 2, axis=-1)
            if freqs is not None:
                q = apply_rotary(q, freqs)
                k = apply_rotary(k, freqs)
            nk = jnp.broadcast_to(null_kv[0], (b, 1, DH))
            nv = jnp.broadcast_to(null_kv[1], (b, 1, DH))
            k = jnp.concatenate((nk, k), axis=1)
            v = jnp.concatenate((nv, v), axis=1)
            q = l2norm(q) * math.sqrt(SCALE)
            k = l2norm(k) * math.sqrt(SCALE)
            sim = jnp.einsum('bhid,bjd->bhij', q, k)
            if attn_bias is not None:
                sim = sim + attn_bias
            if causal:
                i, j = (sim.shape[-2], sim.shape[-1])
                cmask = jnp.triu(jnp.ones((i, j), bool), j - i + 1)
                sim = jnp.where(cmask, -jnp.finfo(sim.dtype).max, sim)
            attn = jax.nn.softmax(sim.astype(jnp.float32), axis=-1).astype(sim.dtype)
            out = jnp.einsum('bhij,bjd->bhid', attn, v)
            out = out.transpose(0, 2, 1, 3).reshape(b, n, H * DH)
            return layernorm(out @ wo, out_g)

        def feedforward(x, g, w1, w2):
            h = layernorm(x, g)
            u, gate = jnp.split(h @ w1, 2, axis=-1)
            return u * jax.nn.silu(gate) @ w2

        def _fwd(x, context, rel_pos_emb, sa_norm_g, sa_wq, sa_wkv, sa_wo, sa_out_g, sa_null_kv, ca_norm_g, ca_wq, ca_wkv, ca_wo, ca_out_g, ca_null_kv, ff_norm_g, ff_w1, ff_w2, final_g, proj_w):
            n = x.shape[1]
            bias = rel_pos_bias(n, n + 1, rel_pos_emb)
            freqs = rotary_freqs(n)
            for l in range(L):
                x = attention(x, None, sa_norm_g[l], sa_wq[l], sa_wkv[l], sa_wo[l], sa_out_g[l], sa_null_kv[l], True, bias, freqs) + x
                x = attention(x, context, ca_norm_g[l], ca_wq[l], ca_wkv[l], ca_wo[l], ca_out_g[l], ca_null_kv[l], False, None, None) + x
                x = feedforward(x, ff_norm_g[l], ff_w1[l], ff_w2[l]) + x
            out = layernorm(x, final_g, stable=True)
            return out @ proj_w
        key = jax.random.key(seed)
        ks = jax.random.split(key, 16)
        B, N, M = (4, 64, 64)
        s = 0.02
        return {'x': jax.random.normal(ks[0], (B, N, D), jnp.float32), 'context': jax.random.normal(ks[1], (B, M, D), jnp.float32), 'rel_pos_emb': jax.random.normal(ks[2], (NUM_BUCKETS, H), jnp.float32), 'sa_norm_g': jnp.ones((L, D), jnp.float32), 'sa_wq': jax.random.normal(ks[3], (L, D, H * DH), jnp.float32) * s, 'sa_wkv': jax.random.normal(ks[4], (L, D, 2 * DH), jnp.float32) * s, 'sa_wo': jax.random.normal(ks[5], (L, H * DH, D), jnp.float32) * s, 'sa_out_g': jnp.ones((L, D), jnp.float32), 'sa_null_kv': jax.random.normal(ks[6], (L, 2, DH), jnp.float32), 'ca_norm_g': jnp.ones((L, D), jnp.float32), 'ca_wq': jax.random.normal(ks[7], (L, D, H * DH), jnp.float32) * s, 'ca_wkv': jax.random.normal(ks[8], (L, D, 2 * DH), jnp.float32) * s, 'ca_wo': jax.random.normal(ks[9], (L, H * DH, D), jnp.float32) * s, 'ca_out_g': jnp.ones((L, D), jnp.float32), 'ca_null_kv': jax.random.normal(ks[10], (L, 2, DH), jnp.float32), 'ff_norm_g': jnp.ones((L, D), jnp.float32), 'ff_w1': jax.random.normal(ks[11], (L, D, 2 * INNER), jnp.float32) * s, 'ff_w2': jax.random.normal(ks[12], (L, INNER, D), jnp.float32) * s, 'final_g': jnp.ones((D,), jnp.float32), 'proj_w': jax.random.normal(ks[13], (D, D), jnp.float32) * s}
    _L0_xattn_all = _L0_xattn_setup()
    _L0_xattn_in = {k: v for k, v in _L0_xattn_all.items() if k in ('rel_pos_emb', 'sa_norm_g', 'sa_wq', 'sa_wkv', 'sa_wo', 'sa_out_g', 'sa_null_kv', 'ca_norm_g', 'ca_wq', 'ca_wkv', 'ca_wo', 'ca_out_g', 'ca_null_kv', 'ff_norm_g', 'ff_w1', 'ff_w2', 'final_g', 'proj_w')}
    del _L0_xattn_all

    def _L0_attn_setup():
        import jax, jax.numpy as jnp
        import numpy as np
        import math
        D_MODEL = 128
        NUM_HEADS = 16
        HEAD = D_MODEL // NUM_HEADS
        EPS = 1e-05

        def _layernorm(x, w, b):
            mean = jnp.mean(x, axis=-1, keepdims=True)
            var = jnp.var(x, axis=-1, keepdims=True)
            return (x - mean) * w / jnp.sqrt(var + EPS) + b
        key = jax.random.key(seed)
        ks = jax.random.split(key, 5)
        x = jax.random.normal(ks[0], (2, 256, D_MODEL), dtype=jnp.float32)
        wq = jax.random.uniform(ks[1], (NUM_HEADS, D_MODEL, HEAD), dtype=jnp.float32) * 0.02
        wk = jax.random.uniform(ks[2], (NUM_HEADS, D_MODEL, HEAD), dtype=jnp.float32) * 0.02
        wv = jax.random.uniform(ks[3], (NUM_HEADS, D_MODEL, HEAD), dtype=jnp.float32) * 0.02
        wo = jax.random.uniform(ks[4], (D_MODEL, D_MODEL), dtype=jnp.float32) * 0.02
        ln_w = jnp.ones((D_MODEL,), dtype=jnp.float32)
        ln_b = jnp.zeros((D_MODEL,), dtype=jnp.float32)
        return {'x': x, 'ln_w': ln_w, 'ln_b': ln_b, 'wq': wq, 'wk': wk, 'wv': wv, 'wo': wo}
    _L0_attn_all = _L0_attn_setup()
    _L0_attn_in = {k: v for k, v in _L0_attn_all.items() if k in ('ln_w', 'ln_b', 'wq', 'wk', 'wv', 'wo')}
    del _L0_attn_all

    def _L0_ffn_setup():
        import jax, jax.numpy as jnp
        import numpy as np
        from jax import lax
        T, B, I, M, O = (32, 64, 128, 128, 128)

        def _xavier(key, shape):
            fan_out, fan_in = shape
            limit = float(np.sqrt(6.0 / (fan_in + fan_out)))
            return jax.random.uniform(key, shape, jnp.float32, -limit, limit)
        key = jax.random.key(seed)
        ks = jax.random.split(key, 9)
        x = jax.random.normal(ks[0], (T, B, I), jnp.float32)
        return {'x': x, 'wf': _xavier(ks[1], (M, I)), 'uf': _xavier(ks[2], (M, M)), 'bf': jnp.zeros((M,), jnp.float32), 'wi': _xavier(ks[3], (M, I)), 'ui': _xavier(ks[4], (M, M)), 'bi': jnp.zeros((M,), jnp.float32), 'wc': _xavier(ks[5], (M, I)), 'uc': _xavier(ks[6], (M, M)), 'bc': jnp.zeros((M,), jnp.float32), 'wo': _xavier(ks[7], (O, I)), 'uo': _xavier(ks[8], (O, M)), 'bo': jnp.zeros((O,), jnp.float32), 'in_c': jnp.zeros((M,), jnp.float32)}
    _L0_ffn_all = _L0_ffn_setup()
    _L0_ffn_in = {k: v for k, v in _L0_ffn_all.items() if k in ('wf', 'uf', 'bf', 'wi', 'ui', 'bi', 'wc', 'uc', 'bc', 'wo', 'uo', 'bo', 'in_c')}
    del _L0_ffn_all
    return {'x': x, 'ctx_1024': ctx_1024, 'L0_xattn_rel_pos_emb': _L0_xattn_in['rel_pos_emb'], 'L0_xattn_sa_norm_g': _L0_xattn_in['sa_norm_g'], 'L0_xattn_sa_wq': _L0_xattn_in['sa_wq'], 'L0_xattn_sa_wkv': _L0_xattn_in['sa_wkv'], 'L0_xattn_sa_wo': _L0_xattn_in['sa_wo'], 'L0_xattn_sa_out_g': _L0_xattn_in['sa_out_g'], 'L0_xattn_sa_null_kv': _L0_xattn_in['sa_null_kv'], 'L0_xattn_ca_norm_g': _L0_xattn_in['ca_norm_g'], 'L0_xattn_ca_wq': _L0_xattn_in['ca_wq'], 'L0_xattn_ca_wkv': _L0_xattn_in['ca_wkv'], 'L0_xattn_ca_wo': _L0_xattn_in['ca_wo'], 'L0_xattn_ca_out_g': _L0_xattn_in['ca_out_g'], 'L0_xattn_ca_null_kv': _L0_xattn_in['ca_null_kv'], 'L0_xattn_ff_norm_g': _L0_xattn_in['ff_norm_g'], 'L0_xattn_ff_w1': _L0_xattn_in['ff_w1'], 'L0_xattn_ff_w2': _L0_xattn_in['ff_w2'], 'L0_xattn_final_g': _L0_xattn_in['final_g'], 'L0_xattn_proj_w': _L0_xattn_in['proj_w'], 'L0_attn_ln_w': _L0_attn_in['ln_w'], 'L0_attn_ln_b': _L0_attn_in['ln_b'], 'L0_attn_wq': _L0_attn_in['wq'], 'L0_attn_wk': _L0_attn_in['wk'], 'L0_attn_wv': _L0_attn_in['wv'], 'L0_attn_wo': _L0_attn_in['wo'], 'L0_ffn_wf': _L0_ffn_in['wf'], 'L0_ffn_uf': _L0_ffn_in['uf'], 'L0_ffn_bf': _L0_ffn_in['bf'], 'L0_ffn_wi': _L0_ffn_in['wi'], 'L0_ffn_ui': _L0_ffn_in['ui'], 'L0_ffn_bi': _L0_ffn_in['bi'], 'L0_ffn_wc': _L0_ffn_in['wc'], 'L0_ffn_uc': _L0_ffn_in['uc'], 'L0_ffn_bc': _L0_ffn_in['bc'], 'L0_ffn_wo': _L0_ffn_in['wo'], 'L0_ffn_uo': _L0_ffn_in['uo'], 'L0_ffn_bo': _L0_ffn_in['bo'], 'L0_ffn_in_c': _L0_ffn_in['in_c']}

def reference(x, ctx_1024, L0_xattn_rel_pos_emb, L0_xattn_sa_norm_g, L0_xattn_sa_wq, L0_xattn_sa_wkv, L0_xattn_sa_wo, L0_xattn_sa_out_g, L0_xattn_sa_null_kv, L0_xattn_ca_norm_g, L0_xattn_ca_wq, L0_xattn_ca_wkv, L0_xattn_ca_wo, L0_xattn_ca_out_g, L0_xattn_ca_null_kv, L0_xattn_ff_norm_g, L0_xattn_ff_w1, L0_xattn_ff_w2, L0_xattn_final_g, L0_xattn_proj_w, L0_attn_ln_w, L0_attn_ln_b, L0_attn_wq, L0_attn_wk, L0_attn_wv, L0_attn_wo, L0_ffn_wf, L0_ffn_uf, L0_ffn_bf, L0_ffn_wi, L0_ffn_ui, L0_ffn_bi, L0_ffn_wc, L0_ffn_uc, L0_ffn_bc, L0_ffn_wo, L0_ffn_uo, L0_ffn_bo, L0_ffn_in_c):
    import jax
    import jax.numpy as jnp

    def _L0_xattn_ref(x, context, rel_pos_emb, sa_norm_g, sa_wq, sa_wkv, sa_wo, sa_out_g, sa_null_kv, ca_norm_g, ca_wq, ca_wkv, ca_wo, ca_out_g, ca_null_kv, ff_norm_g, ff_w1, ff_w2, final_g, proj_w):
        import math
        import jax, jax.numpy as jnp
        import numpy as np
        L, D, H, DH = (6, 128, 16, 64)
        INNER = 4 * D
        ROT = 32
        SCALE = 16.0
        NUM_BUCKETS, MAX_DIST = (32, 128)
        EPS = 1e-05

        def layernorm(x, g, stable=False):
            if stable:
                x = x / jax.lax.stop_gradient(jnp.max(x, axis=-1, keepdims=True))
            mean = jnp.mean(x, axis=-1, keepdims=True)
            var = jnp.var(x, axis=-1, keepdims=True)
            return (x - mean) * jax.lax.rsqrt(var + EPS) * g

        def l2norm(x):
            return x / jnp.clip(jnp.linalg.norm(x, axis=-1, keepdims=True), 1e-12)

        def rel_pos_bias(n_q, n_k, emb):
            rel = jnp.arange(n_k)[None, :] - jnp.arange(n_q)[:, None]
            neg = jnp.maximum(-rel, 0)
            max_exact = NUM_BUCKETS // 2
            is_small = neg < max_exact
            safe = jnp.maximum(neg, 1).astype(jnp.float32)
            val_large = max_exact + (jnp.log(safe / max_exact) / math.log(MAX_DIST / max_exact) * (NUM_BUCKETS - max_exact)).astype(jnp.int32)
            val_large = jnp.minimum(val_large, NUM_BUCKETS - 1)
            bucket = jnp.where(is_small, neg, val_large)
            return jnp.transpose(emb[bucket], (2, 0, 1))

        def rotary_freqs(n):
            inv_freq = 1.0 / 10000.0 ** (jnp.arange(0, ROT, 2, dtype=jnp.float32) / ROT)
            f = jnp.arange(n, dtype=jnp.float32)[:, None] * inv_freq[None, :]
            return jnp.repeat(f, 2, axis=-1)

        def rotate_half(x):
            shape = x.shape
            x = x.reshape(shape[:-1] + (-1, 2))
            x1, x2 = (x[..., 0], x[..., 1])
            return jnp.stack((-x2, x1), axis=-1).reshape(shape)

        def apply_rotary(t, freqs):
            t_rot, t_pass = (t[..., :ROT], t[..., ROT:])
            t_rot = t_rot * jnp.cos(freqs) + rotate_half(t_rot) * jnp.sin(freqs)
            return jnp.concatenate((t_rot, t_pass), axis=-1)

        def attention(x, kv_inp, g, wq, wkv, wo, out_g, null_kv, causal, attn_bias, freqs):
            b, n, _ = x.shape
            xn = layernorm(x, g)
            kv = xn if kv_inp is None else kv_inp
            q = (xn @ wq).reshape(b, n, H, DH).transpose(0, 2, 1, 3) * SCALE
            k, v = jnp.split(kv @ wkv, 2, axis=-1)
            if freqs is not None:
                q = apply_rotary(q, freqs)
                k = apply_rotary(k, freqs)
            nk = jnp.broadcast_to(null_kv[0], (b, 1, DH))
            nv = jnp.broadcast_to(null_kv[1], (b, 1, DH))
            k = jnp.concatenate((nk, k), axis=1)
            v = jnp.concatenate((nv, v), axis=1)
            q = l2norm(q) * math.sqrt(SCALE)
            k = l2norm(k) * math.sqrt(SCALE)
            sim = jnp.einsum('bhid,bjd->bhij', q, k)
            if attn_bias is not None:
                sim = sim + attn_bias
            if causal:
                i, j = (sim.shape[-2], sim.shape[-1])
                cmask = jnp.triu(jnp.ones((i, j), bool), j - i + 1)
                sim = jnp.where(cmask, -jnp.finfo(sim.dtype).max, sim)
            attn = jax.nn.softmax(sim.astype(jnp.float32), axis=-1).astype(sim.dtype)
            out = jnp.einsum('bhij,bjd->bhid', attn, v)
            out = out.transpose(0, 2, 1, 3).reshape(b, n, H * DH)
            return layernorm(out @ wo, out_g)

        def feedforward(x, g, w1, w2):
            h = layernorm(x, g)
            u, gate = jnp.split(h @ w1, 2, axis=-1)
            return u * jax.nn.silu(gate) @ w2

        def _fwd(x, context, rel_pos_emb, sa_norm_g, sa_wq, sa_wkv, sa_wo, sa_out_g, sa_null_kv, ca_norm_g, ca_wq, ca_wkv, ca_wo, ca_out_g, ca_null_kv, ff_norm_g, ff_w1, ff_w2, final_g, proj_w):
            n = x.shape[1]
            bias = rel_pos_bias(n, n + 1, rel_pos_emb)
            freqs = rotary_freqs(n)
            for l in range(L):
                x = attention(x, None, sa_norm_g[l], sa_wq[l], sa_wkv[l], sa_wo[l], sa_out_g[l], sa_null_kv[l], True, bias, freqs) + x
                x = attention(x, context, ca_norm_g[l], ca_wq[l], ca_wkv[l], ca_wo[l], ca_out_g[l], ca_null_kv[l], False, None, None) + x
                x = feedforward(x, ff_norm_g[l], ff_w1[l], ff_w2[l]) + x
            out = layernorm(x, final_g, stable=True)
            return out @ proj_w
        return _fwd(x, context, rel_pos_emb, sa_norm_g, sa_wq, sa_wkv, sa_wo, sa_out_g, sa_null_kv, ca_norm_g, ca_wq, ca_wkv, ca_wo, ca_out_g, ca_null_kv, ff_norm_g, ff_w1, ff_w2, final_g, proj_w)

    def _L0_attn_ref(x, ln_w, ln_b, wq, wk, wv, wo):
        import jax, jax.numpy as jnp
        import numpy as np
        import math
        D_MODEL = 128
        NUM_HEADS = 16
        HEAD = D_MODEL // NUM_HEADS
        EPS = 1e-05

        def _layernorm(x, w, b):
            mean = jnp.mean(x, axis=-1, keepdims=True)
            var = jnp.var(x, axis=-1, keepdims=True)
            return (x - mean) * w / jnp.sqrt(var + EPS) + b
        y = _layernorm(x, ln_w, ln_b)
        seq_len = y.shape[-2]
        q = jnp.einsum('bsd,hde->bhse', y, wq)
        k = jnp.einsum('bsd,hde->bhse', y, wk)
        v = jnp.einsum('bsd,hde->bhse', y, wv)
        scores = jnp.einsum('bhse,bhte->bhst', q, k) / math.sqrt(HEAD)
        causal = jnp.triu(jnp.full((seq_len, seq_len), -jnp.inf, dtype=scores.dtype), k=1)
        scores = scores + causal
        weights = jax.nn.softmax(scores, axis=-1)
        attn = jnp.einsum('bhst,bhte->bshe', weights, v)
        attn = attn.reshape(*attn.shape[:-2], -1)
        out = attn @ wo
        return out + x

    def _L0_ffn_ref(x, wf, uf, bf, wi, ui, bi, wc, uc, bc, wo, uo, bo, in_c):
        import jax, jax.numpy as jnp
        import numpy as np
        from jax import lax
        T, B, I, M, O = (32, 64, 128, 128, 128)

        def _xavier(key, shape):
            fan_out, fan_in = shape
            limit = float(np.sqrt(6.0 / (fan_in + fan_out)))
            return jax.random.uniform(key, shape, jnp.float32, -limit, limit)
        batch = x.shape[1]
        c0 = jnp.broadcast_to(in_c, (batch, in_c.shape[0]))

        def step(c, xt):
            ft = jax.nn.sigmoid(xt @ wf.T + c @ uf.T + bf)
            it = jax.nn.sigmoid(xt @ wi.T + c @ ui.T + bi)
            gt = jnp.tanh(xt @ wc.T + c @ uc.T + bc)
            c = ft * c + it * gt
            return (c, None)
        c_final, _ = lax.scan(step, c0, x)
        h = jnp.tanh(jnp.einsum('tbi,oi->tbo', x, wo) + c_final @ uo.T + bo)
        return h
    x = x + _L0_xattn_ref(_layernorm(x, axis=-1), ctx_1024, L0_xattn_rel_pos_emb, L0_xattn_sa_norm_g, L0_xattn_sa_wq, L0_xattn_sa_wkv, L0_xattn_sa_wo, L0_xattn_sa_out_g, L0_xattn_sa_null_kv, L0_xattn_ca_norm_g, L0_xattn_ca_wq, L0_xattn_ca_wkv, L0_xattn_ca_wo, L0_xattn_ca_out_g, L0_xattn_ca_null_kv, L0_xattn_ff_norm_g, L0_xattn_ff_w1, L0_xattn_ff_w2, L0_xattn_final_g, L0_xattn_proj_w)
    x = x + _L0_attn_ref(_layernorm(x, axis=-1), L0_attn_ln_w, L0_attn_ln_b, L0_attn_wq, L0_attn_wk, L0_attn_wv, L0_attn_wo)
    x = x + _L0_ffn_ref(_layernorm(x, axis=-1), L0_ffn_wf, L0_ffn_uf, L0_ffn_bf, L0_ffn_wi, L0_ffn_ui, L0_ffn_bi, L0_ffn_wc, L0_ffn_uc, L0_ffn_bc, L0_ffn_wo, L0_ffn_uo, L0_ffn_bo, L0_ffn_in_c)
    return x

_drawn_inputs = setup_inputs


def setup_inputs(seed=0):
    import zlib

    import numpy as np

    out = dict(_drawn_inputs(seed))
    spreads = {'L0_xattn_sa_norm_g': (1.0, 0.2),
     'L0_xattn_sa_out_g': (1.0, 0.2),
     'L0_xattn_ca_norm_g': (1.0, 0.571),
     'L0_xattn_ca_out_g': (1.0, 0.2),
     'L0_xattn_ff_norm_g': (1.0, 0.6),
     'L0_xattn_final_g': (1.0, 0.2),
     'L0_attn_ln_w': (1.0, 0.6),
     'L0_attn_ln_b': (0.0, 0.8),
     'L0_ffn_bf': (0.0, 2.0),
     'L0_ffn_bi': (0.0, 2.0),
     'L0_ffn_bc': (0.0, 1.551),
     'L0_ffn_bo': (0.0, 0.8),
     'L0_ffn_in_c': (0.0, 2.0)}
    factors = {'L0_xattn_ca_null_kv': 4.898,
     'L0_xattn_ff_w1': 8.0,
     'L0_xattn_ff_w2': 8.0,
     'L0_attn_wq': 8.0,
     'L0_attn_wk': 8.0,
     'L0_attn_wv': 8.0,
     'L0_attn_wo': 8.0,
     'L0_ffn_uf': 3.615,
     'L0_ffn_wf': 5.053,
     'L0_ffn_wi': 3.72,
     'L0_ffn_ui': 5.213}
    for name, (base, spread) in spreads.items():
        noise = np.random.default_rng([zlib.crc32(name.encode()), seed]).standard_normal(out[name].shape)
        drawn = base * np.exp(spread * noise) if base else spread * noise
        out[name] = jnp.asarray(drawn.astype(out[name].dtype))
    for name, factor in factors.items():
        out[name] = (out[name] * factor).astype(out[name].dtype)
    return out
```

```python
from contextlib import ExitStack

import concourse.bass as bass
from concourse import mybir

ALU = mybir.AluOpType
ACT = mybir.ActivationFunctionType
F32 = mybir.dt.float32
F16 = mybir.dt.float16
AX_X = mybir.AxisListType.X

L, B, N, D = 6, 4, 128, 128
H, DH, ROT = 16, 64, 32
M = 2048
KT_N = M // 128
FF = 512
NBUCK = 32
EPS = 1e-5
GH = 4
NG = H // GH
QCOL = GH * N
UNIT = 1024.0
SIM_SCALE = 16.0 / (UNIT * UNIT)
RUNS = L * B

W_SAQ, W_SAKV, W_SAO, W_CAQ, W_CAKV, W_CAO, W_FF1, W_FF2, W_END = 0, 1024, 1152, 2176, 3200, 3328, 4352, 5376, 5888
T_PROJ, T_Q, T_K, T_V, T_O, T_WF, T_WI, T_WC, T_UF, T_UI, T_UC, T_WO, T_UO = range(13)
C_END = 592
C_FINAL, C_LNW, C_LNB, C_BF, C_BI, C_BC, C_INC = range(7)


class Links:

    def __init__(self, eng, sem, base):
        self.eng, self.sem, self.base, self.k = eng, sem, base, 0

    def __call__(self, ins):
        self.k += 1
        ins.then_inc(self.sem, 1)
        self.eng.wait_ge(self.sem, self.base + self.k)


def build(nc, x, ctxT, wpack, gcols, gout, null_k, null_v, tail_w, tail_cols, bo, emb,
          c_pack, out):
    with ExitStack() as ctx:
        def sb(name, shape, dt=F32):
            return ctx.enter_context(nc.sbuf_tensor(name, shape, dt))

        def psum(name, shape):
            return ctx.enter_context(nc.psum_tensor(name, shape, F32))

        sems = {}

        def sem(name):
            if name not in sems:
                sems[name] = ctx.enter_context(nc.semaphore(name))
            return sems[name]

        def dram(name, shape):
            return nc.dram_tensor(name, shape, F32, kind="Internal").ap()

        psS = psum("psS", [128, 4, 512])
        psO = psum("psO", [128, 2, 512])
        psL = psum("psL", [128, 2, 512])
        psLh = [psL[:, i, :].bitcast(F16).rearrange("p (t c) -> p t c", c=128) for i in range(2)]

        C = sb("C", [128, C_END])
        ident = C[:, 0:128]
        flip = C[:, 128:256]
        cmask = C[:, 256:384]
        onehot = C[0:NBUCK, 384:512]
        cosT = C[:, 512:544]
        sinT = C[:, 544:576]
        hmask = C[:, 576:592]
        ident16 = sb("ident16", [128, 128], F16)
        emb_sb = sb("emb_sb", [NBUCK, H])
        neghalf = sb("neghalf", [128, 17])
        tiny = sb("tiny", [128, 17])
        gcol = sb("gcol", [128, L, 3])
        gout_b = sb("gout_b", [128, L, 2, D])
        W = sb("W", [128, 2, W_END])
        TW = sb("TW", [128, 13, 128])
        TC = sb("TC", [128, 7])
        bo_row = sb("bo_row", [1, 128])
        ones = sb("ones", [1, 128])
        x_in = sb("x_in", [128, B, D])
        xs = sb("xs", [128, B, D])
        xr = sb("xr", [128, D])
        fence = sb("fence", [1, 1])
        stats = sb("stats", [128, 6])
        mv = sb("mv", [128, 2])
        ve = sb("ve", [128, 1])
        rstd = sb("rstd", [128, 1])
        xn = sb("xn", [128, D])
        xnT = sb("xnT", [128, 128])
        qraw = sb("qraw", [128, 17, DH])
        qsq = sb("qsq", [128, 17, DH])
        ss = sb("ss", [128, 17])
        ssc = sb("ssc", [128, 17])
        rn = sb("rn", [128, 17])
        rota = sb("rota", [128, 17, ROT])
        rotb = sb("rotb", [128, 17, ROT])
        qn = sb("qn", [128, 17, DH])
        qs_all = sb("qs_all", [128, 17 * 2 * DH + DH], F16)
        qs = qs_all[:, 0:17 * 2 * DH].rearrange("p (h a d) -> p h a d", a=2, d=DH)
        ks_self = qs_all[:, 16 * 2 * DH:]
        QT = sb("QT", [128, H * N], F16)
        KTs = sb("KTs", [128, 2, 128], F16)
        Vs = sb("Vs", [128, 128])
        ctx_sb = sb("ctx_sb", [128, M])
        kraw = sb("kraw", [128, KT_N, DH])
        ksq = sb("ksq", [128, KT_N, DH])
        kn = sb("kn", [128, KT_N, DH])
        ks = sb("ks", [128, KT_N, 3, DH], F16)
        KT = sb("KT", [128, 2, M], F16)
        V = sb("V", [128, KT_N, 128])
        nk = sb("nk", [2 * L, DH])
        nksq = sb("nksq", [2 * L, DH])
        nkn = sb("nkn", [2 * L, DH])
        nks = sb("nks", [2 * L, 3, DH], F16)
        NKC = sb("NKC", [128, 2, 2 * L], F16)
        nkc = sb("nkc", [128, 2], F16)
        NV = sb("NV", [1, 2 * L, 128])
        nv = sb("nv", [1, 128])
        ET = sb("ET", [128, H * N])
        E0 = sb("E0", [1, H * N])
        P = sb("P", [128, 4, QCOL])
        rden = sb("rden", [64, QCOL])
        oT = sb("oT", [128, H // 2, N])
        eg = sb("eg", [128, FF])
        eg1 = sb("eg1", [128, FF])
        hu = sb("hu", [128, FF])
        hT = sb("hT", [128, FF])
        yb = sb("yb", [128, D])
        tq, tk, tv = (sb(name, [128, 128]) for name in ("tq", "tk", "tv"))
        zT = sb("zT", [128, B, 128])
        cT, cf, ig, fT, iT, gT = (sb(name, [128, 128]) for name in ("cT", "cf", "ig", "fT", "iT", "gT"))
        hy = sb("hy", [128, B, D])

        ts = V[:]
        tkm = P[:].rearrange("p a (b c) -> p (a b) c", c=N)
        toeplitz = [kraw[:].rearrange("p a d -> p (a d)"), ksq[:].rearrange("p a d -> p (a d)")]
        rowmax = V[:].rearrange("p a b -> p (a b)")
        biasW = dram("biasW", [H, 256])
        biasM = dram("biasM", [H, N])
        bias0 = dram("bias0", [H, N])

        block = ctx.enter_context(nc.Block())

        LINKS = 35
        POOL_CONSTS = 5
        TAIL_LINKS = 25
        SA_N, CA_N = 2, KT_N + 1

        @block.sync
        def _(sp):
            for dst, src in ((C[:], c_pack), (emb_sb[:], emb), (gcol[:], gcols), (nk[:], null_k),
                             (NV[:, :, 0:DH], null_v)):
                sp.dma_start(dst, src).then_inc(sem("consts_in"), 16)
            sp.dma_start(x_in[:], x.rearrange("b p d -> p b d")).then_inc(sem("x_in"), 16)
            sp.dma_start(gout_b[:], bass.AP(gout.tensor, 0, [[0, 128], [1, L * 2 * D]])).then_inc(sem("gout_in"), 16)
            sp.dma_start(W[:, 0, :], wpack[0]).then_inc(sem("w_in"), 16)
            sp.wait_ge(sem("bias_ready"), 2)
            sp.dma_start(biasW, ET[0:H, 0:256]).then_inc(sem("bias_out"), 16)
            sp.dma_start(biasM, ET[0:H, 256:384]).then_inc(sem("bias_out"), 16)
            sp.dma_start(bias0, ET[0:H, 384:512]).then_inc(sem("bias_out"), 16)
            sp.wait_ge(sem("bias_out"), 48)
            for i in range(2):
                sp.dma_start(toeplitz[i].rearrange("p (h n) -> p h n", n=N),
                             bass.AP(biasW.tensor, 256 * (H // 2) * i, [[1, 128], [256, H // 2], [1, N]])).then_inc(sem("bias_in"), 16)
            sp.dma_start(rowmax, bass.AP(biasM.tensor, 0, [[0, 128], [1, H * N]])).then_inc(sem("bias_in"), 16)
            sp.dma_start(E0[:], bass.AP(bias0.tensor, 0, [[0, 1], [1, H * N]])).then_inc(sem("bias_in"), 16)
            sp.dma_start(W[:, 1, :], wpack[1]).then_inc(sem("w_in"), 16)
            sp.dma_start(TW[:], tail_w).then_inc(sem("tail_in"), 16)
            sp.dma_start(TC[:], tail_cols).then_inc(sem("tail_in"), 16)
            sp.dma_start(bo_row[:], bo).then_inc(sem("tail_in"), 16)
            sp.dma_start(ctx_sb[:], ctxT[0]).then_inc(sem("ctx_in"), 16)

            def context(n):
                sp.wait_ge(sem("kv_proj"), n * 4)
                sp.dma_start(ctx_sb[:], ctxT[n % B]).then_inc(sem("ctx_in"), 16)

            with sp.Fori(0, L - 2) as l:
                for b in range(1, B + 1):
                    context(l * B + b)
                sp.wait_ge(sem("ff_w2"), (l + 1) * B)
                sp.dma_start(W[:, l % 2, :], wpack[l + 2]).then_inc(sem("w_in"), 16)
            with sp.Fori((L - 2) * B + 1, RUNS) as n:
                context(n)
            for b in range(B):
                sp.wait_ge(sem("y_ready"), b + 1)
                sp.dma_start(out[b], x_in[:, b, :]).then_inc(sem("out"), 16)
            sp.wait_ge(sem("out"), 16 * B)

        @block.gpsimd
        def _(pool):
            nc.gpsimd.memset(neghalf[:], -0.5).then_inc(sem("pool_consts"), 1)
            nc.gpsimd.memset(NV[:, :, DH:128], 1.0).then_inc(sem("pool_consts"), 1)
            nc.gpsimd.memset(Vs[:, DH:128], 1.0).then_inc(sem("pool_consts"), 1)
            nc.gpsimd.memset(tiny[:, 0:16], 1e-24 / 256.0 / (UNIT * UNIT)).then_inc(sem("pool_consts"), 1)
            nc.gpsimd.memset(tiny[:, 16:17], 1e-24 / (UNIT * UNIT)).then_inc(sem("pool_consts"), 1)
            nc.gpsimd.memset(ones[:], 1.0).then_inc(sem("pool_consts"), 1)
            pool.wait_ge(sem("pool_consts"), POOL_CONSTS)

            def power(out_, in_, width, ready, ready_at, done):
                pool.wait_ge(sem(ready), ready_at)
                nc.gpsimd.tensor_tensor(out_, in_, neghalf[0:out_.shape[0], 0:width], ALU.pow).then_inc(sem(done), 1)

            power(rn[0:12, 0:1], ssc[0:12, 0:1], 1, "null_ss", 1, "null_rn")
            pool.wait_ge(sem("ET_exp"), 4)
            nc.gpsimd.affine_select(out=ET[:].rearrange("p (h i) -> p h i", h=H), in_=ET[:].rearrange("p (h i) -> p h i", h=H),
                                    compare_op=ALU.is_ge, fill=0.0, base=0, pattern=[[0, H], [1, N]],
                                    channel_multiplier=-1).then_inc(sem("ET_ready"), 1)
            nc.gpsimd.memset(V[:, :, DH:128], 1.0).then_inc(sem("V_ones"), 1)
            for b in range(B):
                power(rstd[:], ve[:], 1, "in_var", b + 1, "in_rstd")

            with pool.Fori(0, RUNS) as n:
                power(rstd[:], ve[:], 1, "sa_var", n + 1, "sa_rstd")
                power(rn[:], ssc[:], 17, "sa_ss", n + 1, "sa_rn")
                power(rstd[:], ve[:], 1, "sao_var", n + 1, "sao_rstd")
                power(rstd[:], ve[:], 1, "ca_var", n + 1, "ca_rstd")
                power(rn[:, 0:16], ssc[:, 0:16], 16, "ca_ss", n + 1, "ca_rn")
                power(rn[:, 0:16], ssc[:, 0:16], 16, "kv_ss", n + 1, "kv_rn")
                power(rstd[:], ve[:], 1, "cao_var", n + 1, "cao_rstd")
                power(rstd[:], ve[:], 1, "ff_var", n + 1, "ff_rstd")
            with pool.Fori(0, B) as b:
                for tag in ("fin", "y", "y2", "z"):
                    power(rstd[:], ve[:], 1, tag + "_var", b + 1, tag + "_rstd")

        @block.vector
        def _(dve):
            nc_v = nc.vector

            def layernorm(link, tag, n, src, dst):
                link(nc_v.bn_stats(stats[:], src))
                nc_v.memset(fence[:], 0.0)
                link(nc_v.bn_aggr(mv[:], stats[:]))
                nc_v.tensor_scalar(ve[:], mv[:, 1:2], EPS, None, ALU.add).then_inc(sem(tag + "_var"), 1)
                dve.wait_ge(sem(tag + "_rstd"), n + 1)
                return nc_v.tensor_scalar(dst, src, mv[:, 0:1], rstd[:], ALU.subtract, ALU.mult)

            setup = Links(dve, sem("dve_setup"), 0)
            dve.wait_ge(sem("consts_in"), 16 * 5)
            nc_v.tensor_copy(ident16[:], ident).then_inc(sem("ident16"), 1)
            setup(nc_v.tensor_tensor(nksq[:], nk[:], nk[:], ALU.mult))
            setup(nc_v.tensor_reduce(ss[0:12, 0:1], nksq[:], AX_X, ALU.add))
            nc_v.tensor_scalar(ssc[0:12, 0:1], ss[0:12, 0:1], 1e-24, 1.0 / (UNIT * UNIT), ALU.max, ALU.mult).then_inc(sem("null_ss"), 1)
            dve.wait_ge(sem("null_rn"), 1)
            setup(nc_v.tensor_scalar(nkn[:], nk[:], rn[0:12, 0:1], None, ALU.mult))
            for a in (0, 2):
                setup(nc_v.tensor_copy(nks[:, a, :], nkn[:]))
            nc_v.tensor_tensor(nks[:, 1, :], nkn[:], nks[:, 0, :], ALU.subtract).then_inc(sem("null_split"), 1)
            dve.wait_ge(sem("null_T"), 1)
            nc_v.tensor_copy(NKC[:], psLh[0][:, 0:2, 0:2 * L]).then_inc(sem("NKC"), 1)
            dve.wait_ge(sem("bias_mm"), 1)
            setup(nc_v.tensor_copy(ET[0:H, 128:256], psL[0:H, 1, 0:N]))
            setup(nc_v.tensor_copy(ET[0:H, 512:640], ET[0:H, 128:256]))
            setup(nc_v.tensor_copy(ET[0:H, 0:128], ET[0:H, 128:129].broadcast_to([H, 128])))
            src, dst = 512, 640
            shift = 1
            while shift < N:
                setup(nc_v.tensor_copy(ET[0:H, dst:dst + shift], ET[0:H, src:src + shift]))
                setup(nc_v.tensor_tensor(ET[0:H, dst + shift:dst + N], ET[0:H, src + shift:src + N],
                                         ET[0:H, src:src + N - shift], ALU.max))
                src, dst = dst, src
                shift *= 2
            nc_v.tensor_copy(ET[0:H, 256:384], ET[0:H, src:src + N]).then_inc(sem("bias_ready"), 1)
            nc_v.tensor_tensor(ET[0:H, 384:512], ET[0:H, 128:256], ET[0:H, src:src + N], ALU.subtract).then_inc(sem("bias_ready"), 1)
            for g in range(4):
                dve.wait_ge(sem("flip_mm"), g + 1)
                dve.wait_ge(sem("bias_in"), 64)
                nc_v.tensor_tensor(ET[:, g * 512:(g + 1) * 512], psS[:, g, :],
                                   rowmax[:, g * 512:(g + 1) * 512], ALU.subtract).then_inc(sem("ET_sub"), 1)
            dve.wait_ge(sem("x_in"), 16)
            dve.wait_ge(sem("pool_consts"), POOL_CONSTS)
            for b in range(B):
                setup(layernorm(setup, "in", b, x_in[:, b, :], xs[:, b, :]))
            dve.wait_ge(sem("ET_ready"), 1)
            dve.wait_ge(sem("V_ones"), 1)
            dve.wait_ge(sem("gout_in"), 16)

            def split_norm(link, tag, n, heads):
                dve.wait_ge(sem(tag + "_sq"), n + 1)
                link(nc_v.tensor_reduce(ss[:, 0:heads], qsq[:, 0:heads, :], AX_X, ALU.add))
                nc_v.tensor_tensor(ssc[:, 0:heads], ss[:, 0:heads], tiny[:, 0:heads], ALU.max).then_inc(sem(tag + "_ss"), 1)
                dve.wait_ge(sem(tag + "_rn"), n + 1)
                nc_v.tensor_tensor(qn[:, 0:heads, :], qraw[:, 0:heads, :],
                                   rn[:, 0:heads].unsqueeze(2).broadcast_to([128, heads, DH]), ALU.mult).then_inc(sem(tag + "_qn"), 1)
                dve.wait_ge(sem(tag + "_hi"), n + 1)
                nc_v.tensor_tensor(qs[:, 0:heads, 1, :], qn[:, 0:heads, :], qs[:, 0:heads, 0, :], ALU.subtract).then_inc(sem(tag + "_lo"), 1)

            def out_norm(link, tag, n, l, kind):
                dve.wait_ge(sem(tag + "_wo"), n + 1)
                link(layernorm(link, tag, n, psL[:, 0, 0:D], xn[:]))
                link(nc_v.tensor_tensor(xn[:], xn[:], gout_b[:, l, kind, :], ALU.mult))
                link(nc_v.tensor_tensor(xr[:], xr[:], xn[:], ALU.add))

            def normed_T(link, tag, n, l, k):
                layernorm(link, tag, n, xr[:], xn[:]).then_inc(sem(tag + "_xn"), 1)
                dve.wait_ge(sem(tag + "_xT"), n + 1)
                nc_v.tensor_scalar(xnT[:], psL[:, 0, 0:128], gcol[:, l, k:k + 1], None, ALU.mult).then_inc(sem(tag + "_xnT"), 1)

            def evacuate(link, tag, n, g, tiles):
                bank = psO[:, g % 2, :]
                dve.wait_ge(sem(tag + "_pv"), (n * NG + g + 1) * tiles)
                if g > 0:
                    dve.wait_ge(sem(tag + "_o"), (n * NG + g) * 2)
                link(nc_v.reciprocal(rden[:], bank[64:128, :]))
                o4 = bank[0:64, :].rearrange("p (c t n) -> p c t n", t=2, n=N)
                r4 = rden[:].rearrange("p (c t n) -> p c t n", t=2, n=N)
                for par in range(2):
                    nc_v.tensor_tensor(oT[64 * par:64 * par + 64, 2 * g:2 * g + 2, :], o4[:, :, par, :], r4[:, :, par, :],
                                       ALU.mult).then_inc(sem(tag + "_o"), 1)

            with dve.Fori(0, RUNS) as n:
                l, b = n // B, n % B
                link = Links(dve, sem("dve_run"), n * LINKS)
                link(nc_v.tensor_scalar(xr[:], xs[:, b, :], 1.0, None, ALU.mult))
                link(nc_v.tensor_scalar(nkc[:], NKC[:, :, l], 1.0, None, ALU.mult))
                nc_v.tensor_scalar(nv[:], NV[:, l, :], 1.0, None, ALU.mult).then_inc(sem("sa_null"), 1)
                normed_T(link, "sa", n, l, 0)
                dve.wait_ge(sem("sa_raw"), n * 3 + 3)
                first = qraw[:, :, 0:ROT]
                cb = cosT.unsqueeze(1).broadcast_to([128, 17, ROT])
                pairs = qraw[:, :, 0:ROT].rearrange("p h (j t) -> p h j t", t=2)
                pb = rotb[:].rearrange("p h (j t) -> p h j t", t=2)
                sinb = sinT.rearrange("p (j t) -> p j t", t=2).unsqueeze(1).broadcast_to([128, 17, ROT // 2, 2])
                nc_v.tensor_tensor(rota[:], first, cb, ALU.mult)
                nc_v.tensor_tensor(pb[:, :, :, 0], pairs[:, :, :, 1], sinb[:, :, :, 0], ALU.mult)
                link(nc_v.tensor_tensor(pb[:, :, :, 1], pairs[:, :, :, 0], sinb[:, :, :, 1], ALU.mult))
                nc_v.tensor_tensor(first, rota[:], rotb[:], ALU.add).then_inc(sem("sa_rot"), 1)
                split_norm(link, "sa", n, 17)
                dve.wait_ge(sem("sa_kT"), n + 1)
                nc_v.tensor_copy(KTs[:], psLh[0][:, 0:2, :]).then_inc(sem("sa_KT"), 1)
                for g in range(NG):
                    for j in range(SA_N):
                        s = g * SA_N + j
                        dve.wait_ge(sem("sa_exp"), n * NG * SA_N + s + 1)
                        if j == 0:
                            nc_v.tensor_tensor(P[:, s % 4, :], P[:, s % 4, :], ET[:, g * QCOL:(g + 1) * QCOL], ALU.mult).then_inc(sem("sa_p"), 1)
                        else:
                            nc_v.tensor_tensor(P[0:1, s % 4, :], P[0:1, s % 4, :], E0[:, g * QCOL:(g + 1) * QCOL], ALU.mult).then_inc(sem("sa_p"), 1)
                    evacuate(link, "sa", n, g, SA_N)
                out_norm(link, "sao", n, l, 0)
                link(nc_v.tensor_scalar(nkc[:], NKC[:, :, l + L], 1.0, None, ALU.mult))
                nc_v.tensor_scalar(nv[:], NV[:, l + L, :], 1.0, None, ALU.mult).then_inc(sem("ca_null"), 1)
                normed_T(link, "ca", n, l, 1)
                dve.wait_ge(sem("ca_sq"), n + 1)
                split_norm(link, "ca", n, 16)
                for t in range(4):
                    dve.wait_ge(sem("kv_proj"), n * 4 + t + 1)
                    nc_v.tensor_copy(V[:, 4 * t:4 * t + 4, 0:DH],
                                     psS[:, t, :].rearrange("p (a c) -> p a c", c=128)[:, :, DH:128]).then_inc(sem("kv_v"), 1)
                dve.wait_ge(sem("kv_sq"), n + 1)
                link(nc_v.tensor_reduce(ss[:, 0:16], ksq[:], AX_X, ALU.add))
                nc_v.tensor_scalar(ssc[:, 0:16], ss[:, 0:16], 1e-24 / (UNIT * UNIT), None, ALU.max).then_inc(sem("kv_ss"), 1)
                dve.wait_ge(sem("kv_rn"), n + 1)
                nc_v.tensor_tensor(kn[:], kraw[:], rn[:, 0:16].unsqueeze(2).broadcast_to([128, 16, DH]), ALU.mult).then_inc(sem("kv_kn"), 1)
                dve.wait_ge(sem("kv_hi"), n + 1)
                nc_v.tensor_tensor(ks[:, :, 1, :], kn[:], ks[:, :, 0, :], ALU.subtract).then_inc(sem("kv_lo"), 1)
                for part in range(2):
                    dve.wait_ge(sem("kv_T"), n * 4 + 2 * part + 2)
                    nc_v.tensor_copy(KT[:, part, 1024:2048], psLh[1].rearrange("p t c -> p (t c)")).then_inc(sem("kv_KT_v"), 1)
                for g in range(NG):
                    evacuate(link, "ca", n, g, CA_N)
                out_norm(link, "cao", n, l, 1)
                normed_T(link, "ff", n, l, 2)
                dve.wait_ge(sem("ff_exp"), n + 1)
                link(nc_v.tensor_scalar(eg1[:], eg[:], 1.0, None, ALU.add))
                link(nc_v.reciprocal(hu[:], eg1[:]))
                link(nc_v.tensor_tensor(eg1[:], psL[:, 1, :], hu[:], ALU.mult))
                nc_v.tensor_tensor(hu[:], psL[:, 0, :], eg1[:], ALU.mult).then_inc(sem("ff_act"), 1)
                dve.wait_ge(sem("ff_w2"), n + 1)
                link(nc_v.tensor_tensor(xs[:, b, :], xr[:], psL[:, 1, 0:D], ALU.add))
                assert link.k == LINKS, link.k

            with dve.Fori(0, B) as b:
                link = Links(dve, sem("dve_tail"), b * TAIL_LINKS)
                link(nc_v.tensor_scalar(xr[:], xs[:, b, :], 1.0, None, ALU.mult))
                link(nc_v.tensor_reduce(ss[:, 0:1], xr[:], AX_X, ALU.max))
                link(nc_v.reciprocal(ssc[:, 0:1], ss[:, 0:1]))
                link(nc_v.tensor_scalar(xr[:], xr[:], ssc[:, 0:1], None, ALU.mult))
                layernorm(link, "fin", b, xr[:], xn[:]).then_inc(sem("fin_xn"), 1)
                dve.wait_ge(sem("fin_xT"), b + 1)
                dve.wait_ge(sem("tail_in"), 48)
                nc_v.tensor_scalar(xnT[:], psL[:, 0, 0:128], TC[:, C_FINAL:C_FINAL + 1], None, ALU.mult).then_inc(sem("fin_xnT"), 1)
                dve.wait_ge(sem("fin_proj"), b + 1)
                link(nc_v.tensor_tensor(xr[:], x_in[:, b, :], psL[:, 1, 0:D], ALU.add))
                link(layernorm(link, "y", b, xr[:], yb[:]))
                layernorm(link, "y2", b, yb[:], xn[:]).then_inc(sem("y2_xn"), 1)
                link(nc_v.tensor_tensor(xr[:], xr[:], yb[:], ALU.add))
                dve.wait_ge(sem("y2_xT"), b + 1)
                nc_v.tensor_scalar(xnT[:], psL[:, 0, 0:128], TC[:, C_LNW:C_LNW + 1], TC[:, C_LNB:C_LNB + 1], ALU.mult, ALU.add).then_inc(sem("y2_xnT"), 1)
                dve.wait_ge(sem("t_qkv"), b + 1)
                link(nc_v.tensor_copy(tq[:], psL[:, 1, 0:128]))
                link(nc_v.tensor_copy(tv[:], psL[:, 1, 256:384]))
                link(nc_v.tensor_copy(tk[:], psL[:, 1, 128:256]))
                nc_v.tensor_tensor(tkm, tk[:].unsqueeze(1).broadcast_to([128, H, N]),
                                   hmask.unsqueeze(2).broadcast_to([128, H, N]), ALU.mult).then_inc(sem("t_km"), 1)
                dve.wait_ge(sem("t_s"), b + 1)
                for c in range(4):
                    ins = nc_v.scalar_tensor_tensor(out=ts[:, 4 * c:4 * c + 4, :], in0=psS[:, c, :].rearrange("p (h t) -> p h t", t=N),
                                                    scalar=float(8) ** -0.5, in1=cmask.unsqueeze(1).broadcast_to([128, 4, N]),
                                                    op0=ALU.mult, op1=ALU.add)
                link(ins)
                link(nc_v.tensor_reduce(ss[:, 0:H], ts, AX_X, ALU.max))
                nc_v.tensor_tensor(ts, ts, ss[:, 0:H].unsqueeze(2).broadcast_to([128, H, N]), ALU.subtract).then_inc(sem("t_sub"), 1)
                dve.wait_ge(sem("t_exp"), b + 1)
                link(nc_v.tensor_reduce(ssc[:, 0:H], ts, AX_X, ALU.add))
                link(nc_v.reciprocal(rn[:, 0:H], ssc[:, 0:H]))
                for c in range(2, 4):
                    dve.wait_ge(sem("t_pT"), b * 4 + c + 1)
                    nc_v.tensor_copy(tkm[:, 4 * c:4 * c + 4, :].rearrange("p h t -> p (h t)"), psS[:, c, :]).then_inc(sem("t_pT_v"), 1)
                dve.wait_ge(sem("t_pv"), b + 1)
                nc_v.tensor_tensor(xn[:].rearrange("p (h e) -> p h e", e=8), psL[:, 0, 0:128].rearrange("p (h e) -> p h e", e=8),
                                   rn[:, 0:H].unsqueeze(2).broadcast_to([128, H, 8]), ALU.mult).then_inc(sem("t_o"), 1)
                dve.wait_ge(sem("t_oT"), b + 1)
                nc_v.tensor_copy(xnT[:], psL[:, 1, 0:128]).then_inc(sem("t_oT_sb"), 1)
                dve.wait_ge(sem("t_wo"), b + 1)
                link(nc_v.tensor_tensor(xr[:], xr[:], psL[:, 0, 0:128], ALU.add))
                link(nc_v.tensor_scalar(x_in[:, b, :], xr[:], 1.0, None, ALU.mult))
                layernorm(link, "z", b, xr[:], xn[:]).then_inc(sem("z_xn"), 1)
                dve.wait_ge(sem("z_xT"), b + 1)
                link(nc_v.tensor_scalar(zT[:, b, :], psL[:, 0, 0:128], 1.0, None, ALU.mult))
                assert link.k == TAIL_LINKS, link.k
            link = Links(dve, sem("dve_rec"), 0)
            nc_v.tensor_copy(cT[:], TC[:, C_INC:C_INC + 1].broadcast_to([128, 128])).then_inc(sem("c_ready"), 1)
            for t in range(B):
                dve.wait_ge(sem("gate_f"), t + 1)
                dve.wait_ge(sem("c_ready"), t + 1)
                link(nc_v.tensor_tensor(cf[:], fT[:], cT[:], ALU.mult))
                dve.wait_ge(sem("gate_g"), t + 1)
                link(nc_v.tensor_tensor(ig[:], iT[:], gT[:], ALU.mult))
                nc_v.tensor_tensor(cT[:], cf[:], ig[:], ALU.add).then_inc(sem("c_ready"), 1)
            for t in range(B):
                dve.wait_ge(sem("y_tanh"), t + 1)
                nc_v.tensor_tensor(x_in[:, t, :], x_in[:, t, :], hy[:, t, :], ALU.add).then_inc(sem("y_ready"), 1)

        @block.scalar
        def _(act):
            nc_a = nc.scalar
            act.wait_ge(sem("bias_in"), 64)
            nc_a.activation(E0[:], E0[:], ACT.Exp).then_inc(sem("E0_ready"), 1)
            for g in range(4):
                act.wait_ge(sem("ET_sub"), g + 1)
                nc_a.activation(ET[:, g * 512:(g + 1) * 512], ET[:, g * 512:(g + 1) * 512], ACT.Exp).then_inc(sem("ET_exp"), 1)
            act.wait_ge(sem("E0_ready"), 1)

            def exps(tag, n, tiles):
                for s in range(NG * tiles):
                    rows = 128 if s % tiles < tiles - 1 else 1
                    act.wait_ge(sem(tag + "_qk"), n * NG * tiles + s + 1)
                    if s >= 4:
                        act.wait_ge(sem(tag + "_pv"), n * NG * tiles + s - 3)
                    nc_a.activation(P[0:rows, s % 4, :], psS[0:rows, s % 4, :], ACT.Exp, scale=SIM_SCALE).then_inc(sem(tag + "_exp"), 1)

            def halves(tag, n, heads):
                act.wait_ge(sem(tag + "_qn"), n + 1)
                if heads == 17:
                    nc_a.activation(ks_self[:, 128:192], qn[:, 16, :], ACT.Copy)
                nc_a.activation(qs[:, 0:heads, 0, :], qn[:, 0:heads, :], ACT.Copy).then_inc(sem(tag + "_hi"), 1)

            def queries(tag, n):
                for i in range(2):
                    act.wait_ge(sem(tag + "_qT"), n * 2 + i + 1)
                    nc_a.activation(QT[:, i * 1024:(i + 1) * 1024], psLh[i].rearrange("p t c -> p (t c)"), ACT.Copy).then_inc(sem(tag + "_QT"), 1)

            with act.Fori(0, RUNS) as n:
                act.wait_ge(sem("sa_proj"), n * 3 + 1)
                nc_a.activation(qraw[:, 16, :], psL[:, 1, 0:DH], ACT.Copy)
                nc_a.activation(Vs[:, 0:DH], psL[:, 1, DH:128], ACT.Copy).then_inc(sem("sa_raw"), 1)
                for i in range(2):
                    act.wait_ge(sem("sa_proj"), n * 3 + 2 + i)
                    nc_a.activation(qraw[:, 8 * i:8 * i + 8, :].rearrange("p h d -> p (h d)"), psL[:, i, :], ACT.Copy).then_inc(sem("sa_raw"), 1)
                act.wait_ge(sem("sa_rot"), n + 1)
                nc_a.activation(qsq[:], qraw[:], ACT.Square, scale=1.0 / UNIT).then_inc(sem("sa_sq"), 1)
                halves("sa", n, 17)
                queries("sa", n)
                exps("sa", n, SA_N)
                for i in range(2):
                    act.wait_ge(sem("ca_proj"), n * 2 + i + 1)
                    nc_a.activation(qraw[:, 8 * i:8 * i + 8, :].rearrange("p h d -> p (h d)"), psL[:, i, :], ACT.Copy).then_inc(sem("ca_raw"), 1)
                act.wait_ge(sem("ca_raw"), n * 2 + 2)
                nc_a.activation(qsq[:, 0:16, :], qraw[:, 0:16, :], ACT.Square, scale=1.0 / UNIT).then_inc(sem("ca_sq"), 1)
                halves("ca", n, 16)
                queries("ca", n)
                for t in range(4):
                    act.wait_ge(sem("kv_v"), n * 4 + t + 1)
                    nc_a.activation(kraw[:, 4 * t:4 * t + 4, :],
                                    psS[:, t, :].rearrange("p (a c) -> p a c", c=128)[:, :, 0:DH], ACT.Copy).then_inc(sem("kv_raw"), 1)
                act.wait_ge(sem("kv_raw"), n * 4 + 4)
                nc_a.activation(ksq[:], kraw[:], ACT.Square, scale=1.0 / UNIT).then_inc(sem("kv_sq"), 1)
                act.wait_ge(sem("kv_kn"), n + 1)
                for a in (0, 2):
                    ins = nc_a.activation(ks[:, :, a, :], kn[:], ACT.Copy)
                ins.then_inc(sem("kv_hi"), 1)
                for part in range(2):
                    act.wait_ge(sem("kv_T"), n * 4 + 2 * part + 1)
                    nc_a.activation(KT[:, part, 0:1024], psLh[0].rearrange("p t c -> p (t c)"), ACT.Copy).then_inc(sem("kv_KT_a"), 1)
                exps("ca", n, CA_N)
                act.wait_ge(sem("ff_w1"), n + 1)
                nc_a.activation(eg[:], psL[:, 1, :], ACT.Exp, scale=-1.0).then_inc(sem("ff_exp"), 1)
                act.wait_ge(sem("ff_hT"), n + 1)
                nc_a.activation(hT[:], psL[:, 0, :], ACT.Copy).then_inc(sem("ff_hT_sb"), 1)

            with act.Fori(0, B) as b:
                act.wait_ge(sem("t_sub"), b + 1)
                nc_a.activation(ts, ts, ACT.Exp).then_inc(sem("t_exp"), 1)
                for c in range(2):
                    act.wait_ge(sem("t_pT"), b * 4 + c + 1)
                    nc_a.activation(tkm[:, 4 * c:4 * c + 4, :].rearrange("p h t -> p (h t)"), psS[:, c, :], ACT.Copy).then_inc(sem("t_pT_a"), 1)
            for t in range(B):
                act.wait_ge(sem("gates"), t + 1)
                if t > 0:
                    act.wait_ge(sem("c_ready"), t + 1)
                nc_a.activation(fT[:], psL[:, 0, 0:128], ACT.Sigmoid, bias=TC[:, C_BF:C_BF + 1]).then_inc(sem("gate_f"), 1)
                nc_a.activation(iT[:], psL[:, 0, 128:256], ACT.Sigmoid, bias=TC[:, C_BI:C_BI + 1])
                nc_a.activation(gT[:], psL[:, 0, 256:384], ACT.Tanh, bias=TC[:, C_BC:C_BC + 1]).then_inc(sem("gate_g"), 1)
            for t in range(B):
                act.wait_ge(sem("y_mm"), t + 1)
                nc_a.activation(hy[:, t, :], psS[:, t, 0:128], ACT.Tanh).then_inc(sem("y_tanh"), 1)

        @block.tensor
        def _(pe):
            mm = nc.tensor.matmul
            pe.wait_ge(sem("ident16"), 1)
            pe.wait_ge(sem("consts_in"), 16 * 5)
            pe.wait_ge(sem("null_split"), 1)
            for i in range(2):
                ins = nc.tensor.transpose(psLh[0][:, i, 0:2 * L], nks[:, i:i + 2].rearrange("p a d -> p (a d)"), ident16[0:2 * L, 0:2 * L])
            ins.then_inc(sem("null_T"), 1)
            mm(psL[0:H, 1, 0:N], emb_sb[:], onehot, start=True, stop=True).then_inc(sem("bias_mm"), 1)
            pe.wait_ge(sem("bias_in"), 64)
            for g in range(4):
                mm(psS[:, g, :], flip, toeplitz[g // 2][:, (g % 2) * 512:(g % 2) * 512 + 512], start=True, stop=True).then_inc(sem("flip_mm"), 1)

            def turn_x(tag, n):
                pe.wait_ge(sem(tag + "_xn"), n + 1)
                nc.tensor.transpose(psL[:, 0, 0:128], xn[:], ident).then_inc(sem(tag + "_xT"), 1)

            def turn_q(tag, n):
                pe.wait_ge(sem(tag + "_lo"), n + 1)
                for i in range(2):
                    for h in range(8):
                        ins = nc.tensor.transpose(psLh[i][:, h, :], qs[:, 8 * i + h].rearrange("p a d -> p (a d)"), ident16[:])
                    ins.then_inc(sem(tag + "_qT"), 1)

            def attend(tag, n, tiles, keys, values, exp_sem):
                total = NG * tiles
                base = n * total
                for s in range(total + 2):
                    if s < total:
                        g, j = s // tiles, s % tiles
                        if s >= 4:
                            pe.wait_ge(sem(tag + "_exp"), base + s - 3)
                        q = QT[:, g * QCOL:(g + 1) * QCOL]
                        rows = 128 if j < tiles - 1 else 1
                        for part in range(2):
                            lhs = keys[:, part, 128 * j:128 * j + 128] if rows == 128 else nkc[:, part:part + 1]
                            ins = mm(psS[0:rows, s % 4, :], lhs, q, start=(part == 0), stop=(part == 1))
                        ins.then_inc(sem(tag + "_qk"), 1)
                    if s >= 2:
                        s2 = s - 2
                        g, j = s2 // tiles, s2 % tiles
                        if j == 0 and g >= 2:
                            pe.wait_ge(sem(tag + "_o"), n * NG * 2 + 2 * (g - 1))
                        pe.wait_ge(sem(exp_sem), base + s2 + 1)
                        if j < tiles - 1:
                            ins = mm(psO[:, g % 2, :], values[:, j, :], P[:, s2 % 4, :], start=(j == 0), stop=False)
                            ins.then_inc(sem(tag + "_pv"), 1)
                        else:
                            ins = mm(psO[:, g % 2, :], nv[:], P[0:1, s2 % 4, :], start=False, stop=True)
                            ins.then_inc(sem(tag + "_pv"), 1)

            def project_out(tag, n, w, done):
                pe.wait_ge(sem(tag + "_o"), n * NG * 2 + 2 * NG)
                for c in range(H // 2):
                    ins = mm(psL[:, 0, 0:D], oT[:, c, :], w[:, c * D:(c + 1) * D], start=(c == 0), stop=(c == H // 2 - 1))
                ins.then_inc(sem(done), 1)

            with pe.Fori(0, RUNS) as n:
                l = n // B
                slot = l % 2
                pe.wait_ge(sem("w_in"), 16 * (l + 1))
                turn_x("sa", n)
                pe.wait_ge(sem("sa_xnT"), n + 1)
                mm(psL[:, 1, 0:128], xnT[:], W[:, slot, W_SAKV:W_SAKV + 128], start=True, stop=True).then_inc(sem("sa_proj"), 1)
                mm(psL[:, 0, :], xnT[:], W[:, slot, W_SAQ:W_SAQ + 512], start=True, stop=True).then_inc(sem("sa_proj"), 1)
                pe.wait_ge(sem("sa_raw"), n * 3 + 1)
                mm(psL[:, 1, :], xnT[:], W[:, slot, W_SAQ + 512:W_SAQ + 1024], start=True, stop=True).then_inc(sem("sa_proj"), 1)
                turn_q("sa", n)
                pe.wait_ge(sem("sa_QT"), n * 2 + 1)
                for i in range(2):
                    ins = nc.tensor.transpose(psLh[0][:, i, :], ks_self[:, DH * i:DH * i + 128], ident16[:])
                ins.then_inc(sem("sa_kT"), 1)
                pe.wait_ge(sem("sa_QT"), n * 2 + 2)
                pe.wait_ge(sem("sa_KT"), n + 1)
                pe.wait_ge(sem("sa_null"), n + 1)
                attend("sa", n, SA_N, KTs[:], Vs[:].unsqueeze(1), "sa_p")
                project_out("sa", n, W[:, slot, W_SAO:W_SAO + 1024], "sao_wo")
                turn_x("ca", n)
                pe.wait_ge(sem("ca_xnT"), n + 1)
                for i in range(2):
                    mm(psL[:, i, :], xnT[:], W[:, slot, W_CAQ + 512 * i:W_CAQ + 512 * i + 512], start=True, stop=True).then_inc(sem("ca_proj"), 1)
                turn_q("ca", n)
                pe.wait_ge(sem("ctx_in"), n * 16 + 16)
                for t in range(4):
                    for a in range(4):
                        k = 4 * t + a
                        ins = mm(psS[:, t, a * 128:(a + 1) * 128], ctx_sb[:, k * 128:(k + 1) * 128],
                                 W[:, slot, W_CAKV:W_CAKV + 128], start=True, stop=True)
                    ins.then_inc(sem("kv_proj"), 1)
                pe.wait_ge(sem("kv_lo"), n + 1)
                pe.wait_ge(sem("ca_QT"), n * 2 + 2)
                for part in range(2):
                    for i in range(2):
                        if part == 1:
                            pe.wait_ge(sem("kv_KT_a" if i == 0 else "kv_KT_v"), n * 2 + 1)
                        for t in range(8):
                            ins = nc.tensor.transpose(psLh[i][:, t, :], ks[:, 8 * i + t, part:part + 2, :].rearrange("p a d -> p (a d)"), ident16[:])
                        ins.then_inc(sem("kv_T"), 1)
                pe.wait_ge(sem("kv_KT_a"), n * 2 + 2)
                pe.wait_ge(sem("kv_KT_v"), n * 2 + 2)
                pe.wait_ge(sem("kv_raw"), n * 4 + 4)
                pe.wait_ge(sem("ca_null"), n + 1)
                attend("ca", n, CA_N, KT[:], V[:], "ca_exp")
                project_out("ca", n, W[:, slot, W_CAO:W_CAO + 1024], "cao_wo")
                turn_x("ff", n)
                pe.wait_ge(sem("ff_xnT"), n + 1)
                mm(psL[:, 0, :], xnT[:], W[:, slot, W_FF1:W_FF1 + 512], start=True, stop=True)
                mm(psL[:, 1, :], xnT[:], W[:, slot, W_FF1 + 512:W_FF1 + 1024], start=True, stop=True).then_inc(sem("ff_w1"), 1)
                pe.wait_ge(sem("ff_act"), n + 1)
                for c in range(4):
                    ins = nc.tensor.transpose(psL[:, 0, c * 128:(c + 1) * 128], hu[:, c * 128:(c + 1) * 128], ident)
                ins.then_inc(sem("ff_hT"), 1)
                pe.wait_ge(sem("ff_hT_sb"), n + 1)
                for c in range(4):
                    ins = mm(psL[:, 1, 0:D], hT[:, c * 128:(c + 1) * 128], W[:, slot, W_FF2 + c * D:W_FF2 + (c + 1) * D],
                             start=(c == 0), stop=(c == 3))
                ins.then_inc(sem("ff_w2"), 1)

            def tail_w(k):
                return TW[:, k, :]

            pe.wait_ge(sem("tail_in"), 48)
            with pe.Fori(0, B) as b:
                turn_x("fin", b)
                pe.wait_ge(sem("fin_xnT"), b + 1)
                mm(psL[:, 1, 0:D], xnT[:], tail_w(T_PROJ), start=True, stop=True).then_inc(sem("fin_proj"), 1)
                turn_x("y2", b)
                pe.wait_ge(sem("y2_xnT"), b + 1)
                mm(psL[:, 1, 0:128], tail_w(T_Q), xnT[:], start=True, stop=True)
                mm(psL[:, 1, 128:256], tail_w(T_K), xnT[:], start=True, stop=True)
                mm(psL[:, 1, 256:384], xnT[:], tail_w(T_V), start=True, stop=True).then_inc(sem("t_qkv"), 1)
                pe.wait_ge(sem("t_km"), b + 1)
                for c in range(4):
                    ins = mm(psS[:, c, :], tq[:], tkm[:, 4 * c:4 * c + 4, :].rearrange("p h t -> p (h t)"), start=True, stop=True)
                ins.then_inc(sem("t_s"), 1)
                pe.wait_ge(sem("t_exp"), b + 1)
                for c in range(4):
                    for h in range(4 * c, 4 * c + 4):
                        ins = nc.tensor.transpose(psS[:, c, (h % 4) * 128:(h % 4) * 128 + 128], ts[:, h, :], ident)
                    ins.then_inc(sem("t_pT"), 1)
                pe.wait_ge(sem("t_pT_a"), b * 2 + 2)
                pe.wait_ge(sem("t_pT_v"), b * 2 + 2)
                for h in range(H):
                    ins = mm(psL[:, 0, 8 * h:8 * h + 8], tkm[:, h, :], tv[:, 8 * h:8 * h + 8], start=True, stop=True)
                ins.then_inc(sem("t_pv"), 1)
                pe.wait_ge(sem("t_o"), b + 1)
                nc.tensor.transpose(psL[:, 1, 0:128], xn[:], ident).then_inc(sem("t_oT"), 1)
                pe.wait_ge(sem("t_oT_sb"), b + 1)
                mm(psL[:, 0, 0:D], xnT[:], tail_w(T_O), start=True, stop=True).then_inc(sem("t_wo"), 1)
                turn_x("z", b)
            pe.wait_ge(sem("dve_tail"), B * TAIL_LINKS)
            for t in range(B):
                pe.wait_ge(sem("c_ready"), t + 1)
                if t > 0:
                    pe.wait_ge(sem("gate_g"), t)
                for k, (w, u) in enumerate(((T_WF, T_UF), (T_WI, T_UI), (T_WC, T_UC))):
                    mm(psL[:, 0, 128 * k:128 * k + 128], tail_w(w), zT[:, t, :], start=True, stop=False)
                    ins = mm(psL[:, 0, 128 * k:128 * k + 128], tail_w(u), cT[:], start=False, stop=True)
                ins.then_inc(sem("gates"), 1)
            pe.wait_ge(sem("c_ready"), B + 1)
            for t in range(B):
                mm(psS[:, t, 0:128], zT[:, t, :], tail_w(T_WO), start=True, stop=False)
                mm(psS[:, t, 0:128], cT[:], tail_w(T_UO), start=False, stop=False)
                mm(psS[:, t, 0:128], ones[:], bo_row[:], start=False, stop=True).then_inc(sem("y_mm"), 1)


_OUTS = [((4, 128, 128), 'float32')]


def constants(np):
    c = np.zeros((128, C_END), np.float32)
    c[:, 0:128] = np.eye(128)
    c[:, 128:256] = np.eye(128)[::-1]
    c[:, 256:384] = np.where(np.arange(128)[None, :] > np.arange(128)[:, None], -3.0e38, 0.0)
    neg = np.arange(N)
    safe = np.maximum(neg, 1).astype(np.float32)
    large = 16 + (np.log(safe / np.float32(16)) / np.float32(np.log(128 / 16)) * np.float32(16)).astype(np.int32)
    bucket = np.where(neg < 16, neg, np.minimum(large, NBUCK - 1))
    c[bucket, 384 + neg] = 1.0
    inv = (1.0 / 10000.0 ** (np.arange(0, ROT, 2, dtype=np.float32) / ROT)).astype(np.float32)
    f = np.arange(N, dtype=np.float32)[:, None] * inv[None, :]
    c[:, 512:544] = np.repeat(np.cos(f), 2, axis=-1)
    c[:, 544:576] = np.stack((-np.sin(f), np.sin(f)), -1).reshape(N, ROT)
    c[:, 576:592] = np.arange(128)[:, None] // 8 == np.arange(16)[None, :]
    return c


def kernel(**inputs):
    import numpy as np
    import concourse.bacc as _bacc
    from concourse.bass_utils import run_bass_kernel_spmd as _run

    t = {k: np.asarray(v) for k, v in inputs.items()}
    xa = {k[9:]: v for k, v in t.items() if k.startswith("L0_xattn_")}
    at = {k[8:]: v for k, v in t.items() if k.startswith("L0_attn_")}
    ff = {k[7:]: v for k, v in t.items() if k.startswith("L0_ffn_")}

    def rows(w, c):
        return w.reshape(L, c, 128, -1).transpose(0, 2, 1, 3).reshape(L, 128, -1)

    def heads(w):
        return w.transpose(1, 0, 2).reshape(128, 128)

    arrays = {
        "x": t["x"],
        "ctxT": t["ctx_1024"].transpose(0, 2, 1),
        "wpack": np.concatenate([xa["sa_wq"], xa["sa_wkv"], rows(xa["sa_wo"], 8), xa["ca_wq"], xa["ca_wkv"],
                                 rows(xa["ca_wo"], 8), xa["ff_w1"], rows(xa["ff_w2"], 4)], axis=2),
        "gcols": np.stack([xa["sa_norm_g"], xa["ca_norm_g"], xa["ff_norm_g"]], 1).transpose(2, 0, 1),
        "gout": np.stack([xa["sa_out_g"], xa["ca_out_g"]], 1),
        "null_k": np.concatenate([xa["sa_null_kv"][:, 0], xa["ca_null_kv"][:, 0]], 0),
        "null_v": np.concatenate([xa["sa_null_kv"][:, 1], xa["ca_null_kv"][:, 1]], 0)[None],
        "tail_w": np.stack([xa["proj_w"], heads(at["wq"]), heads(at["wk"]), heads(at["wv"]), at["wo"],
                            ff["wf"].T, ff["wi"].T, ff["wc"].T, ff["uf"].T, ff["ui"].T, ff["uc"].T,
                            ff["wo"].T, ff["uo"].T], 1),
        "tail_cols": np.stack([xa["final_g"], at["ln_w"], at["ln_b"], ff["bf"], ff["bi"], ff["bc"], ff["in_c"]], 1),
        "bo": ff["bo"][None],
        "emb": xa["rel_pos_emb"],
        "c_pack": constants(np),
    }
    arrays = {k: np.ascontiguousarray(v) for k, v in arrays.items()}
    nc = _bacc.Bacc("TRN2", target_bir_lowering=False, num_devices=1)
    args = [nc.dram_tensor(k, v.shape, mybir.dt.from_np(v.dtype), kind="ExternalInput").ap() for k, v in arrays.items()]
    outs = [nc.dram_tensor(f"out_{i}", shape, mybir.dt.from_np(np.dtype(d)), kind="ExternalOutput").ap()
            for i, (shape, d) in enumerate(_OUTS)]
    build(nc, *args, *outs)
    r = _run(nc, [arrays], core_ids=[0])
    return r.results[0]["out_0"]
```

```python
from contextlib import ExitStack

import concourse.bass as bass
from concourse import mybir

ALU = mybir.AluOpType
ACT = mybir.ActivationFunctionType
F32 = mybir.dt.float32
F16 = mybir.dt.float16
AX_X = mybir.AxisListType.X

L, B, N, D = 6, 4, 128, 128
H, DH, ROT = 16, 64, 32
M = 2048
KT_N = M // 128
FF = 512
NBUCK = 32
EPS = 1e-5
GH = 4
NG = H // GH
QCOL = GH * N
UNIT = 1024.0
SIM_SCALE = 16.0 / (UNIT * UNIT)
RUNS = L * B
CA_N = KT_N + 1
SLOTS = 3
PSLOTS = 4
AHEAD = 2

W_SAQ, W_SAKV, W_SAO, W_CAQ, W_CAKV, W_CAO, W_FF1, W_FF2, W_END = 0, 1024, 1152, 2176, 3200, 3328, 4352, 5376, 5888
T_PROJ, T_Q, T_K, T_V, T_O, T_WF, T_WI, T_WC, T_UF, T_UI, T_UC, T_WO, T_UO = range(13)
C_END = 592
C_FINAL, C_LNW, C_LNB, C_BF, C_BI, C_BC, C_INC = range(7)


class Links:

    def __init__(self, eng, sem, base):
        self.eng, self.sem, self.base, self.k = eng, sem, base, 0

    def __call__(self, ins):
        self.k += 1
        ins.then_inc(self.sem, 1)
        self.eng.wait_ge(self.sem, self.base + self.k)


def build(nc, x, ctxT, wpack, gcols, gout, null_k, null_v, tail_w, tail_cols, bo, emb,
          c_pack, out):
    with ExitStack() as ctx:
        def sb(name, shape, dt=F32):
            return ctx.enter_context(nc.sbuf_tensor(name, shape, dt))

        def psum(name, shape):
            return ctx.enter_context(nc.psum_tensor(name, shape, F32))

        sems = {}

        def sem(name):
            if name not in sems:
                sems[name] = ctx.enter_context(nc.semaphore(name))
            return sems[name]

        def dram(name, shape):
            return nc.dram_tensor(name, shape, F32, kind="Internal").ap()

        psS = psum("psS", [128, SLOTS, 512])
        psO = psum("psO", [128, 2, 512])
        psA = psum("psA", [128, 512])
        psL = psum("psL", [128, 2, 512])
        psLh = [psL[:, i, :].bitcast(F16).rearrange("p (t c) -> p t c", c=128) for i in range(2)]
        psFour = [psA[:], psL[:, 0, :], psL[:, 1, :], psO[:, 0, :]]

        C = sb("C", [128, C_END])
        ident = C[:, 0:128]
        flip = C[:, 128:256]
        cmask = C[:, 256:384]
        onehot = C[0:NBUCK, 384:512]
        cosT = C[:, 512:544]
        sinT = C[:, 544:576]
        hmask = C[:, 576:592]
        ident16 = sb("ident16", [128, 128], F16)
        emb_sb = sb("emb_sb", [NBUCK, H])
        neghalf = sb("neghalf", [128, 17])
        tiny = sb("tiny", [128, 17])
        gcol = sb("gcol", [128, L, 3])
        gout_b = sb("gout_b", [128, L, 2, D])
        W = sb("W", [128, 2, W_END])
        TW = sb("TW", [128, 13, 128])
        TC = sb("TC", [128, 7])
        bo_row = sb("bo_row", [1, 128])
        ones = sb("ones", [1, 128])
        x_in = sb("x_in", [128, B, D])
        xs = sb("xs", [128, B, D])

        class Rows:

            def __init__(self, tag):
                self.fence = sb(tag + "_fence", [1, 1])
                self.stats = sb(tag + "_stats", [128, 6])
                self.mv = sb(tag + "_mv", [128, 2])
                self.ve = sb(tag + "_ve", [128, 1])
                self.rstd = sb(tag + "_rstd", [128, 1])
                self.x = sb(tag + "_x", [128, D])
                self.xn = sb(tag + "_xn", [128, D])
                self.xnT = sb(tag + "_xnT", [128, 128])

        front = Rows("front")
        back = Rows("back")
        qraw = sb("qraw", [128, 17, DH])
        qsq = sb("qsq", [128, 17, DH])
        ss = sb("ss", [128, 17])
        ssc = sb("ssc", [128, 17])
        rn = sb("rn", [128, 17])
        qn = qsq
        rota, rotb = qsq[:, :, 0:ROT], qsq[:, :, ROT:2 * ROT]
        qs_all = sb("qs_all", [128, 17 * 2 * DH + DH], F16)
        qs = qs_all[:, 0:17 * 2 * DH].rearrange("p (h a d) -> p h a d", a=2, d=DH)
        ks_self = qs_all[:, 16 * 2 * DH:]
        QTs = sb("QTs", [128, H * N], F16)
        QT = sb("QT", [128, 2, H * N], F16)
        KTs = sb("KTs", [128, 2, 128], F16)
        Vs = sb("Vs", [128, 128])
        ctx_sb = sb("ctx_sb", [128, M])
        kraw = sb("kraw", [128, KT_N, DH])
        ksq = sb("ksq", [128, KT_N, DH])
        kn = ksq
        ks = sb("ks", [128, KT_N, 3, DH], F16)
        KT = sb("KT", [128, 2, 2, M], F16)
        V = sb("V", [128, 2, KT_N, 128])
        nk = sb("nk", [2 * L, DH])
        nksq = sb("nksq", [2 * L, DH])
        nkn = sb("nkn", [2 * L, DH])
        nks = sb("nks", [2 * L, 3, DH], F16)
        NKC = sb("NKC", [128, 2, 2 * L], F16)
        nkcs = sb("nkcs", [128, 2], F16)
        nkc = sb("nkc", [128, 2, 2], F16)
        rows_sb = sb("rows_sb", [33, H * N])
        E0 = rows_sb[0:1, :]
        NV = rows_sb[32:33, 0:2 * L * 128].rearrange("p (l d) -> p l d", d=128)
        nvs = sb("nvs", [1, 128])
        nv = sb("nv", [1, 2, 128])
        ET = sb("ET", [128, H * N])
        P = sb("P", [128, PSLOTS, QCOL])
        rden = sb("rden", [64, QCOL])
        oT = sb("oT", [128, H // 2, N])
        Ps = sb("Ps", [128, 2, QCOL])
        Psn = sb("Psn", [1, 2, QCOL])
        rdens = sb("rdens", [64, QCOL])
        oTs = sb("oTs", [128, H // 2, N])
        eg = sb("eg", [128, FF])
        eg1 = sb("eg1", [128, FF])
        hu = sb("hu", [128, FF])
        hT = sb("hT", [128, FF])
        yb, tq, tk, tv, cT, cf, ig, fT, iT, gT = (W[:, 0, 128 * k:128 * k + 128] for k in range(10))
        zT, hy = (W[:, 0, 1280 + 512 * k:1792 + 512 * k].rearrange("p (b d) -> p b d", d=D) for k in range(2))

        ts = V[:, 0]
        tkm = V[:, 1]
        toeplitz = [kraw[:].rearrange("p a d -> p (a d)"), ksq[:].rearrange("p a d -> p (a d)")]
        rowmax = V[:, 0].rearrange("p a b -> p (a b)")
        biasW = dram("biasW", [H, 256])
        biasM = dram("biasM", [H, N])
        bias0 = dram("bias0", [H, N])

        block = ctx.enter_context(nc.Block())

        FRONT_LINKS, BACK_LINKS = 18, 11
        POOL_CONSTS = 5
        TAIL_LINKS = 25
        STEPS = NG * CA_N

        PLAN_PE = {
            5: ["f_turn_sa"], 6: ["f_proj_sa"], 7: ["f_proj_sa2"], 8: ["b_wo"], 13: ["b_turn"], 14: ["f_turn_q_sa"],
            15: ["f_turn_k_sa"], 16: ["b_gate"], 18: ["f_sk0"], 19: ["f_sk1"], 20: ["f_sn0"], 21: ["f_sn1"],
            22: ["f_sv0"], 23: ["f_sv1"], 24: ["b_up"], 28: ["b_turn_h"], 29: ["f_sk2"], 30: ["f_sk3"],
            31: ["f_sn2", "b_down"], 32: ["f_sn3"], 33: ["f_sv2"], 34: ["f_sv3"], 40: ["f_wo"], 44: ["f_turn_ca"],
            45: ["f_proj_ca"], 47: ["f_kv0"], 48: ["f_kv1"], 50: ["f_kv2"], 51: ["f_kv3"], 55: ["f_turn_q_ca"],
            61: ["f_turn_k0"], 63: ["f_turn_k1"],
        }
        PLAN_ACT = {
            7: ["f_raw_sa"], 8: ["f_raw_sa2"], 10: ["f_sq_sa"], 13: ["f_hi_sa"], 15: ["f_QT_sa"], 17: ["b_exp"],
            19: ["f_se0"], 20: ["f_se1"], 21: ["f_sne0"], 22: ["f_sne1"], 29: ["b_hT"], 30: ["f_se2"], 31: ["f_se3"],
            32: ["f_sne2"], 33: ["f_sne3"], 46: ["f_raw_ca"], 47: ["f_sq_ca"], 48: ["f_kraw0"], 49: ["f_kraw1"],
            50: ["f_hi_ca"], 51: ["f_kraw2"], 52: ["f_kraw3"], 53: ["f_ksq"], 56: ["f_QT_ca"], 58: ["f_khi"],
            62: ["f_KT0"], 64: ["f_KT1"],
        }
        PLAN_DVE = {
            3: ["f_begin", "f_norm_sa"], 6: ["f_xnT_sa"], 9: ["f_rot"], 10: ["f_ss_sa", "b_out"], 12: ["f_split_sa"],
            14: ["b_xnT"], 16: ["f_KT_sa"], 18: ["b_silu"], 20: ["f_sp0"], 21: ["f_sp1"], 22: ["f_snp0"],
            23: ["f_snp1"], 24: ["f_sevac0"], 25: ["b_act", "f_sevac1"], 27: ["evac0"], 31: ["f_sp2"], 32: ["f_sp3"],
            33: ["f_snp2"], 34: ["f_snp3", "b_end"], 35: ["f_sevac2"], 36: ["f_sevac3"], 41: ["f_out"], 42: ["evac1"],
            45: ["f_xnT_ca"], 48: ["f_V0", "f_ss_ca"], 49: ["f_V1"], 50: ["f_split_ca"], 51: ["f_V2"], 52: ["f_V3"],
            54: ["f_kss"], 57: ["f_ksplit"], 60: ["evac2"], 62: ["f_KT0"], 64: ["f_KT1"], 70: ["evac3"],
        }
        PLAN_POOL = {
            3: ["f_sa"], 10: ["f_sa_q", "b_out", "b_ff"], 41: ["f_out", "f_ca"], 48: ["f_ca_q"], 54: ["f_kv"],
        }
        STEPS_ALL = STEPS + AHEAD + 1

        def drive(eng, plan, stages, core_step=None):
            def window(core, back, front):
                for s in range(STEPS_ALL):
                    if core is not None and core_step is not None:
                        core_step(s, *core)
                    for name in plan.get(s, ()):
                        part = {"b": back, "f": front, "e": core}[name[0]]
                        if part is not None:
                            stages[name](*part)

            window(None, None, (0, 0))
            window((0, 0), None, (1, 1))
            with eng.Fori(0, (RUNS - 2) // 2) as k:
                window((k * 2 + 1, 1), (k * 2, 0), (k * 2 + 2, 0))
                window((k * 2 + 2, 0), (k * 2 + 1, 1), (k * 2 + 3, 1))
            window((RUNS - 1, 1), (RUNS - 2, 0), None)
            window(None, (RUNS - 1, 1), None)

        @block.sync
        def _(sp):
            for dst, src in ((C[:], c_pack), (emb_sb[:], emb), (gcol[:], gcols), (nk[:], null_k),
                             (NV[:, :, 0:DH], null_v)):
                sp.dma_start(dst, src).then_inc(sem("consts_in"), 16)
            sp.dma_start(x_in[:], x.rearrange("b p d -> p b d")).then_inc(sem("x_in"), 16)
            sp.dma_start(gout_b[:], bass.AP(gout.tensor, 0, [[0, 128], [1, L * 2 * D]])).then_inc(sem("gout_in"), 16)
            sp.dma_start(W[:, 0, :], wpack[0]).then_inc(sem("w_in"), 16)
            sp.wait_ge(sem("bias_ready"), 2)
            sp.dma_start(biasW, ET[0:H, 0:256]).then_inc(sem("bias_out"), 16)
            sp.dma_start(biasM, ET[0:H, 256:384]).then_inc(sem("bias_out"), 16)
            sp.dma_start(bias0, ET[0:H, 384:512]).then_inc(sem("bias_out"), 16)
            sp.wait_ge(sem("bias_out"), 48)
            for i in range(2):
                sp.dma_start(toeplitz[i].rearrange("p (h n) -> p h n", n=N),
                             bass.AP(biasW.tensor, 256 * (H // 2) * i, [[1, 128], [256, H // 2], [1, N]])).then_inc(sem("bias_in"), 16)
            sp.dma_start(rowmax, bass.AP(biasM.tensor, 0, [[0, 128], [1, H * N]])).then_inc(sem("bias_in"), 16)
            sp.dma_start(E0, bass.AP(bias0.tensor, 0, [[0, 1], [1, H * N]])).then_inc(sem("bias_in"), 16)
            sp.dma_start(W[:, 1, :], wpack[1]).then_inc(sem("w_in"), 16)
            sp.dma_start(TW[:], tail_w).then_inc(sem("tail_in"), 16)
            sp.dma_start(TC[:], tail_cols).then_inc(sem("tail_in"), 16)
            sp.dma_start(bo_row[:], bo).then_inc(sem("tail_in"), 16)
            sp.dma_start(ctx_sb[:], ctxT[0]).then_inc(sem("ctx_in"), 16)

            def context(n):
                sp.wait_ge(sem("kv_proj"), n * 4)
                sp.dma_start(ctx_sb[:], ctxT[n % B]).then_inc(sem("ctx_in"), 16)

            context(1)
            with sp.Fori(0, L - 2) as l:
                for b in range(2, B + 2):
                    context(l * B + b)
                sp.wait_ge(sem("ff_w2"), (l + 1) * B)
                sp.dma_start(W[:, l % 2, :], wpack[l + 2]).then_inc(sem("w_in"), 16)
            with sp.Fori((L - 2) * B + 2, RUNS) as n:
                context(n)
            for b in range(B):
                sp.wait_ge(sem("y_ready"), b + 1)
                sp.dma_start(out[b], x_in[:, b, :]).then_inc(sem("out"), 16)
            sp.wait_ge(sem("out"), 16 * B)

        @block.gpsimd
        def _(pool):
            nc.gpsimd.memset(neghalf[:], -0.5).then_inc(sem("pool_consts"), 1)
            nc.gpsimd.memset(Vs[:, DH:128], 1.0).then_inc(sem("pool_consts"), 1)
            nc.gpsimd.memset(tiny[:, 0:16], 1e-24 / 256.0 / (UNIT * UNIT)).then_inc(sem("pool_consts"), 1)
            nc.gpsimd.memset(tiny[:, 16:17], 1e-24 / (UNIT * UNIT)).then_inc(sem("pool_consts"), 1)
            nc.gpsimd.memset(ones[:], 1.0).then_inc(sem("pool_consts"), 1)
            pool.wait_ge(sem("pool_consts"), POOL_CONSTS)

            def power(out_, in_, width, ready, ready_at, done):
                pool.wait_ge(sem(ready), ready_at)
                nc.gpsimd.tensor_tensor(out_, in_, neghalf[0:out_.shape[0], 0:width], ALU.pow).then_inc(sem(done), 1)

            power(rn[0:12, 0:1], ssc[0:12, 0:1], 1, "null_ss", 1, "null_rn")
            pool.wait_ge(sem("ET_exp"), 4)
            nc.gpsimd.affine_select(out=ET[:].rearrange("p (h i) -> p h i", h=H), in_=ET[:].rearrange("p (h i) -> p h i", h=H),
                                    compare_op=ALU.is_ge, fill=0.0, base=0, pattern=[[0, H], [1, N]],
                                    channel_multiplier=-1).then_inc(sem("ET_ready"), 1)
            nc.gpsimd.memset(V[:, :, :, DH:128], 1.0).then_inc(sem("V_ones"), 1)
            for b in range(B):
                power(front.rstd[:], front.ve[:], 1, "in_var", b + 1, "in_rstd")

            def row_power(rows, tag):
                return lambda n, par: power(rows.rstd[:], rows.ve[:], 1, tag + "_var", n + 1, tag + "_rstd")

            def head_power(tag, width):
                return lambda n, par: power(rn[:, 0:width], ssc[:, 0:width], width, tag + "_ss", n + 1, tag + "_rn")

            drive(pool, PLAN_POOL, {
                "f_sa": row_power(front, "sa"), "f_sa_q": head_power("sa", 17), "f_out": row_power(front, "sao"),
                "f_ca": row_power(front, "ca"), "f_ca_q": head_power("ca", 16), "f_kv": head_power("kv", 16),
                "b_out": row_power(back, "cao"), "b_ff": row_power(back, "ff"),
            })
            with pool.Fori(0, B) as b:
                for tag in ("fin", "y", "y2", "z"):
                    power(front.rstd[:], front.ve[:], 1, tag + "_var", b + 1, tag + "_rstd")

        @block.vector
        def _(dve):
            nc_v = nc.vector

            def layernorm(link, rows, tag, n, src, dst):
                link(nc_v.bn_stats(rows.stats[:], src))
                nc_v.memset(rows.fence[:], 0.0)
                link(nc_v.bn_aggr(rows.mv[:], rows.stats[:]))
                nc_v.tensor_scalar(rows.ve[:], rows.mv[:, 1:2], EPS, None, ALU.add).then_inc(sem(tag + "_var"), 1)
                dve.wait_ge(sem(tag + "_rstd"), n + 1)
                return nc_v.tensor_scalar(dst, src, rows.mv[:, 0:1], rows.rstd[:], ALU.subtract, ALU.mult)

            setup = Links(dve, sem("dve_setup"), 0)
            dve.wait_ge(sem("consts_in"), 16 * 5)
            nc_v.tensor_copy(ident16[:], ident).then_inc(sem("ident16"), 1)
            setup(nc_v.memset(NV[:, :, DH:128], 1.0))
            setup(nc_v.tensor_tensor(nksq[:], nk[:], nk[:], ALU.mult))
            setup(nc_v.tensor_reduce(ss[0:12, 0:1], nksq[:], AX_X, ALU.add))
            nc_v.tensor_scalar(ssc[0:12, 0:1], ss[0:12, 0:1], 1e-24, 1.0 / (UNIT * UNIT), ALU.max, ALU.mult).then_inc(sem("null_ss"), 1)
            dve.wait_ge(sem("null_rn"), 1)
            setup(nc_v.tensor_scalar(nkn[:], nk[:], rn[0:12, 0:1], None, ALU.mult))
            for a in (0, 2):
                setup(nc_v.tensor_copy(nks[:, a, :], nkn[:]))
            nc_v.tensor_tensor(nks[:, 1, :], nkn[:], nks[:, 0, :], ALU.subtract).then_inc(sem("null_split"), 1)
            dve.wait_ge(sem("null_T"), 1)
            nc_v.tensor_copy(NKC[:], psLh[0][:, 0:2, 0:2 * L]).then_inc(sem("NKC"), 1)
            dve.wait_ge(sem("bias_mm"), 1)
            setup(nc_v.tensor_copy(ET[0:H, 128:256], psL[0:H, 1, 0:N]))
            setup(nc_v.tensor_copy(ET[0:H, 512:640], ET[0:H, 128:256]))
            setup(nc_v.tensor_copy(ET[0:H, 0:128], ET[0:H, 128:129].broadcast_to([H, 128])))
            src, dst = 512, 640
            shift = 1
            while shift < N:
                setup(nc_v.tensor_copy(ET[0:H, dst:dst + shift], ET[0:H, src:src + shift]))
                setup(nc_v.tensor_tensor(ET[0:H, dst + shift:dst + N], ET[0:H, src + shift:src + N],
                                         ET[0:H, src:src + N - shift], ALU.max))
                src, dst = dst, src
                shift *= 2
            nc_v.tensor_copy(ET[0:H, 256:384], ET[0:H, src:src + N]).then_inc(sem("bias_ready"), 1)
            nc_v.tensor_tensor(ET[0:H, 384:512], ET[0:H, 128:256], ET[0:H, src:src + N], ALU.subtract).then_inc(sem("bias_ready"), 1)
            for g in range(4):
                dve.wait_ge(sem("flip_mm"), g + 1)
                dve.wait_ge(sem("bias_in"), 64)
                nc_v.tensor_tensor(ET[:, g * 512:(g + 1) * 512], psFour[g],
                                   rowmax[:, g * 512:(g + 1) * 512], ALU.subtract).then_inc(sem("ET_sub"), 1)
            dve.wait_ge(sem("x_in"), 16)
            dve.wait_ge(sem("pool_consts"), POOL_CONSTS)
            for b in range(B):
                setup(layernorm(setup, front, "in", b, x_in[:, b, :], xs[:, b, :]))
            dve.wait_ge(sem("ET_ready"), 1)
            dve.wait_ge(sem("V_ones"), 1)
            dve.wait_ge(sem("gout_in"), 16)

            links = {}

            def begin(which, n, per):
                links[which] = Links(dve, sem("dve_" + which), n * per)

            def norms(tag, heads):
                def stage(n, par):
                    dve.wait_ge(sem(tag + "_sq"), n + 1)
                    links["front"](nc_v.tensor_reduce(ss[:, 0:heads], qsq[:, 0:heads, :], AX_X, ALU.add))
                    nc_v.tensor_tensor(ssc[:, 0:heads], ss[:, 0:heads], tiny[:, 0:heads], ALU.max).then_inc(sem(tag + "_ss"), 1)
                return stage

            def split(tag, heads):
                def stage(n, par):
                    dve.wait_ge(sem(tag + "_rn"), n + 1)
                    nc_v.tensor_tensor(qn[:, 0:heads, :], qraw[:, 0:heads, :],
                                       rn[:, 0:heads].unsqueeze(2).broadcast_to([128, heads, DH]), ALU.mult).then_inc(sem(tag + "_qn"), 1)
                    dve.wait_ge(sem(tag + "_hi"), n + 1)
                    nc_v.tensor_tensor(qs[:, 0:heads, 1, :], qn[:, 0:heads, :], qs[:, 0:heads, 0, :], ALU.subtract).then_inc(sem(tag + "_lo"), 1)
                return stage

            def out_norm(link, rows, tag, n, src, kind):
                dve.wait_ge(sem(tag + "_wo"), n + 1)
                link(layernorm(link, rows, tag, n, src, rows.xn[:]))
                link(nc_v.tensor_tensor(rows.xn[:], rows.xn[:], gout_b[:, n // B, kind, :], ALU.mult))
                link(nc_v.tensor_tensor(rows.x[:], rows.x[:], rows.xn[:], ALU.add))

            def norm_rows(link, rows, tag, n):
                layernorm(link, rows, tag, n, rows.x[:], rows.xn[:]).then_inc(sem(tag + "_xn"), 1)

            def turned(rows, tag, k, src):
                def stage(n, par):
                    dve.wait_ge(sem(tag + "_xT"), n + 1)
                    nc_v.tensor_scalar(rows.xnT[:], src, gcol[:, n // B, k:k + 1], None, ALU.mult).then_inc(sem(tag + "_xnT"), 1)
                return stage

            def evacuate(tag, n, g, bank, rd, dst, pv_at):
                dve.wait_ge(sem(tag + "_pv"), pv_at)
                if g > 0:
                    dve.wait_ge(sem(tag + "_o"), (n * NG + g) * 2)
                nc_v.reciprocal(rd[:], bank[64:128, :]).then_inc(sem(tag + "_rden"), 1)
                dve.wait_ge(sem(tag + "_rden"), n * NG + g + 1)
                o4 = bank[0:64, :].rearrange("p (c t n) -> p c t n", t=2, n=N)
                r4 = rd[:].rearrange("p (c t n) -> p c t n", t=2, n=N)
                for par in range(2):
                    nc_v.tensor_tensor(dst[64 * par:64 * par + 64, 2 * g:2 * g + 2, :], o4[:, :, par, :], r4[:, :, par, :],
                                       ALU.mult).then_inc(sem(tag + "_o"), 1)

            def f_begin(n, par):
                begin("front", n, FRONT_LINKS)
                link = links["front"]
                link(nc_v.tensor_scalar(front.x[:], xs[:, n % B, :], 1.0, None, ALU.mult))
                link(nc_v.tensor_scalar(nkcs[:], NKC[:, :, n // B], 1.0, None, ALU.mult))
                link(nc_v.tensor_scalar(nvs[:], NV[:, n // B, :], 1.0, None, ALU.mult))
                link(nc_v.tensor_scalar(nkc[:, par], NKC[:, :, n // B + L], 1.0, None, ALU.mult))
                nc_v.tensor_scalar(nv[:, par], NV[:, n // B + L, :], 1.0, None, ALU.mult).then_inc(sem("null_ready"), 1)

            def f_rot(n, par):
                dve.wait_ge(sem("sa_raw"), n * 3 + 3)
                first = qraw[:, :, 0:ROT]
                pairs = first.rearrange("p h (j t) -> p h j t", t=2)
                pb = rotb.rearrange("p h (j t) -> p h j t", t=2)
                sinb = sinT.rearrange("p (j t) -> p j t", t=2).unsqueeze(1).broadcast_to([128, 17, ROT // 2, 2])
                nc_v.tensor_tensor(rota, first, cosT.unsqueeze(1).broadcast_to([128, 17, ROT]), ALU.mult)
                nc_v.tensor_tensor(pb[:, :, :, 0], pairs[:, :, :, 1], sinb[:, :, :, 0], ALU.mult)
                links["front"](nc_v.tensor_tensor(pb[:, :, :, 1], pairs[:, :, :, 0], sinb[:, :, :, 1], ALU.mult))
                nc_v.tensor_tensor(first, rota, rotb, ALU.add).then_inc(sem("sa_rot"), 1)

            def f_KT_sa(n, par):
                dve.wait_ge(sem("sa_kT"), n + 1)
                nc_v.tensor_copy(KTs[:], psLh[0][:, 0:2, :]).then_inc(sem("sa_KT"), 1)

            def weigh(g, null):
                def stage(n, par):
                    if null:
                        dve.wait_ge(sem("sa_nexp"), n * NG + g + 1)
                        nc_v.tensor_tensor(Psn[:, g % 2, :], Psn[:, g % 2, :], E0[:, g * QCOL:(g + 1) * QCOL], ALU.mult).then_inc(sem("sa_np"), 1)
                    else:
                        dve.wait_ge(sem("sa_exp"), n * NG + g + 1)
                        nc_v.tensor_tensor(Ps[:, g % 2, :], Ps[:, g % 2, :], ET[:, g * QCOL:(g + 1) * QCOL], ALU.mult).then_inc(sem("sa_p"), 1)
                return stage

            def f_out(n, par):
                out_norm(links["front"], front, "sao", n, psL[:, 0, 0:D], 0)
                link = links["front"]
                link(nc_v.tensor_scalar(xs[:, n % B, :], front.x[:], 1.0, None, ALU.mult))
                norm_rows(link, front, "ca", n)

            def f_V(t):
                def stage(n, par):
                    dve.wait_ge(sem("kv_proj"), n * 4 + t + 1)
                    nc_v.tensor_copy(V[:, par, 4 * t:4 * t + 4, 0:DH],
                                     psL[:, t % 2, :].rearrange("p (a c) -> p a c", c=128)[:, :, DH:128]).then_inc(sem("kv_v"), 1)
                return stage

            def f_kss(n, par):
                dve.wait_ge(sem("kv_sq"), n + 1)
                links["front"](nc_v.tensor_reduce(ss[:, 0:16], ksq[:], AX_X, ALU.add))
                nc_v.tensor_scalar(ssc[:, 0:16], ss[:, 0:16], 1e-24 / (UNIT * UNIT), None, ALU.max).then_inc(sem("kv_ss"), 1)

            def f_ksplit(n, par):
                dve.wait_ge(sem("kv_rn"), n + 1)
                nc_v.tensor_tensor(kn[:], kraw[:], rn[:, 0:16].unsqueeze(2).broadcast_to([128, 16, DH]), ALU.mult).then_inc(sem("kv_kn"), 1)
                dve.wait_ge(sem("kv_hi"), n + 1)
                nc_v.tensor_tensor(ks[:, :, 1, :], kn[:], ks[:, :, 0, :], ALU.subtract).then_inc(sem("kv_lo"), 1)

            def f_KT(part):
                def stage(n, par):
                    dve.wait_ge(sem("kv_T"), n * 4 + 2 * part + 2)
                    ins = nc_v.tensor_copy(KT[:, par, part, 1024:2048], psLh[1].rearrange("p t c -> p (t c)"))
                    ins.then_inc(sem("kv_KT_v"), 1)
                    if part == 1:
                        assert links["front"].k == FRONT_LINKS, links["front"].k
                return stage

            def b_out(n, par):
                begin("back", n, BACK_LINKS)
                link = links["back"]
                link(nc_v.tensor_scalar(back.x[:], xs[:, n % B, :], 1.0, None, ALU.mult))
                out_norm(link, back, "cao", n, psA[:, 0:D], 1)
                norm_rows(link, back, "ff", n)

            def b_silu(n, par):
                link = links["back"]
                dve.wait_ge(sem("ff_exp"), n + 1)
                link(nc_v.tensor_scalar(eg1[:], eg[:], 1.0, None, ALU.add))
                link(nc_v.reciprocal(hu[:], eg1[:]))
                nc_v.tensor_tensor(eg1[:], psA[:], hu[:], ALU.mult).then_inc(sem("ff_silu"), 1)

            def b_act(n, par):
                dve.wait_ge(sem("ff_up"), n + 1)
                nc_v.tensor_tensor(hu[:], psA[:], eg1[:], ALU.mult).then_inc(sem("ff_act"), 1)

            def b_end(n, par):
                dve.wait_ge(sem("ff_w2"), n + 1)
                links["back"](nc_v.tensor_tensor(xs[:, n % B, :], back.x[:], psA[:, 0:D], ALU.add))
                assert links["back"].k == BACK_LINKS, links["back"].k

            stages = {
                "f_begin": f_begin, "f_norm_sa": lambda n, par: norm_rows(links["front"], front, "sa", n),
                "f_xnT_sa": turned(front, "sa", 0, psL[:, 0, 0:128]), "f_rot": f_rot, "f_ss_sa": norms("sa", 17),
                "f_split_sa": split("sa", 17), "f_KT_sa": f_KT_sa, "f_out": f_out,
                "f_xnT_ca": turned(front, "ca", 1, psL[:, 0, 0:128]), "f_ss_ca": norms("ca", 16),
                "f_split_ca": split("ca", 16), "f_kss": f_kss, "f_ksplit": f_ksplit,
                "b_out": b_out, "b_xnT": turned(back, "ff", 2, psA[:, 0:128]), "b_silu": b_silu, "b_act": b_act, "b_end": b_end,
            }
            for g in range(NG):
                stages[f"f_sp{g}"] = weigh(g, False)
                stages[f"f_snp{g}"] = weigh(g, True)
                stages[f"f_sevac{g}"] = lambda n, par, g=g: evacuate("sa", n, g, psL[:, g % 2, :], rdens, oTs, n * NG + g + 1)
                stages[f"evac{g}"] = lambda n, par, g=g: evacuate("ca", n, g, psO[:, g % 2, :], rden, oT, (n * NG + g + 1) * CA_N)
                stages[f"f_V{g}"] = f_V(g)
            for part in range(2):
                stages[f"f_KT{part}"] = f_KT(part)
            drive(dve, PLAN_DVE, stages)

            with dve.Fori(0, B) as b:
                link = Links(dve, sem("dve_tail"), b * TAIL_LINKS)
                link(nc_v.tensor_scalar(front.x[:], xs[:, b, :], 1.0, None, ALU.mult))
                link(nc_v.tensor_reduce(ss[:, 0:1], front.x[:], AX_X, ALU.max))
                link(nc_v.reciprocal(ssc[:, 0:1], ss[:, 0:1]))
                link(nc_v.tensor_scalar(front.x[:], front.x[:], ssc[:, 0:1], None, ALU.mult))
                layernorm(link, front, "fin", b, front.x[:], front.xn[:]).then_inc(sem("fin_xn"), 1)
                dve.wait_ge(sem("fin_xT"), b + 1)
                dve.wait_ge(sem("tail_in"), 48)
                nc_v.tensor_scalar(front.xnT[:], psA[:, 0:128], TC[:, C_FINAL:C_FINAL + 1], None, ALU.mult).then_inc(sem("fin_xnT"), 1)
                dve.wait_ge(sem("fin_proj"), b + 1)
                link(nc_v.tensor_tensor(front.x[:], x_in[:, b, :], psL[:, 0, 0:D], ALU.add))
                link(layernorm(link, front, "y", b, front.x[:], yb))
                layernorm(link, front, "y2", b, yb, front.xn[:]).then_inc(sem("y2_xn"), 1)
                link(nc_v.tensor_tensor(front.x[:], front.x[:], yb, ALU.add))
                dve.wait_ge(sem("y2_xT"), b + 1)
                nc_v.tensor_scalar(front.xnT[:], psA[:, 0:128], TC[:, C_LNW:C_LNW + 1], TC[:, C_LNB:C_LNB + 1], ALU.mult, ALU.add).then_inc(sem("y2_xnT"), 1)
                dve.wait_ge(sem("t_qkv"), b + 1)
                link(nc_v.tensor_copy(tq, psL[:, 0, 0:128]))
                link(nc_v.tensor_copy(tv, psL[:, 0, 256:384]))
                link(nc_v.tensor_copy(tk, psL[:, 0, 128:256]))
                nc_v.tensor_tensor(tkm, tk.unsqueeze(1).broadcast_to([128, H, N]),
                                   hmask.unsqueeze(2).broadcast_to([128, H, N]), ALU.mult).then_inc(sem("t_km"), 1)
                dve.wait_ge(sem("t_s"), b + 1)
                for c in range(4):
                    ins = nc_v.scalar_tensor_tensor(out=ts[:, 4 * c:4 * c + 4, :], in0=psFour[c].rearrange("p (h t) -> p h t", t=N),
                                                    scalar=float(8) ** -0.5, in1=cmask.unsqueeze(1).broadcast_to([128, 4, N]),
                                                    op0=ALU.mult, op1=ALU.add)
                link(ins)
                link(nc_v.tensor_reduce(ss[:, 0:H], ts, AX_X, ALU.max))
                nc_v.tensor_tensor(ts, ts, ss[:, 0:H].unsqueeze(2).broadcast_to([128, H, N]), ALU.subtract).then_inc(sem("t_sub"), 1)
                dve.wait_ge(sem("t_exp"), b + 1)
                link(nc_v.tensor_reduce(ssc[:, 0:H], ts, AX_X, ALU.add))
                link(nc_v.reciprocal(rn[:, 0:H], ssc[:, 0:H]))
                for c in range(2, 4):
                    dve.wait_ge(sem("t_pT"), b * 4 + c + 1)
                    nc_v.tensor_copy(tkm[:, 4 * c:4 * c + 4, :].rearrange("p h t -> p (h t)"), psFour[c]).then_inc(sem("t_pT_v"), 1)
                dve.wait_ge(sem("t_pv"), b + 1)
                nc_v.tensor_tensor(front.xn[:].rearrange("p (h e) -> p h e", e=8), psA[:, 0:128].rearrange("p (h e) -> p h e", e=8),
                                   rn[:, 0:H].unsqueeze(2).broadcast_to([128, H, 8]), ALU.mult).then_inc(sem("t_o"), 1)
                dve.wait_ge(sem("t_oT"), b + 1)
                nc_v.tensor_copy(front.xnT[:], psL[:, 0, 0:128]).then_inc(sem("t_oT_sb"), 1)
                dve.wait_ge(sem("t_wo"), b + 1)
                link(nc_v.tensor_tensor(front.x[:], front.x[:], psA[:, 0:128], ALU.add))
                link(nc_v.tensor_scalar(x_in[:, b, :], front.x[:], 1.0, None, ALU.mult))
                layernorm(link, front, "z", b, front.x[:], front.xn[:]).then_inc(sem("z_xn"), 1)
                dve.wait_ge(sem("z_xT"), b + 1)
                link(nc_v.tensor_scalar(zT[:, b, :], psA[:, 0:128], 1.0, None, ALU.mult))
                assert link.k == TAIL_LINKS, link.k
            link = Links(dve, sem("dve_rec"), 0)
            nc_v.tensor_copy(cT, TC[:, C_INC:C_INC + 1].broadcast_to([128, 128])).then_inc(sem("c_ready"), 1)
            for t in range(B):
                dve.wait_ge(sem("gate_f"), t + 1)
                dve.wait_ge(sem("c_ready"), t + 1)
                link(nc_v.tensor_tensor(cf, fT, cT, ALU.mult))
                dve.wait_ge(sem("gate_g"), t + 1)
                link(nc_v.tensor_tensor(ig, iT, gT, ALU.mult))
                nc_v.tensor_tensor(cT, cf, ig, ALU.add).then_inc(sem("c_ready"), 1)
            for t in range(B):
                dve.wait_ge(sem("y_tanh"), t + 1)
                nc_v.tensor_tensor(x_in[:, t, :], x_in[:, t, :], hy[:, t, :], ALU.add).then_inc(sem("y_ready"), 1)

        @block.scalar
        def _(act):
            nc_a = nc.scalar
            act.wait_ge(sem("bias_in"), 64)
            nc_a.activation(E0, E0, ACT.Exp).then_inc(sem("E0_ready"), 1)
            for g in range(4):
                act.wait_ge(sem("ET_sub"), g + 1)
                nc_a.activation(ET[:, g * 512:(g + 1) * 512], ET[:, g * 512:(g + 1) * 512], ACT.Exp).then_inc(sem("ET_exp"), 1)
            act.wait_ge(sem("E0_ready"), 1)

            def core_step(s, n, par):
                if s >= STEPS:
                    return
                rows = 1 if s % CA_N == CA_N - 1 else 128
                act.wait_ge(sem("ca_qk"), n * STEPS + s + 1)
                if s >= PSLOTS:
                    act.wait_ge(sem("ca_pv"), n * STEPS + s - PSLOTS + 1)
                nc_a.activation(P[0:rows, s % PSLOTS, :], psS[0:rows, s % SLOTS, :], ACT.Exp, scale=SIM_SCALE).then_inc(sem("ca_exp"), 1)

            def halves(tag, heads):
                def stage(n, par):
                    act.wait_ge(sem(tag + "_qn"), n + 1)
                    if heads == 17:
                        nc_a.activation(ks_self[:, 128:192], qn[:, 16, :], ACT.Copy)
                    nc_a.activation(qs[:, 0:heads, 0, :], qn[:, 0:heads, :], ACT.Copy).then_inc(sem(tag + "_hi"), 1)
                return stage

            def queries(tag):
                def stage(n, par):
                    dst = QTs[:] if tag == "sa" else QT[:, par]
                    for i in range(2):
                        act.wait_ge(sem(tag + "_qT"), n * 2 + i + 1)
                        nc_a.activation(dst[:, i * 1024:(i + 1) * 1024], psLh[i].rearrange("p t c -> p (t c)"), ACT.Copy).then_inc(sem(tag + "_QT"), 1)
                return stage

            def raw(i, bank):
                return nc_a.activation(qraw[:, 8 * i:8 * i + 8, :].rearrange("p h d -> p (h d)"), bank, ACT.Copy)

            def f_raw_sa(n, par):
                act.wait_ge(sem("sa_proj"), n * 3 + 1)
                nc_a.activation(qraw[:, 16, :], psL[:, 1, 0:DH], ACT.Copy)
                nc_a.activation(Vs[:, 0:DH], psL[:, 1, DH:128], ACT.Copy).then_inc(sem("sa_raw"), 1)
                act.wait_ge(sem("sa_proj"), n * 3 + 2)
                raw(0, psL[:, 0, :]).then_inc(sem("sa_raw"), 1)

            def f_raw_sa2(n, par):
                act.wait_ge(sem("sa_proj"), n * 3 + 3)
                raw(1, psL[:, 1, :]).then_inc(sem("sa_raw"), 1)

            def f_raw_ca(n, par):
                for i in range(2):
                    act.wait_ge(sem("ca_proj"), n * 2 + i + 1)
                    raw(i, psL[:, i, :]).then_inc(sem("ca_raw"), 1)

            def f_sq_sa(n, par):
                act.wait_ge(sem("sa_rot"), n + 1)
                nc_a.activation(qsq[:], qraw[:], ACT.Square, scale=1.0 / UNIT).then_inc(sem("sa_sq"), 1)

            def f_sq_ca(n, par):
                act.wait_ge(sem("ca_raw"), n * 2 + 2)
                nc_a.activation(qsq[:, 0:16, :], qraw[:, 0:16, :], ACT.Square, scale=1.0 / UNIT).then_inc(sem("ca_sq"), 1)

            def self_exp(g, null):
                def stage(n, par):
                    if null:
                        act.wait_ge(sem("sa_nqk"), n * NG + g + 1)
                        nc_a.activation(Psn[:, g % 2, :], psL[0:1, g % 2, :], ACT.Exp, scale=SIM_SCALE).then_inc(sem("sa_nexp"), 1)
                    else:
                        act.wait_ge(sem("sa_qk"), n * NG + g + 1)
                        nc_a.activation(Ps[:, g % 2, :], psL[:, g % 2, :], ACT.Exp, scale=SIM_SCALE).then_inc(sem("sa_exp"), 1)
                return stage

            def f_kraw(t):
                def stage(n, par):
                    act.wait_ge(sem("kv_v"), n * 4 + t + 1)
                    nc_a.activation(kraw[:, 4 * t:4 * t + 4, :],
                                    psL[:, t % 2, :].rearrange("p (a c) -> p a c", c=128)[:, :, 0:DH], ACT.Copy).then_inc(sem("kv_raw"), 1)
                return stage

            def f_ksq(n, par):
                act.wait_ge(sem("kv_raw"), n * 4 + 4)
                nc_a.activation(ksq[:], kraw[:], ACT.Square, scale=1.0 / UNIT).then_inc(sem("kv_sq"), 1)

            def f_khi(n, par):
                act.wait_ge(sem("kv_kn"), n + 1)
                for a in (0, 2):
                    ins = nc_a.activation(ks[:, :, a, :], kn[:], ACT.Copy)
                ins.then_inc(sem("kv_hi"), 1)

            def f_KT(part):
                def stage(n, par):
                    act.wait_ge(sem("kv_T"), n * 4 + 2 * part + 1)
                    nc_a.activation(KT[:, par, part, 0:1024], psLh[0].rearrange("p t c -> p (t c)"), ACT.Copy).then_inc(sem("kv_KT_a"), 1)
                return stage

            def b_exp(n, par):
                act.wait_ge(sem("ff_gate"), n + 1)
                nc_a.activation(eg[:], psA[:], ACT.Exp, scale=-1.0).then_inc(sem("ff_exp"), 1)

            def b_hT(n, par):
                act.wait_ge(sem("ff_hT"), n + 1)
                nc_a.activation(hT[:], psA[:], ACT.Copy).then_inc(sem("ff_hT_sb"), 1)

            stages = {
                "f_raw_sa": f_raw_sa, "f_raw_sa2": f_raw_sa2, "f_sq_sa": f_sq_sa, "f_hi_sa": halves("sa", 17), "f_QT_sa": queries("sa"),
                "f_raw_ca": f_raw_ca, "f_sq_ca": f_sq_ca, "f_hi_ca": halves("ca", 16), "f_QT_ca": queries("ca"),
                "f_ksq": f_ksq, "f_khi": f_khi, "b_exp": b_exp, "b_hT": b_hT,
            }
            for g in range(NG):
                stages[f"f_se{g}"] = self_exp(g, False)
                stages[f"f_sne{g}"] = self_exp(g, True)
                stages[f"f_kraw{g}"] = f_kraw(g)
            for part in range(2):
                stages[f"f_KT{part}"] = f_KT(part)
            drive(act, PLAN_ACT, stages, core_step)

            with act.Fori(0, B) as b:
                act.wait_ge(sem("t_sub"), b + 1)
                nc_a.activation(ts, ts, ACT.Exp).then_inc(sem("t_exp"), 1)
                for c in range(2):
                    act.wait_ge(sem("t_pT"), b * 4 + c + 1)
                    nc_a.activation(tkm[:, 4 * c:4 * c + 4, :].rearrange("p h t -> p (h t)"), psFour[c], ACT.Copy).then_inc(sem("t_pT_a"), 1)
            for t in range(B):
                act.wait_ge(sem("gates"), t + 1)
                if t > 0:
                    act.wait_ge(sem("c_ready"), t + 1)
                nc_a.activation(fT, psA[:, 0:128], ACT.Sigmoid, bias=TC[:, C_BF:C_BF + 1]).then_inc(sem("gate_f"), 1)
                nc_a.activation(iT, psA[:, 128:256], ACT.Sigmoid, bias=TC[:, C_BI:C_BI + 1])
                nc_a.activation(gT, psA[:, 256:384], ACT.Tanh, bias=TC[:, C_BC:C_BC + 1]).then_inc(sem("gate_g"), 1)
            for t in range(B):
                act.wait_ge(sem("y_mm"), t + 1)
                nc_a.activation(hy[:, t, :], psFour[t][:, 0:128], ACT.Tanh).then_inc(sem("y_tanh"), 1)

        @block.tensor
        def _(pe):
            mm = nc.tensor.matmul
            pe.wait_ge(sem("ident16"), 1)
            pe.wait_ge(sem("consts_in"), 16 * 5)
            pe.wait_ge(sem("null_split"), 1)
            for i in range(2):
                ins = nc.tensor.transpose(psLh[0][:, i, 0:2 * L], nks[:, i:i + 2].rearrange("p a d -> p (a d)"), ident16[0:2 * L, 0:2 * L])
            ins.then_inc(sem("null_T"), 1)
            mm(psL[0:H, 1, 0:N], emb_sb[:], onehot, start=True, stop=True).then_inc(sem("bias_mm"), 1)
            pe.wait_ge(sem("bias_in"), 64)
            for g in range(4):
                mm(psFour[g], flip, toeplitz[g // 2][:, (g % 2) * 512:(g % 2) * 512 + 512], start=True, stop=True).then_inc(sem("flip_mm"), 1)

            def turn_x(rows, tag, bank, n):
                pe.wait_ge(sem(tag + "_xn"), n + 1)
                nc.tensor.transpose(bank[:, 0:128], rows.xn[:], ident).then_inc(sem(tag + "_xT"), 1)

            def turn_q(tag):
                def stage(n, par):
                    pe.wait_ge(sem(tag + "_lo"), n + 1)
                    for i in range(2):
                        for h in range(8):
                            ins = nc.tensor.transpose(psLh[i][:, h, :], qs[:, 8 * i + h].rearrange("p a d -> p (a d)"), ident16[:])
                        ins.then_inc(sem(tag + "_qT"), 1)
                return stage

            def scores(bank, rows, keys, q):
                for part in range(2):
                    ins = mm(bank[0:rows, :], keys[part], q, start=(part == 0), stop=(part == 1))
                return ins

            def core_step(s, n, par):
                base = n * STEPS
                if s == 0:
                    pe.wait_ge(sem("ca_QT"), n * 2 + 2)
                    pe.wait_ge(sem("kv_KT_a"), n * 2 + 2)
                    pe.wait_ge(sem("kv_KT_v"), n * 2 + 2)
                    pe.wait_ge(sem("null_ready"), n + 1)
                    pe.wait_ge(sem("kv_v"), n * 4 + 4)
                if s < STEPS:
                    g, j = s // CA_N, s % CA_N
                    if s >= SLOTS:
                        pe.wait_ge(sem("ca_exp"), base + s - SLOTS + 1)
                    null = j == CA_N - 1
                    keys = [nkc[:, par, p:p + 1] if null else KT[:, par, p, 128 * j:128 * j + 128] for p in range(2)]
                    scores(psS[:, s % SLOTS, :], 1 if null else 128, keys, QT[:, par, g * QCOL:(g + 1) * QCOL]).then_inc(sem("ca_qk"), 1)
                s2 = s - AHEAD
                if 0 <= s2 < STEPS:
                    g, j = s2 // CA_N, s2 % CA_N
                    if j == 0 and (g >= 2 or not isinstance(n, int) or n > 0):
                        pe.wait_ge(sem("ca_o"), n * NG * 2 + 2 * (g - 1))
                    pe.wait_ge(sem("ca_exp"), base + s2 + 1)
                    if j < CA_N - 1:
                        ins = mm(psO[:, g % 2, :], V[:, par, j, :], P[:, s2 % PSLOTS, :], start=(j == 0), stop=False)
                    else:
                        ins = mm(psO[:, g % 2, :], nv[:, par], P[0:1, s2 % PSLOTS, :], start=False, stop=True)
                    ins.then_inc(sem("ca_pv"), 1)

            def weights(n, a, b):
                return W[:, (n // B) % 2, a:b]

            def f_proj_sa(n, par):
                pe.wait_ge(sem("w_in"), (n // B + 1) * 16)
                pe.wait_ge(sem("sa_xnT"), n + 1)
                mm(psL[:, 1, 0:128], front.xnT[:], weights(n, W_SAKV, W_SAKV + 128), start=True, stop=True).then_inc(sem("sa_proj"), 1)
                mm(psL[:, 0, :], front.xnT[:], weights(n, W_SAQ, W_SAQ + 512), start=True, stop=True).then_inc(sem("sa_proj"), 1)

            def f_proj_sa2(n, par):
                pe.wait_ge(sem("sa_raw"), n * 3 + 1)
                mm(psL[:, 1, :], front.xnT[:], weights(n, W_SAQ + 512, W_SAQ + 1024), start=True, stop=True).then_inc(sem("sa_proj"), 1)

            def f_turn_k_sa(n, par):
                pe.wait_ge(sem("sa_QT"), n * 2 + 1)
                for i in range(2):
                    ins = nc.tensor.transpose(psLh[0][:, i, :], ks_self[:, DH * i:DH * i + 128], ident16[:])
                ins.then_inc(sem("sa_kT"), 1)

            def self_key(g):
                def stage(n, par):
                    pe.wait_ge(sem("sa_QT"), n * 2 + 2)
                    pe.wait_ge(sem("sa_KT"), n + 1)
                    if g >= 2:
                        pe.wait_ge(sem("sa_o"), n * NG * 2 + 2 * (g - 1))
                    scores(psL[:, g % 2, :], 128, [KTs[:, p, :] for p in range(2)], QTs[:, g * QCOL:(g + 1) * QCOL]).then_inc(sem("sa_qk"), 1)
                return stage

            def self_null(g):
                def stage(n, par):
                    pe.wait_ge(sem("null_ready"), n + 1)
                    pe.wait_ge(sem("sa_exp"), n * NG + g + 1)
                    scores(psL[:, g % 2, :], 1, [nkcs[:, p:p + 1] for p in range(2)], QTs[:, g * QCOL:(g + 1) * QCOL]).then_inc(sem("sa_nqk"), 1)
                return stage

            def self_sum(g):
                def stage(n, par):
                    pe.wait_ge(sem("sa_p"), n * NG + g + 1)
                    pe.wait_ge(sem("sa_np"), n * NG + g + 1)
                    mm(psL[:, g % 2, :], Vs[:], Ps[:, g % 2, :], start=True, stop=False)
                    mm(psL[:, g % 2, :], nvs[:], Psn[:, g % 2, :], start=False, stop=True).then_inc(sem("sa_pv"), 1)
                return stage

            def project_out(bank, o, tag, done, w):
                def stage(n, par):
                    pe.wait_ge(sem(tag + "_o"), n * NG * 2 + 2 * NG)
                    for c in range(H // 2):
                        ins = mm(bank[:, 0:D], o[:, c, :], weights(n, w + c * D, w + (c + 1) * D), start=(c == 0), stop=(c == H // 2 - 1))
                    ins.then_inc(sem(done), 1)
                return stage

            def f_proj_ca(n, par):
                pe.wait_ge(sem("ca_xnT"), n + 1)
                for i in range(2):
                    mm(psL[:, i, :], front.xnT[:], weights(n, W_CAQ + 512 * i, W_CAQ + 512 * i + 512), start=True, stop=True).then_inc(sem("ca_proj"), 1)

            def f_kv(t):
                def stage(n, par):
                    pe.wait_ge(sem("ctx_in"), n * 16 + 16)
                    if t >= 2:
                        pe.wait_ge(sem("kv_raw"), n * 4 + t - 1)
                    else:
                        pe.wait_ge(sem("ca_raw"), n * 2 + 2)
                    for a in range(4):
                        k = 4 * t + a
                        ins = mm(psL[:, t % 2, a * 128:(a + 1) * 128], ctx_sb[:, k * 128:(k + 1) * 128],
                                 weights(n, W_CAKV, W_CAKV + 128), start=True, stop=True)
                    ins.then_inc(sem("kv_proj"), 1)
                return stage

            def f_turn_q_ca(n, par):
                pe.wait_ge(sem("kv_raw"), n * 4 + 4)
                turn_q("ca")(n, par)

            def f_turn_k(part):
                def stage(n, par):
                    pe.wait_ge(sem("kv_lo"), n + 1)
                    for i in range(2):
                        if part == 1:
                            pe.wait_ge(sem("kv_KT_a" if i == 0 else "kv_KT_v"), n * 2 + 1)
                        else:
                            pe.wait_ge(sem("ca_QT"), n * 2 + i + 1)
                        for t in range(8):
                            ins = nc.tensor.transpose(psLh[i][:, t, :], ks[:, 8 * i + t, part:part + 2, :].rearrange("p a d -> p (a d)"), ident16[:])
                        ins.then_inc(sem("kv_T"), 1)
                return stage

            def b_gate(n, par):
                pe.wait_ge(sem("ff_xnT"), n + 1)
                mm(psA[:], back.xnT[:], weights(n, W_FF1 + 512, W_FF1 + 1024), start=True, stop=True).then_inc(sem("ff_gate"), 1)

            def b_up(n, par):
                pe.wait_ge(sem("ff_silu"), n + 1)
                mm(psA[:], back.xnT[:], weights(n, W_FF1, W_FF1 + 512), start=True, stop=True).then_inc(sem("ff_up"), 1)

            def b_turn_h(n, par):
                pe.wait_ge(sem("ff_act"), n + 1)
                for c in range(4):
                    ins = nc.tensor.transpose(psA[:, c * 128:(c + 1) * 128], hu[:, c * 128:(c + 1) * 128], ident)
                ins.then_inc(sem("ff_hT"), 1)

            def b_down(n, par):
                pe.wait_ge(sem("ff_hT_sb"), n + 1)
                for c in range(4):
                    ins = mm(psA[:, 0:D], hT[:, c * 128:(c + 1) * 128], weights(n, W_FF2 + c * D, W_FF2 + (c + 1) * D),
                             start=(c == 0), stop=(c == 3))
                ins.then_inc(sem("ff_w2"), 1)

            stages = {
                "f_turn_sa": lambda n, par: turn_x(front, "sa", psL[:, 0, :], n), "f_proj_sa": f_proj_sa, "f_proj_sa2": f_proj_sa2,
                "f_turn_q_sa": turn_q("sa"), "f_turn_k_sa": f_turn_k_sa,
                "f_wo": project_out(psL[:, 0, :], oTs, "sa", "sao_wo", W_SAO),
                "f_turn_ca": lambda n, par: turn_x(front, "ca", psL[:, 0, :], n), "f_proj_ca": f_proj_ca, "f_turn_q_ca": f_turn_q_ca,
                "b_wo": project_out(psA[:], oT, "ca", "cao_wo", W_CAO),
                "b_turn": lambda n, par: turn_x(back, "ff", psA[:], n),
                "b_gate": b_gate, "b_up": b_up, "b_turn_h": b_turn_h, "b_down": b_down,
            }
            for g in range(NG):
                stages[f"f_sk{g}"] = self_key(g)
                stages[f"f_sn{g}"] = self_null(g)
                stages[f"f_sv{g}"] = self_sum(g)
                stages[f"f_kv{g}"] = f_kv(g)
            for part in range(2):
                stages[f"f_turn_k{part}"] = f_turn_k(part)
            drive(pe, PLAN_PE, stages, core_step)

            def tail_w(k):
                return TW[:, k, :]

            pe.wait_ge(sem("tail_in"), 48)
            with pe.Fori(0, B) as b:
                turn_x(front, "fin", psA[:], b)
                pe.wait_ge(sem("fin_xnT"), b + 1)
                mm(psL[:, 0, 0:D], front.xnT[:], tail_w(T_PROJ), start=True, stop=True).then_inc(sem("fin_proj"), 1)
                turn_x(front, "y2", psA[:], b)
                pe.wait_ge(sem("y2_xnT"), b + 1)
                mm(psL[:, 0, 0:128], tail_w(T_Q), front.xnT[:], start=True, stop=True)
                mm(psL[:, 0, 128:256], tail_w(T_K), front.xnT[:], start=True, stop=True)
                mm(psL[:, 0, 256:384], front.xnT[:], tail_w(T_V), start=True, stop=True).then_inc(sem("t_qkv"), 1)
                pe.wait_ge(sem("t_km"), b + 1)
                for c in range(4):
                    ins = mm(psFour[c], tq, tkm[:, 4 * c:4 * c + 4, :].rearrange("p h t -> p (h t)"), start=True, stop=True)
                ins.then_inc(sem("t_s"), 1)
                pe.wait_ge(sem("t_exp"), b + 1)
                for c in range(4):
                    for h in range(4 * c, 4 * c + 4):
                        ins = nc.tensor.transpose(psFour[c][:, (h % 4) * 128:(h % 4) * 128 + 128], ts[:, h, :], ident)
                    ins.then_inc(sem("t_pT"), 1)
                pe.wait_ge(sem("t_pT_a"), b * 2 + 2)
                pe.wait_ge(sem("t_pT_v"), b * 2 + 2)
                for h in range(H):
                    ins = mm(psA[:, 8 * h:8 * h + 8], tkm[:, h, :], tv[:, 8 * h:8 * h + 8], start=True, stop=True)
                ins.then_inc(sem("t_pv"), 1)
                pe.wait_ge(sem("t_o"), b + 1)
                nc.tensor.transpose(psL[:, 0, 0:128], front.xn[:], ident).then_inc(sem("t_oT"), 1)
                pe.wait_ge(sem("t_oT_sb"), b + 1)
                mm(psA[:, 0:D], front.xnT[:], tail_w(T_O), start=True, stop=True).then_inc(sem("t_wo"), 1)
                turn_x(front, "z", psA[:], b)
            pe.wait_ge(sem("dve_tail"), B * TAIL_LINKS)
            for t in range(B):
                pe.wait_ge(sem("c_ready"), t + 1)
                if t > 0:
                    pe.wait_ge(sem("gate_g"), t)
                for k, (w, u) in enumerate(((T_WF, T_UF), (T_WI, T_UI), (T_WC, T_UC))):
                    mm(psA[:, 128 * k:128 * k + 128], tail_w(w), zT[:, t, :], start=True, stop=False)
                    ins = mm(psA[:, 128 * k:128 * k + 128], tail_w(u), cT, start=False, stop=True)
                ins.then_inc(sem("gates"), 1)
            pe.wait_ge(sem("c_ready"), B + 1)
            for t in range(B):
                mm(psFour[t][:, 0:128], zT[:, t, :], tail_w(T_WO), start=True, stop=False)
                mm(psFour[t][:, 0:128], cT, tail_w(T_UO), start=False, stop=False)
                mm(psFour[t][:, 0:128], ones[:], bo_row[:], start=False, stop=True).then_inc(sem("y_mm"), 1)


_OUTS = [((4, 128, 128), 'float32')]


def constants(np):
    c = np.zeros((128, C_END), np.float32)
    c[:, 0:128] = np.eye(128)
    c[:, 128:256] = np.eye(128)[::-1]
    c[:, 256:384] = np.where(np.arange(128)[None, :] > np.arange(128)[:, None], -3.0e38, 0.0)
    neg = np.arange(N)
    safe = np.maximum(neg, 1).astype(np.float32)
    large = 16 + (np.log(safe / np.float32(16)) / np.float32(np.log(128 / 16)) * np.float32(16)).astype(np.int32)
    bucket = np.where(neg < 16, neg, np.minimum(large, NBUCK - 1))
    c[bucket, 384 + neg] = 1.0
    inv = (1.0 / 10000.0 ** (np.arange(0, ROT, 2, dtype=np.float32) / ROT)).astype(np.float32)
    f = np.arange(N, dtype=np.float32)[:, None] * inv[None, :]
    c[:, 512:544] = np.repeat(np.cos(f), 2, axis=-1)
    c[:, 544:576] = np.stack((-np.sin(f), np.sin(f)), -1).reshape(N, ROT)
    c[:, 576:592] = np.arange(128)[:, None] // 8 == np.arange(16)[None, :]
    return c


def kernel(**inputs):
    import numpy as np
    import concourse.bacc as _bacc
    from concourse.bass_utils import run_bass_kernel_spmd as _run

    t = {k: np.asarray(v) for k, v in inputs.items()}
    xa = {k[9:]: v for k, v in t.items() if k.startswith("L0_xattn_")}
    at = {k[8:]: v for k, v in t.items() if k.startswith("L0_attn_")}
    ff = {k[7:]: v for k, v in t.items() if k.startswith("L0_ffn_")}

    def rows(w, c):
        return w.reshape(L, c, 128, -1).transpose(0, 2, 1, 3).reshape(L, 128, -1)

    def heads(w):
        return w.transpose(1, 0, 2).reshape(128, 128)

    arrays = {
        "x": t["x"],
        "ctxT": t["ctx_1024"].transpose(0, 2, 1),
        "wpack": np.concatenate([xa["sa_wq"], xa["sa_wkv"], rows(xa["sa_wo"], 8), xa["ca_wq"], xa["ca_wkv"],
                                 rows(xa["ca_wo"], 8), xa["ff_w1"], rows(xa["ff_w2"], 4)], axis=2),
        "gcols": np.stack([xa["sa_norm_g"], xa["ca_norm_g"], xa["ff_norm_g"]], 1).transpose(2, 0, 1),
        "gout": np.stack([xa["sa_out_g"], xa["ca_out_g"]], 1),
        "null_k": np.concatenate([xa["sa_null_kv"][:, 0], xa["ca_null_kv"][:, 0]], 0),
        "null_v": np.concatenate([xa["sa_null_kv"][:, 1], xa["ca_null_kv"][:, 1]], 0)[None],
        "tail_w": np.stack([xa["proj_w"], heads(at["wq"]), heads(at["wk"]), heads(at["wv"]), at["wo"],
                            ff["wf"].T, ff["wi"].T, ff["wc"].T, ff["uf"].T, ff["ui"].T, ff["uc"].T,
                            ff["wo"].T, ff["uo"].T], 1),
        "tail_cols": np.stack([xa["final_g"], at["ln_w"], at["ln_b"], ff["bf"], ff["bi"], ff["bc"], ff["in_c"]], 1),
        "bo": ff["bo"][None],
        "emb": xa["rel_pos_emb"],
        "c_pack": constants(np),
    }
    arrays = {k: np.ascontiguousarray(v) for k, v in arrays.items()}
    nc = _bacc.Bacc("TRN2", target_bir_lowering=False, num_devices=1)
    args = [nc.dram_tensor(k, v.shape, mybir.dt.from_np(v.dtype), kind="ExternalInput").ap() for k, v in arrays.items()]
    outs = [nc.dram_tensor(f"out_{i}", shape, mybir.dt.from_np(np.dtype(d)), kind="ExternalOutput").ap()
            for i, (shape, d) in enumerate(_OUTS)]
    build(nc, *args, *outs)
    r = _run(nc, [arrays], core_ids=[0])
    return r.results[0]["out_0"]
```

```python
from contextlib import ExitStack

import concourse.bass as bass
from concourse import mybir

ALU = mybir.AluOpType
ACT = mybir.ActivationFunctionType
F32 = mybir.dt.float32
F16 = mybir.dt.float16
F32R = mybir.dt.float32r
AX_X = mybir.AxisListType.X

L, B, N, D = 6, 4, 128, 128
H, DH, ROT = 16, 64, 32
M = 2048
KT_N = M // 128
FF = 512
NBUCK = 32
EPS = 1e-5
GH = 4
NG = H // GH
QCOL = GH * N
UNIT = 1024.0
SIM_SCALE = 16.0 / (UNIT * UNIT)
RUNS = L * B
CA_N = KT_N + 1
SLOTS = 3
PSLOTS = 4
HSLOTS = 8
AHEAD = 6
LOW = 1

W_SAQ, W_SAKV, W_SAO, W_CAQ, W_CAKV, W_CAO, W_FF1, W_FF2, W_END = 0, 1024, 1152, 2176, 3200, 3328, 4352, 5376, 5888
T_PROJ, T_Q, T_K, T_V, T_O, T_WF, T_WI, T_WC, T_UF, T_UI, T_UC, T_WO, T_UO = range(13)
C_END = 592
C_FINAL, C_LNW, C_LNB, C_BF, C_BI, C_BC, C_INC = range(7)


class Links:

    def __init__(self, eng, sem, base):
        self.eng, self.sem, self.base, self.k = eng, sem, base, 0

    def __call__(self, ins):
        self.k += 1
        ins.then_inc(self.sem, 1)
        self.eng.wait_ge(self.sem, self.base + self.k)


def build(nc, x, ctxT, wpack, gcols, gout, null_k, null_v, tail_w, tail_cols, bo, emb,
          c_pack, out):
    with ExitStack() as ctx:
        def sb(name, shape, dt=F32):
            return ctx.enter_context(nc.sbuf_tensor(name, shape, dt))

        def psum(name, shape):
            return ctx.enter_context(nc.psum_tensor(name, shape, F32))

        sems = {}

        def sem(name):
            if name not in sems:
                sems[name] = ctx.enter_context(nc.semaphore(name))
            return sems[name]

        def dram(name, shape):
            return nc.dram_tensor(name, shape, F32, kind="Internal").ap()

        psS = psum("psS", [128, SLOTS, 512])
        psO = psum("psO", [128, 2, 512])
        psA = psum("psA", [128, 512])
        psL = psum("psL", [128, 2, 512])
        psLh = [psL[:, i, :].bitcast(F16).rearrange("p (t c) -> p t c", c=128) for i in range(2)]
        psFour = [psA[:], psL[:, 0, :], psL[:, 1, :], psO[:, 0, :]]

        C = sb("C", [128, C_END])
        ident = C[:, 0:128]
        flip = C[:, 128:256]
        cmask = C[:, 256:384]
        onehot = C[0:NBUCK, 384:512]
        cosT = C[:, 512:544]
        sinT = C[:, 544:576]
        hmask = C[:, 576:592]
        ident16 = sb("ident16", [128, 128], F16)
        emb_sb = sb("emb_sb", [NBUCK, H])
        neghalf = sb("neghalf", [128, 17])
        tiny = sb("tiny", [128, 17])
        gcol = sb("gcol", [128, L, 3])
        W = sb("W", [128, W_END])
        TW = W[:, 0:13 * 128].rearrange("p (k n) -> p k n", n=128)
        gsa = sb("gsa", [128, D])
        gca = sb("gca", [128, D])
        TC = sb("TC", [128, 7])
        bo_row = sb("bo_row", [1, 128])
        ones = sb("ones", [1, 128])
        x_in = sb("x_in", [128, B, D])
        xs = sb("xs", [128, B, D])

        class Rows:

            def __init__(self, tag):
                self.fence = sb(tag + "_fence", [1, 1])
                self.stats = sb(tag + "_stats", [128, 6])
                self.mv = sb(tag + "_mv", [128, 2])
                self.ve = sb(tag + "_ve", [128, 1])
                self.rstd = sb(tag + "_rstd", [128, 1])
                self.x = sb(tag + "_x", [128, D])
                self.xn = sb(tag + "_xn", [128, D])
                self.xnT = sb(tag + "_xnT", [128, 128])

        front = Rows("front")
        back = Rows("back")
        qraw = sb("qraw", [128, 17, DH])
        qsq = sb("qsq", [128, 17, DH])
        ss = sb("ss", [128, 17])
        ssc = sb("ssc", [128, 17])
        rn = sb("rn", [128, 17])
        qn = qsq
        rota, rotb = qsq[:, :, 0:ROT], qsq[:, :, ROT:2 * ROT]
        qs_all = sb("qs_all", [128, 17 * 2 * DH + DH], F16)
        qs = qs_all[:, 0:17 * 2 * DH].rearrange("p (h a d) -> p h a d", a=2, d=DH)
        ks_self = qs_all[:, 16 * 2 * DH:]
        QTs = sb("QTs", [128, H * N], F16)
        QT = sb("QT", [128, 2, H * N], F16)
        KTs = sb("KTs", [128, 2, 128], F16)
        Vs = sb("Vs", [128, 128])
        ctx_sb = sb("ctx_sb", [128, M])
        kraw = sb("kraw", [128, KT_N, DH])
        ksq = sb("ksq", [128, KT_N, DH])
        kn = ksq
        ks = sb("ks", [128, KT_N, 3, DH], F16)
        KT = sb("KT", [128, 2, 2, M], F16)
        V = sb("V", [128, 2, KT_N, 128], F32R)
        VL = sb("VL", [128, 2, KT_N, DH], F32R)
        nk = sb("nk", [2 * L, DH])
        nksq = sb("nksq", [2 * L, DH])
        nkn = sb("nkn", [2 * L, DH])
        nks = sb("nks", [2 * L, 3, DH], F16)
        NKC = sb("NKC", [128, 2, 2 * L], F16)
        nkcs = sb("nkcs", [128, 2], F16)
        nkc = sb("nkc", [128, 2, 2], F16)
        rows_sb = sb("rows_sb", [33, H * N])
        E0 = rows_sb[0:1, :]
        NV = rows_sb[32:33, 0:2 * L * 128].rearrange("p (l d) -> p l d", d=128)
        nvs = sb("nvs", [1, 128])
        nv = sb("nv", [1, 2, 128])
        ET = sb("ET", [128, H * N])
        P = sb("P", [128, PSLOTS, QCOL])
        PH = sb("PH", [128, HSLOTS, QCOL], F32R)
        PL = sb("PL", [128, HSLOTS, QCOL], F32R)
        Pn = sb("Pn", [1, QCOL])
        rden = sb("rden", [64, 3, N])
        oT = sb("oT", [128, H // 2, N])
        Ps = sb("Ps", [128, 2, QCOL])
        Psn = sb("Psn", [1, 2, QCOL])
        rdens = sb("rdens", [64, 3, N])
        oTs = sb("oTs", [128, H // 2, N])
        eg1 = sb("eg1", [128, FF])
        hu = sb("hu", [128, FF])
        eg = hT = eg1
        cT, cf, ig, fT, iT, gT = (W[:, W_CAO + 128 * k:W_CAO + 128 * k + 128] for k in range(6))
        zT, hy = (W[:, W_FF1 + 512 + 512 * k:W_FF1 + 1024 + 512 * k].rearrange("p (b d) -> p b d", d=D) for k in range(2))

        class Tail:

            def __init__(self, k, rows, banks, s, keys):
                self.rows, self.banks = rows, banks
                self.y, self.q, self.k, self.v = (W[:, 13 * 128 + 512 * k + 128 * i:13 * 128 + 512 * k + 128 * i + 128] for i in range(4))
                self.s, self.km = (t.rearrange("p (h t) -> p h t", t=N) for t in (s, keys))
                self.peak, self.sum, self.inv = (sb(f"tail{k}_{name}", [128, H]) for name in ("peak", "sum", "inv"))

        tails = [Tail(0, front, psFour, ctx_sb[:], ET[:]),
                 Tail(1, back, [psS[:, 0, :], psS[:, 1, :], psS[:, 2, :], psO[:, 1, :]],
                      P[:].rearrange("p a c -> p (a c)"), QT[:].rearrange("p a c -> p (a c)").bitcast(F32))]
        toeplitz = [kraw[:].rearrange("p a d -> p (a d)"), ksq[:].rearrange("p a d -> p (a d)")]
        rowmax = ctx_sb[:]
        biasW = dram("biasW", [H, 256])
        biasM = dram("biasM", [H, N])
        bias0 = dram("bias0", [H, N])

        block = ctx.enter_context(nc.Block())

        FRONT_LINKS, BACK_LINKS = 14, 12
        POOL_CONSTS = 5
        TAIL_LINKS = 25
        STEPS = NG * CA_N
        TILES = NG * KT_N

        def tile(s):
            return s // CA_N * KT_N + s % CA_N

        def is_null(s):
            return s % CA_N == CA_N - 1

        def at(s, core, back):
            if s < 0:
                return (STEPS + s, *back) if back is not None else None
            return (s, *core) if core is not None else None

        def slot(s, par, slots):
            assert 2 * STEPS % slots == 0
            return (STEPS * par + s) % slots

        PLAN_PE = {
            4: ["f_turn_sa"], 5: ["f_proj_sa", "f_proj_sa2", "f_kv0"], 7: ["f_kv1"], 10: ["f_kv2"], 14: ["f_kv3"],
            15: ["b_wo"], 16: ["f_turn_q_sa"], 19: ["b_turn"], 20: ["b_gate"], 21: ["f_turn_k_sa"], 24: ["f_sk0"],
            26: ["f_sk1"], 27: ["f_sn0", "f_sn1"], 28: ["f_sv0"], 32: ["f_sv1", "b_up"], 34: ["f_sk2", "f_sn2"],
            39: ["f_sv2", "f_sk3"], 40: ["b_turn_h"], 43: ["f_sn3"], 45: ["f_sv3"], 50: ["f_wo"], 52: ["b_down"],
            54: ["f_turn_ca"], 55: ["f_proj_ca", "f_turn_k0"], 59: ["f_turn_k1"], 65: ["f_turn_q_ca"],
        }
        PLAN_ACT = {
            4: ["f_raw_sa", "f_raw_sa2"], 8: ["f_kraw0", "f_sq_sa"], 10: ["f_kraw1"],
            14: ["f_hi_sa", "f_kraw2", "f_kraw3"], 15: ["f_ksq"], 18: ["f_QT_sa"], 21: ["b_exp"], 22: ["f_khi"],
            23: ["f_se0"], 24: ["f_se1"], 25: ["f_sne0"], 28: ["f_sne1"], 32: ["f_se2"], 33: ["f_sne2"], 38: ["f_se3"],
            39: ["b_hT"], 43: ["f_sne3"], 54: ["f_raw_ca"], 55: ["f_KT0", "f_sq_ca"], 59: ["f_KT1"], 61: ["f_hi_ca"],
            65: ["f_QT_ca"],
        }
        PLAN_DVE = {
            0: ["f_begin", "f_norm_sa"], 1: ["f_xnT_sa"], 3: ["b_e12", "b_e13"], 4: ["b_e14"], 6: ["f_V0", "f_V1"],
            7: ["b_e15"], 8: ["f_ss_sa"], 11: ["f_V2"], 12: ["f_unit_sa"], 13: ["f_V3"], 15: ["b_out", "f_kss"],
            17: ["b_xnT"], 18: ["f_null"], 19: ["f_kunit"], 22: ["f_KT_sa", "e0"], 23: ["e1"], 24: ["f_sp0", "b_one"],
            25: ["b_silu", "f_sp1"], 27: ["f_se0", "f_se1", "e2"], 28: ["f_se2", "f_se3"], 29: ["b_act"],
            32: ["f_se4", "f_se5"], 33: ["f_se6", "f_sp2"], 34: ["f_se7"], 36: ["e3", "f_se8"], 39: ["f_sp3"],
            42: ["f_se9"], 43: ["f_se10"], 44: ["f_se11"], 45: ["f_se12", "f_se13"], 46: ["f_se14", "f_se15"],
            49: ["e4", "f_out"], 50: ["f_xnT_ca"], 52: ["e5", "e6"], 53: ["e7"], 56: ["f_ss_ca", "f_KT0"], 58: ["e8"],
            59: ["f_unit_ca"], 60: ["b_end", "e9"], 61: ["f_KT1"], 62: ["e10"], 65: ["e11"],
        }
        PLAN_POOL = {
            0: ["f_sa"], 1: ["f_rot"], 5: ["f_sa_q"], 7: ["f_low_sa"], 8: ["b_out"], 12: ["b_ff"], 14: ["f_kv"],
            17: ["f_snp0"], 20: ["f_klow"], 22: ["f_snp1", "f_snp2"], 26: ["f_snp3"], 32: ["f_out"], 34: ["f_ca"],
            39: ["f_ca_q"], 60: ["f_low_ca"],
        }

        def drive(eng, plan, stages, core_step=None):
            def window(core, back, front):
                for s in range(STEPS):
                    if core_step is not None:
                        core_step(s, core, back)
                    for name in plan.get(s, ()):
                        part = {"b": back, "f": front, "e": core}[name[0]]
                        if part is not None:
                            stages[name](*part)

            window(None, None, (0, 0))
            window((0, 0), None, (1, 1))
            with eng.Fori(0, (RUNS - 2) // 2) as k:
                window((k * 2 + 1, 1), (k * 2, 0), (k * 2 + 2, 0))
                window((k * 2 + 2, 0), (k * 2 + 1, 1), (k * 2 + 3, 1))
            window((RUNS - 1, 1), (RUNS - 2, 0), None)
            window(None, (RUNS - 1, 1), None)

        @block.sync
        def _(sp):
            for dst, src in ((C[:], c_pack), (emb_sb[:], emb), (gcol[:], gcols), (nk[:], null_k),
                             (NV[:, :, 0:DH], null_v)):
                sp.dma_start(dst, src).then_inc(sem("consts_in"), 16)
            sp.dma_start(x_in[:], x.rearrange("b p d -> p b d")).then_inc(sem("x_in"), 16)

            def front_weights(l):
                sp.dma_start(W[:, 0:W_CAO], wpack[l, :, 0:W_CAO]).then_inc(sem("w_front"), 16)
                sp.dma_start(gsa[:], gout[l, 0].partition_broadcast(128)).then_inc(sem("w_front"), 16)

            def back_weights(l):
                sp.dma_start(W[:, W_CAO:W_END], wpack[l, :, W_CAO:W_END]).then_inc(sem("w_back"), 16)
                sp.dma_start(gca[:], gout[l, 1].partition_broadcast(128)).then_inc(sem("w_back"), 16)

            front_weights(0)
            back_weights(0)
            sp.wait_ge(sem("bias_ready"), 2)
            sp.dma_start(biasW, ET[0:H, 0:256]).then_inc(sem("bias_out"), 16)
            sp.dma_start(biasM, ET[0:H, 256:384]).then_inc(sem("bias_out"), 16)
            sp.dma_start(bias0, ET[0:H, 384:512]).then_inc(sem("bias_out"), 16)
            sp.wait_ge(sem("bias_out"), 48)
            for i in range(2):
                sp.dma_start(toeplitz[i].rearrange("p (h n) -> p h n", n=N),
                             bass.AP(biasW.tensor, 256 * (H // 2) * i, [[1, 128], [256, H // 2], [1, N]])).then_inc(sem("bias_in"), 16)
            sp.dma_start(rowmax, bass.AP(biasM.tensor, 0, [[0, 128], [1, H * N]])).then_inc(sem("bias_in"), 16)
            sp.dma_start(E0, bass.AP(bias0.tensor, 0, [[0, 1], [1, H * N]])).then_inc(sem("bias_in"), 16)
            sp.dma_start(TC[:], tail_cols).then_inc(sem("tail_in"), 16)
            sp.dma_start(bo_row[:], bo).then_inc(sem("tail_in"), 16)
            sp.wait_ge(sem("ET_sub"), 4)
            sp.dma_start(ctx_sb[:], ctxT[0]).then_inc(sem("ctx_in"), 16)

            def context(n):
                sp.wait_ge(sem("kv_proj"), n * 4)
                sp.dma_start(ctx_sb[:], ctxT[n % B]).then_inc(sem("ctx_in"), 16)

            for n in range(1, B):
                context(n)
            with sp.Fori(1, L) as l:
                context(l * B)
                sp.wait_ge(sem("ca_proj"), l * B * 2)
                front_weights(l)
                context(l * B + 1)
                sp.wait_ge(sem("ff_w2"), l * B)
                back_weights(l)
                context(l * B + 2)
                context(l * B + 3)
            sp.wait_ge(sem("ca_proj"), RUNS * 2)
            sp.dma_start(TW, tail_w).then_inc(sem("tail_in"), 16)
            for b in range(B):
                sp.wait_ge(sem("y_ready"), b + 1)
                sp.dma_start(out[b], x_in[:, b, :]).then_inc(sem("out"), 16)
            sp.wait_ge(sem("out"), 16 * B)

        @block.gpsimd
        def _(pool):
            nc.gpsimd.memset(neghalf[:], -0.5).then_inc(sem("pool_consts"), 1)
            nc.gpsimd.memset(Vs[:, DH:128], 1.0).then_inc(sem("pool_consts"), 1)
            nc.gpsimd.memset(tiny[:, 0:16], 1e-24 / 256.0 / (UNIT * UNIT)).then_inc(sem("pool_consts"), 1)
            nc.gpsimd.memset(tiny[:, 16:17], 1e-24 / (UNIT * UNIT)).then_inc(sem("pool_consts"), 1)
            nc.gpsimd.memset(ones[:], 1.0).then_inc(sem("pool_consts"), 1)
            pool.wait_ge(sem("pool_consts"), POOL_CONSTS)

            def power(out_, in_, width, ready, ready_at, done):
                pool.wait_ge(sem(ready), ready_at)
                nc.gpsimd.tensor_tensor(out_, in_, neghalf[0:out_.shape[0], 0:width], ALU.pow).then_inc(sem(done), 1)

            power(rn[0:12, 0:1], ssc[0:12, 0:1], 1, "null_ss", 1, "null_rn")
            nc.gpsimd.memset(V[:, :, :, DH:128].bitcast(F32), 1.0).then_inc(sem("V_ones"), 1)
            for b in range(B):
                power(front.rstd[:], front.ve[:], 1, "in_var", b + 1, "in_rstd")
            pool.wait_ge(sem("ET_exp"), 4)
            nc.gpsimd.affine_select(out=ET[:].rearrange("p (h i) -> p h i", h=H), in_=ET[:].rearrange("p (h i) -> p h i", h=H),
                                    compare_op=ALU.is_ge, fill=0.0, base=0, pattern=[[0, H], [1, N]],
                                    channel_multiplier=-1).then_inc(sem("ET_ready"), 1)

            def row_power(rows, tag):
                return lambda n, par: power(rows.rstd[:], rows.ve[:], 1, tag + "_var", n + 1, tag + "_rstd")

            def head_power(tag, width):
                return lambda n, par: power(rn[:, 0:width], ssc[:, 0:width], width, tag + "_ss", n + 1, tag + "_rn")

            def f_rot(n, par):
                pool.wait_ge(sem("sa_raw"), n * 3 + 3)
                first = qraw[:, :, 0:ROT]
                pairs = first.rearrange("p h (j t) -> p h j t", t=2)
                pb = rotb.rearrange("p h (j t) -> p h j t", t=2)
                sinb = sinT.rearrange("p (j t) -> p j t", t=2).unsqueeze(1).broadcast_to([128, 17, ROT // 2, 2])
                for i in range(2):
                    nc.gpsimd.tensor_tensor(pb[:, :, :, i], pairs[:, :, :, 1 - i], sinb[:, :, :, i], ALU.mult).then_inc(sem("rot_parts"), 1)
                nc.gpsimd.tensor_tensor(rota, first, cosT.unsqueeze(1).broadcast_to([128, 17, ROT]), ALU.mult).then_inc(sem("rot_parts"), 1)
                pool.wait_ge(sem("rot_parts"), n * 3 + 3)
                nc.gpsimd.tensor_tensor(first, rota, rotb, ALU.add).then_inc(sem("sa_rot"), 1)

            def low(tag, half, whole, high):
                def stage(n, par):
                    pool.wait_ge(sem(tag + "_hi"), n + 1)
                    nc.gpsimd.tensor_tensor(half, whole, high, ALU.subtract).then_inc(sem(tag + "_lo"), 1)
                return stage

            def null_weigh(g):
                def stage(n, par):
                    pool.wait_ge(sem("sa_nexp"), n * NG + g + 1)
                    nc.gpsimd.tensor_tensor(Psn[:, g % 2, :], Psn[:, g % 2, :], E0[:, g * QCOL:(g + 1) * QCOL], ALU.mult).then_inc(sem("sa_np"), 1)
                return stage

            pool.wait_ge(sem("E0_ready"), 1)
            drive(pool, PLAN_POOL, {
                "f_rot": f_rot,
                "f_low_sa": low("sa", qs[:, :, 1, :], qn[:], qs[:, :, 0, :]),
                "f_low_ca": low("ca", qs[:, 0:H, 1, :], qn[:, 0:H, :], qs[:, 0:H, 0, :]),
                "f_klow": low("kv", ks[:, :, 1, :], kn[:], ks[:, :, 0, :]),
                **{f"f_snp{g}": null_weigh(g) for g in range(NG)},
                "f_sa": row_power(front, "sa"), "f_sa_q": head_power("sa", 17), "f_out": row_power(front, "sao"),
                "f_ca": row_power(front, "ca"), "f_ca_q": head_power("ca", 16), "f_kv": head_power("kv", 16),
                "b_out": row_power(back, "cao"), "b_ff": row_power(back, "ff"),
            })
            with pool.Fori(0, B // 2) as pair:
                for tags in (("fin",), ("y", "y2"), ("z",)):
                    for k, tag in ((k, tag) for k in range(2) for tag in tags):
                        t = tails[k]
                        power(t.rows.rstd[:], t.rows.ve[:], 1, tag + "_var", pair * 2 + k + 1, tag + "_rstd")

        @block.vector
        def _(dve):
            nc_v = nc.vector

            def layernorm(link, rows, tag, n, src, dst):
                link(nc_v.bn_stats(rows.stats[:], src))
                nc_v.memset(rows.fence[:], 0.0)
                link(nc_v.bn_aggr(rows.mv[:], rows.stats[:]))
                nc_v.tensor_scalar(rows.ve[:], rows.mv[:, 1:2], EPS, None, ALU.add).then_inc(sem(tag + "_var"), 1)
                dve.wait_ge(sem(tag + "_rstd"), n + 1)
                return nc_v.tensor_scalar(dst, src, rows.mv[:, 0:1], rows.rstd[:], ALU.subtract, ALU.mult)

            setup = Links(dve, sem("dve_setup"), 0)
            dve.wait_ge(sem("consts_in"), 16 * 5)
            nc_v.tensor_copy(ident16[:], ident).then_inc(sem("ident16"), 1)
            setup(nc_v.memset(NV[:, :, DH:128], 1.0))
            setup(nc_v.tensor_tensor(nksq[:], nk[:], nk[:], ALU.mult))
            setup(nc_v.tensor_reduce(ss[0:12, 0:1], nksq[:], AX_X, ALU.add))
            nc_v.tensor_scalar(ssc[0:12, 0:1], ss[0:12, 0:1], 1e-24, 1.0 / (UNIT * UNIT), ALU.max, ALU.mult).then_inc(sem("null_ss"), 1)
            dve.wait_ge(sem("null_rn"), 1)
            setup(nc_v.tensor_scalar(nkn[:], nk[:], rn[0:12, 0:1], None, ALU.mult))
            for a in (0, 2):
                setup(nc_v.tensor_copy(nks[:, a, :], nkn[:]))
            nc_v.tensor_tensor(nks[:, 1, :], nkn[:], nks[:, 0, :], ALU.subtract).then_inc(sem("null_split"), 1)
            dve.wait_ge(sem("null_T"), 1)
            nc_v.tensor_copy(NKC[:], psLh[0][:, 0:2, 0:2 * L]).then_inc(sem("NKC"), 1)
            dve.wait_ge(sem("bias_mm"), 1)
            setup(nc_v.tensor_copy(ET[0:H, 128:256], psL[0:H, 1, 0:N]))
            setup(nc_v.tensor_copy(ET[0:H, 512:640], ET[0:H, 128:256]))
            setup(nc_v.tensor_copy(ET[0:H, 0:128], ET[0:H, 128:129].broadcast_to([H, 128])))
            src, dst = 512, 640
            shift = 1
            while shift < N:
                setup(nc_v.tensor_copy(ET[0:H, dst:dst + shift], ET[0:H, src:src + shift]))
                setup(nc_v.tensor_tensor(ET[0:H, dst + shift:dst + N], ET[0:H, src + shift:src + N],
                                         ET[0:H, src:src + N - shift], ALU.max))
                src, dst = dst, src
                shift *= 2
            nc_v.tensor_copy(ET[0:H, 256:384], ET[0:H, src:src + N]).then_inc(sem("bias_ready"), 1)
            nc_v.tensor_tensor(ET[0:H, 384:512], ET[0:H, 128:256], ET[0:H, src:src + N], ALU.subtract).then_inc(sem("bias_ready"), 1)
            dve.wait_ge(sem("x_in"), 16)
            dve.wait_ge(sem("pool_consts"), POOL_CONSTS)
            for b in range(B):
                setup(layernorm(setup, front, "in", b, x_in[:, b, :], xs[:, b, :]))
            for g in range(4):
                dve.wait_ge(sem("flip_mm"), g + 1)
                dve.wait_ge(sem("bias_in"), 64)
                nc_v.tensor_tensor(ET[:, g * 512:(g + 1) * 512], psFour[g],
                                   rowmax[:, g * 512:(g + 1) * 512], ALU.subtract).then_inc(sem("ET_sub"), 1)
            dve.wait_ge(sem("ET_ready"), 1)
            dve.wait_ge(sem("V_ones"), 1)

            links = {}

            def begin(which, n, per):
                links[which] = Links(dve, sem("dve_" + which), n * per)

            def norms(tag, heads):
                def stage(n, par):
                    dve.wait_ge(sem(tag + "_sq"), n + 1)
                    links["front"](nc_v.tensor_reduce(ss[:, 0:heads], qsq[:, 0:heads, :], AX_X, ALU.add))
                    nc_v.tensor_tensor(ssc[:, 0:heads], ss[:, 0:heads], tiny[:, 0:heads], ALU.max).then_inc(sem(tag + "_ss"), 1)
                return stage

            def unit(tag, heads):
                def stage(n, par):
                    dve.wait_ge(sem(tag + "_rn"), n + 1)
                    nc_v.tensor_tensor(qn[:, 0:heads, :], qraw[:, 0:heads, :],
                                       rn[:, 0:heads].unsqueeze(2).broadcast_to([128, heads, DH]), ALU.mult).then_inc(sem(tag + "_qn"), 1)
                return stage

            def out_norm(link, rows, tag, n, src, gain):
                dve.wait_ge(sem(tag + "_wo"), n + 1)
                link(layernorm(link, rows, tag, n, src, rows.xn[:]))
                link(nc_v.tensor_tensor(rows.xn[:], rows.xn[:], gain[:], ALU.mult))
                link(nc_v.tensor_tensor(rows.x[:], rows.x[:], rows.xn[:], ALU.add))

            def norm_rows(link, rows, tag, n):
                layernorm(link, rows, tag, n, rows.x[:], rows.xn[:]).then_inc(sem(tag + "_xn"), 1)

            def turned(rows, tag, k, src):
                def stage(n, par):
                    dve.wait_ge(sem(tag + "_xT"), n + 1)
                    nc_v.tensor_scalar(rows.xnT[:], src, gcol[:, n // B, k:k + 1], None, ALU.mult).then_inc(sem(tag + "_xnT"), 1)
                return stage

            def evacuate(tag, n, h, bank, rd, dst, pv_at):
                def product(k):
                    cols, half = slice((k % GH) * N, (k % GH + 1) * N), 64 * (k % 2)
                    dve.wait_ge(sem(tag + "_rden"), n * H + k + 1)
                    nc_v.tensor_tensor(dst[half:half + 64, k // 2, :], bank[0:64, cols], rd[:, k % 3, :], ALU.mult).then_inc(sem(tag + "_o"), 1)

                if h % GH == 0:
                    dve.wait_ge(sem(tag + "_pv"), pv_at)
                if h >= 3:
                    dve.wait_ge(sem(tag + "_o"), n * H + h - 2)
                nc_v.reciprocal(rd[:, h % 3, :], bank[64:128, (h % GH) * N:(h % GH + 1) * N]).then_inc(sem(tag + "_rden"), 1)
                if h % GH > 0:
                    product(h - 1)
                if h % GH == GH - 1:
                    product(h)

            def core_step(s, core, back):
                step = at(s - LOW, core, back)
                if step is None or is_null(step[0]):
                    return
                t, n, par = step
                dve.wait_ge(sem("p_hi"), n * TILES + tile(t) + 1)
                dve.wait_ge(sem("ca_exp"), n * STEPS + t + 1)
                here = slot(t, par, HSLOTS)
                nc_v.tensor_tensor(PL[:, here, :], P[:, slot(t, par, PSLOTS), :], PH[:, here, :], ALU.subtract).then_inc(sem("p_lo"), 1)

            def f_begin(n, par):
                begin("front", n, FRONT_LINKS)
                link = links["front"]
                link(nc_v.tensor_scalar(front.x[:], xs[:, n % B, :], 1.0, None, ALU.mult))

            def f_null(n, par):
                nc_v.tensor_scalar(nkcs[:], NKC[:, :, n // B], 1.0, None, ALU.mult).then_inc(sem("null_ready"), 1)
                nc_v.tensor_scalar(nkc[:, par], NKC[:, :, n // B + L], 1.0, None, ALU.mult).then_inc(sem("null_ready"), 1)
                nc_v.tensor_scalar(nvs[:], NV[:, n // B, :], 1.0, None, ALU.mult).then_inc(sem("null_ready"), 1)
                nc_v.tensor_scalar(nv[:, par], NV[:, n // B + L, :], 1.0, None, ALU.mult).then_inc(sem("null_ready"), 1)

            def f_KT_sa(n, par):
                dve.wait_ge(sem("sa_kT"), n + 1)
                nc_v.tensor_copy(KTs[:], psLh[0][:, 0:2, :]).then_inc(sem("sa_KT"), 1)

            def weigh(g):
                def stage(n, par):
                    dve.wait_ge(sem("sa_exp"), n * NG + g + 1)
                    nc_v.tensor_tensor(Ps[:, g % 2, :], Ps[:, g % 2, :], ET[:, g * QCOL:(g + 1) * QCOL], ALU.mult).then_inc(sem("sa_p"), 1)
                return stage

            def f_out(n, par):
                out_norm(links["front"], front, "sao", n, psL[:, 0, 0:D], gsa)
                link = links["front"]
                link(nc_v.tensor_scalar(xs[:, n % B, :], front.x[:], 1.0, None, ALU.mult))
                norm_rows(link, front, "ca", n)

            def f_V(t):
                def stage(n, par):
                    dve.wait_ge(sem("kv_proj"), n * 4 + t + 1)
                    v = psL[:, t % 2, :].rearrange("p (a c) -> p a c", c=128)[:, :, DH:128]
                    high = V[:, par, 4 * t:4 * t + 4, 0:DH]
                    nc_v.tensor_copy(high, v).then_inc(sem("kv_vh"), 1)
                    dve.wait_ge(sem("kv_vh"), n * 4 + t + 1)
                    nc_v.tensor_tensor(VL[:, par, 4 * t:4 * t + 4, :], v, high, ALU.subtract).then_inc(sem("kv_v"), 1)
                return stage

            def f_kss(n, par):
                dve.wait_ge(sem("kv_sq"), n + 1)
                links["front"](nc_v.tensor_reduce(ss[:, 0:16], ksq[:], AX_X, ALU.add))
                nc_v.tensor_scalar(ssc[:, 0:16], ss[:, 0:16], 1e-24 / (UNIT * UNIT), None, ALU.max).then_inc(sem("kv_ss"), 1)

            def f_kunit(n, par):
                dve.wait_ge(sem("kv_rn"), n + 1)
                nc_v.tensor_tensor(kn[:], kraw[:], rn[:, 0:16].unsqueeze(2).broadcast_to([128, 16, DH]), ALU.mult).then_inc(sem("kv_kn"), 1)

            def f_KT(part):
                def stage(n, par):
                    dve.wait_ge(sem("kv_T"), n * 4 + 2 * part + 2)
                    ins = nc_v.tensor_copy(KT[:, par, part, 1024:2048], psLh[1].rearrange("p t c -> p (t c)"))
                    ins.then_inc(sem("kv_KT_v"), 1)
                    if part == 1:
                        assert links["front"].k == FRONT_LINKS, links["front"].k
                return stage

            def b_out(n, par):
                begin("back", n, BACK_LINKS)
                link = links["back"]
                link(nc_v.tensor_scalar(back.x[:], xs[:, n % B, :], 1.0, None, ALU.mult))
                out_norm(link, back, "cao", n, psA[:, 0:D], gca)
                norm_rows(link, back, "ff", n)

            def b_one(n, par):
                link = links["back"]
                dve.wait_ge(sem("ff_exp"), n + 1)
                link(nc_v.tensor_scalar(eg1[:], eg[:], 1.0, None, ALU.add))
                link(nc_v.reciprocal(hu[:, 0:FF // 2], eg1[:, 0:FF // 2]))

            def b_silu(n, par):
                link = links["back"]
                link(nc_v.reciprocal(hu[:, FF // 2:FF], eg1[:, FF // 2:FF]))
                nc_v.tensor_tensor(eg1[:], psA[:], hu[:], ALU.mult).then_inc(sem("ff_silu"), 1)

            def b_act(n, par):
                dve.wait_ge(sem("ff_up"), n + 1)
                nc_v.tensor_tensor(hu[:], psA[:], eg1[:], ALU.mult).then_inc(sem("ff_act"), 1)

            def b_end(n, par):
                dve.wait_ge(sem("ff_w2"), n + 1)
                links["back"](nc_v.tensor_tensor(xs[:, n % B, :], back.x[:], psA[:, 0:D], ALU.add))
                assert links["back"].k == BACK_LINKS, links["back"].k

            stages = {
                "f_begin": f_begin, "f_norm_sa": lambda n, par: norm_rows(links["front"], front, "sa", n),
                "f_xnT_sa": turned(front, "sa", 0, psL[:, 0, 0:128]), "f_ss_sa": norms("sa", 17),
                "f_unit_sa": unit("sa", 17), "f_KT_sa": f_KT_sa, "f_null": f_null, "f_out": f_out,
                "f_xnT_ca": turned(front, "ca", 1, psL[:, 0, 0:128]), "f_ss_ca": norms("ca", 16),
                "f_unit_ca": unit("ca", 16), "f_kss": f_kss, "f_kunit": f_kunit,
                "b_out": b_out, "b_xnT": turned(back, "ff", 2, psA[:, 0:128]), "b_one": b_one, "b_silu": b_silu, "b_act": b_act, "b_end": b_end,
            }
            for g in range(NG):
                stages[f"f_sp{g}"] = weigh(g)
                stages[f"f_V{g}"] = f_V(g)
            for part in range(2):
                stages[f"f_KT{part}"] = f_KT(part)
            for h in range(H):
                stages[f"f_se{h}"] = lambda n, par, h=h: evacuate("sa", n, h, psL[:, h // GH % 2, :], rdens, oTs, n * NG + h // GH + 1)
                stages[f"b_e{h}" if h >= H - GH else f"e{h}"] = lambda n, par, h=h: evacuate(
                    "ca", n, h, psO[:, h // GH % 2, :], rden, oT, (n * NG + h // GH + 1) * CA_N)
            drive(dve, PLAN_DVE, stages, core_step)

            def largest(t, b):
                x = t.rows.x[:]
                link(nc_v.tensor_scalar(x, xs[:, b, :], 1.0, None, ALU.mult))
                link(nc_v.tensor_reduce(t.peak[:, 0:1], x, AX_X, ALU.max))
                link(nc_v.reciprocal(t.inv[:, 0:1], t.peak[:, 0:1]))
                link(nc_v.tensor_scalar(x, x, t.inv[:, 0:1], None, ALU.mult))
                layernorm(link, t.rows, "fin", b, x, t.rows.xn[:]).then_inc(sem("fin_xn"), 1)

            def final_gain(t, b):
                dve.wait_ge(sem("fin_xT"), b + 1)
                nc_v.tensor_scalar(t.rows.xnT[:], t.banks[0][:, 0:128], TC[:, C_FINAL:C_FINAL + 1], None, ALU.mult).then_inc(sem("fin_xnT"), 1)

            def attention_in(t, b):
                x = t.rows.x[:]
                dve.wait_ge(sem("fin_proj"), b + 1)
                link(nc_v.tensor_tensor(x, x_in[:, b, :], t.banks[1][:, 0:D], ALU.add))
                link(layernorm(link, t.rows, "y", b, x, t.y))
                layernorm(link, t.rows, "y2", b, t.y, t.rows.xn[:]).then_inc(sem("y2_xn"), 1)
                link(nc_v.tensor_tensor(x, x, t.y, ALU.add))

            def attention_gain(t, b):
                dve.wait_ge(sem("y2_xT"), b + 1)
                nc_v.tensor_scalar(t.rows.xnT[:], t.banks[0][:, 0:128], TC[:, C_LNW:C_LNW + 1], TC[:, C_LNB:C_LNB + 1], ALU.mult, ALU.add).then_inc(sem("y2_xnT"), 1)

            def own_keys(t, b):
                dve.wait_ge(sem("t_qkv"), b + 1)
                link(nc_v.tensor_copy(t.q, t.banks[1][:, 0:128]))
                link(nc_v.tensor_copy(t.v, t.banks[1][:, 256:384]))
                link(nc_v.tensor_copy(t.k, t.banks[1][:, 128:256]))
                nc_v.tensor_tensor(t.km, t.k.unsqueeze(1).broadcast_to([128, H, N]),
                                   hmask.unsqueeze(2).broadcast_to([128, H, N]), ALU.mult).then_inc(sem("t_km"), 1)

            def masked(t, b):
                dve.wait_ge(sem("t_s"), b + 1)
                for c in range(4):
                    ins = nc_v.scalar_tensor_tensor(out=t.s[:, 4 * c:4 * c + 4, :], in0=t.banks[c].rearrange("p (h t) -> p h t", t=N),
                                                    scalar=float(8) ** -0.5, in1=cmask.unsqueeze(1).broadcast_to([128, 4, N]),
                                                    op0=ALU.mult, op1=ALU.add)
                link(ins)
                link(nc_v.tensor_reduce(t.peak[:], t.s, AX_X, ALU.max))
                nc_v.tensor_tensor(t.s, t.s, t.peak[:].unsqueeze(2).broadcast_to([128, H, N]), ALU.subtract).then_inc(sem("t_sub"), 1)

            def sums(t, b):
                dve.wait_ge(sem("t_exp"), b + 1)
                link(nc_v.tensor_reduce(t.sum[:], t.s, AX_X, ALU.add))
                link(nc_v.reciprocal(t.inv[:], t.sum[:]))

            def turned_half(t, b):
                for c in range(2, 4):
                    dve.wait_ge(sem("t_pT"), b * 4 + c + 1)
                    nc_v.tensor_copy(t.km[:, 4 * c:4 * c + 4, :].rearrange("p h t -> p (h t)"), t.banks[c]).then_inc(sem("t_pT_v"), 1)

            def attention_out(t, b):
                dve.wait_ge(sem("t_pv"), b + 1)
                nc_v.tensor_tensor(t.rows.xn[:].rearrange("p (h e) -> p h e", e=8), t.banks[0][:, 0:128].rearrange("p (h e) -> p h e", e=8),
                                   t.inv[:].unsqueeze(2).broadcast_to([128, H, 8]), ALU.mult).then_inc(sem("t_o"), 1)

            def out_columns(t, b):
                dve.wait_ge(sem("t_oT"), b + 1)
                nc_v.tensor_copy(t.rows.xnT[:], t.banks[1][:, 0:128]).then_inc(sem("t_oT_sb"), 1)

            def residual(t, b):
                x = t.rows.x[:]
                dve.wait_ge(sem("t_wo"), b + 1)
                link(nc_v.tensor_tensor(x, x, t.banks[0][:, 0:128], ALU.add))
                link(nc_v.tensor_scalar(x_in[:, b, :], x, 1.0, None, ALU.mult))
                layernorm(link, t.rows, "z", b, x, t.rows.xn[:]).then_inc(sem("z_xn"), 1)

            def z_columns(t, b):
                dve.wait_ge(sem("z_xT"), b + 1)
                link(nc_v.tensor_scalar(zT[:, b, :], t.banks[0][:, 0:128], 1.0, None, ALU.mult))

            dve.wait_ge(sem("tail_in"), 48)
            with dve.Fori(0, B // 2) as pair:
                link = Links(dve, sem("dve_tail"), pair * (2 * TAIL_LINKS))
                for stage in (largest, final_gain, attention_in, attention_gain, own_keys, masked, sums, turned_half,
                              attention_out, out_columns, residual, z_columns):
                    for k, t in enumerate(tails):
                        stage(t, pair * 2 + k)
                assert link.k == 2 * TAIL_LINKS, link.k
            link = Links(dve, sem("dve_rec"), 0)
            nc_v.tensor_copy(cT, TC[:, C_INC:C_INC + 1].broadcast_to([128, 128])).then_inc(sem("c_ready"), 1)
            for t in range(B):
                dve.wait_ge(sem("gate_f"), t + 1)
                dve.wait_ge(sem("c_ready"), t + 1)
                link(nc_v.tensor_tensor(cf, fT, cT, ALU.mult))
                dve.wait_ge(sem("gate_g"), t + 1)
                link(nc_v.tensor_tensor(ig, iT, gT, ALU.mult))
                nc_v.tensor_tensor(cT, cf, ig, ALU.add).then_inc(sem("c_ready"), 1)
            for t in range(B):
                dve.wait_ge(sem("y_tanh"), t + 1)
                nc_v.tensor_tensor(x_in[:, t, :], x_in[:, t, :], hy[:, t, :], ALU.add).then_inc(sem("y_ready"), 1)

        @block.scalar
        def _(act):
            nc_a = nc.scalar
            act.wait_ge(sem("bias_in"), 64)
            nc_a.activation(E0, E0, ACT.Exp).then_inc(sem("E0_ready"), 1)
            for g in range(4):
                act.wait_ge(sem("ET_sub"), g + 1)
                nc_a.activation(ET[:, g * 512:(g + 1) * 512], ET[:, g * 512:(g + 1) * 512], ACT.Exp).then_inc(sem("ET_exp"), 1)
            act.wait_ge(sem("E0_ready"), 1)

            def core_step(s, core, back):
                if core is None:
                    return
                n, par = core
                first = isinstance(n, int) and n == 0
                act.wait_ge(sem("ca_qk"), n * STEPS + s + 1)
                if is_null(s):
                    if s >= CA_N or not first:
                        act.wait_ge(sem("ca_pv"), n * STEPS + s - CA_N + 1)
                    nc_a.activation(Pn[:], psS[0:1, s % SLOTS, :], ACT.Exp, scale=SIM_SCALE).then_inc(sem("ca_exp"), 1)
                    return
                if s >= HSLOTS or not first:
                    act.wait_ge(sem("ca_pv"), n * STEPS + s - HSLOTS + 1)
                nc_a.activation(PH[:, slot(s, par, HSLOTS), :], psS[:, s % SLOTS, :], ACT.Exp, scale=SIM_SCALE).then_inc(sem("p_hi"), 1)
                old = s - PSLOTS
                if old >= 0:
                    act.wait_ge(sem("p_lo"), n * TILES + tile(old) + (0 if is_null(old) else 1))
                elif not first:
                    act.wait_ge(sem("p_lo"), n * TILES - TILES + tile(STEPS + old) + (0 if old == -1 else 1))
                nc_a.activation(P[:, slot(s, par, PSLOTS), :], psS[:, s % SLOTS, :], ACT.Exp, scale=SIM_SCALE).then_inc(sem("ca_exp"), 1)

            def halves(tag, heads):
                def stage(n, par):
                    act.wait_ge(sem(tag + "_qn"), n + 1)
                    if heads == 17:
                        nc_a.activation(ks_self[:, 128:192], qn[:, 16, :], ACT.Copy)
                    nc_a.activation(qs[:, 0:heads, 0, :], qn[:, 0:heads, :], ACT.Copy).then_inc(sem(tag + "_hi"), 1)
                return stage

            def queries(tag):
                def stage(n, par):
                    dst = QTs[:] if tag == "sa" else QT[:, par]
                    for i in range(2):
                        act.wait_ge(sem(tag + "_qT"), n * 2 + i + 1)
                        nc_a.activation(dst[:, i * 1024:(i + 1) * 1024], psLh[i].rearrange("p t c -> p (t c)"), ACT.Copy).then_inc(sem(tag + "_QT"), 1)
                return stage

            def raw(i, bank):
                return nc_a.activation(qraw[:, 8 * i:8 * i + 8, :].rearrange("p h d -> p (h d)"), bank, ACT.Copy)

            def f_raw_sa(n, par):
                act.wait_ge(sem("sa_proj"), n * 3 + 1)
                nc_a.activation(qraw[:, 16, :], psL[:, 1, 0:DH], ACT.Copy)
                nc_a.activation(Vs[:, 0:DH], psL[:, 1, DH:128], ACT.Copy).then_inc(sem("sa_raw"), 1)
                act.wait_ge(sem("sa_proj"), n * 3 + 2)
                raw(0, psL[:, 0, :]).then_inc(sem("sa_raw"), 1)

            def f_raw_sa2(n, par):
                act.wait_ge(sem("sa_proj"), n * 3 + 3)
                raw(1, psL[:, 1, :]).then_inc(sem("sa_raw"), 1)

            def f_raw_ca(n, par):
                for i in range(2):
                    act.wait_ge(sem("ca_proj"), n * 2 + i + 1)
                    raw(i, psL[:, i, :]).then_inc(sem("ca_raw"), 1)

            def f_sq_sa(n, par):
                act.wait_ge(sem("sa_rot"), n + 1)
                nc_a.activation(qsq[:], qraw[:], ACT.Square, scale=1.0 / UNIT).then_inc(sem("sa_sq"), 1)

            def f_sq_ca(n, par):
                act.wait_ge(sem("ca_raw"), n * 2 + 2)
                nc_a.activation(qsq[:, 0:16, :], qraw[:, 0:16, :], ACT.Square, scale=1.0 / UNIT).then_inc(sem("ca_sq"), 1)

            def self_exp(g, null):
                def stage(n, par):
                    if null:
                        act.wait_ge(sem("sa_nqk"), n * NG + g + 1)
                        nc_a.activation(Psn[:, g % 2, :], psL[0:1, g % 2, :], ACT.Exp, scale=SIM_SCALE).then_inc(sem("sa_nexp"), 1)
                    else:
                        act.wait_ge(sem("sa_qk"), n * NG + g + 1)
                        nc_a.activation(Ps[:, g % 2, :], psL[:, g % 2, :], ACT.Exp, scale=SIM_SCALE).then_inc(sem("sa_exp"), 1)
                return stage

            def f_kraw(t):
                def stage(n, par):
                    act.wait_ge(sem("kv_v"), n * 4 + t + 1)
                    nc_a.activation(kraw[:, 4 * t:4 * t + 4, :],
                                    psL[:, t % 2, :].rearrange("p (a c) -> p a c", c=128)[:, :, 0:DH], ACT.Copy).then_inc(sem("kv_raw"), 1)
                return stage

            def f_ksq(n, par):
                act.wait_ge(sem("kv_raw"), n * 4 + 4)
                nc_a.activation(ksq[:], kraw[:], ACT.Square, scale=1.0 / UNIT).then_inc(sem("kv_sq"), 1)

            def f_khi(n, par):
                act.wait_ge(sem("kv_kn"), n + 1)
                for a in (0, 2):
                    ins = nc_a.activation(ks[:, :, a, :], kn[:], ACT.Copy)
                ins.then_inc(sem("kv_hi"), 1)

            def f_KT(part):
                def stage(n, par):
                    act.wait_ge(sem("kv_T"), n * 4 + 2 * part + 1)
                    nc_a.activation(KT[:, par, part, 0:1024], psLh[0].rearrange("p t c -> p (t c)"), ACT.Copy).then_inc(sem("kv_KT_a"), 1)
                return stage

            def b_exp(n, par):
                act.wait_ge(sem("ff_gate"), n + 1)
                nc_a.activation(eg[:], psA[:], ACT.Exp, scale=-1.0).then_inc(sem("ff_exp"), 1)

            def b_hT(n, par):
                act.wait_ge(sem("ff_hT"), n + 1)
                nc_a.activation(hT[:], psA[:], ACT.Copy).then_inc(sem("ff_hT_sb"), 1)

            stages = {
                "f_raw_sa": f_raw_sa, "f_raw_sa2": f_raw_sa2, "f_sq_sa": f_sq_sa, "f_hi_sa": halves("sa", 17), "f_QT_sa": queries("sa"),
                "f_raw_ca": f_raw_ca, "f_sq_ca": f_sq_ca, "f_hi_ca": halves("ca", 16), "f_QT_ca": queries("ca"),
                "f_ksq": f_ksq, "f_khi": f_khi, "b_exp": b_exp, "b_hT": b_hT,
            }
            for g in range(NG):
                stages[f"f_se{g}"] = self_exp(g, False)
                stages[f"f_sne{g}"] = self_exp(g, True)
                stages[f"f_kraw{g}"] = f_kraw(g)
            for part in range(2):
                stages[f"f_KT{part}"] = f_KT(part)
            drive(act, PLAN_ACT, stages, core_step)

            with act.Fori(0, B // 2) as pair:
                for k, t in enumerate(tails):
                    act.wait_ge(sem("t_sub"), pair * 2 + k + 1)
                    nc_a.activation(t.s, t.s, ACT.Exp).then_inc(sem("t_exp"), 1)
                for k, t in enumerate(tails):
                    for c in range(2):
                        act.wait_ge(sem("t_pT"), (pair * 2 + k) * 4 + c + 1)
                        nc_a.activation(t.km[:, 4 * c:4 * c + 4, :].rearrange("p h t -> p (h t)"), t.banks[c], ACT.Copy).then_inc(sem("t_pT_a"), 1)
            for t in range(B):
                act.wait_ge(sem("gates"), t + 1)
                if t > 0:
                    act.wait_ge(sem("c_ready"), t + 1)
                nc_a.activation(fT, psA[:, 0:128], ACT.Sigmoid, bias=TC[:, C_BF:C_BF + 1]).then_inc(sem("gate_f"), 1)
                nc_a.activation(iT, psA[:, 128:256], ACT.Sigmoid, bias=TC[:, C_BI:C_BI + 1])
                nc_a.activation(gT, psA[:, 256:384], ACT.Tanh, bias=TC[:, C_BC:C_BC + 1]).then_inc(sem("gate_g"), 1)
            for t in range(B):
                act.wait_ge(sem("y_mm"), t + 1)
                nc_a.activation(hy[:, t, :], psFour[t][:, 0:128], ACT.Tanh).then_inc(sem("y_tanh"), 1)

        @block.tensor
        def _(pe):
            mm = nc.tensor.matmul
            pe.wait_ge(sem("ident16"), 1)
            pe.wait_ge(sem("consts_in"), 16 * 5)
            pe.wait_ge(sem("null_split"), 1)
            for i in range(2):
                ins = nc.tensor.transpose(psLh[0][:, i, 0:2 * L], nks[:, i:i + 2].rearrange("p a d -> p (a d)"), ident16[0:2 * L, 0:2 * L])
            ins.then_inc(sem("null_T"), 1)
            mm(psL[0:H, 1, 0:N], emb_sb[:], onehot, start=True, stop=True).then_inc(sem("bias_mm"), 1)
            pe.wait_ge(sem("bias_in"), 64)
            for g in range(4):
                mm(psFour[g], flip, toeplitz[g // 2][:, (g % 2) * 512:(g % 2) * 512 + 512], start=True, stop=True).then_inc(sem("flip_mm"), 1)

            def turn_x(rows, tag, bank, n):
                pe.wait_ge(sem(tag + "_xn"), n + 1)
                nc.tensor.transpose(bank[:, 0:128], rows.xn[:], ident).then_inc(sem(tag + "_xT"), 1)

            def turn_q(tag):
                def stage(n, par):
                    pe.wait_ge(sem(tag + "_lo"), n + 1)
                    for i in range(2):
                        for h in range(8):
                            ins = nc.tensor.transpose(psLh[i][:, h, :], qs[:, 8 * i + h].rearrange("p a d -> p (a d)"), ident16[:])
                        ins.then_inc(sem(tag + "_qT"), 1)
                return stage

            def scores(bank, rows, keys, q):
                for part in range(2):
                    ins = mm(bank[0:rows, :], keys[part], q, start=(part == 0), stop=(part == 1))
                return ins

            def core_step(s, core, back):
                if core is not None:
                    n, par = core
                    first = isinstance(n, int) and n == 0
                    if s == 0:
                        pe.wait_ge(sem("ca_QT"), n * 2 + 2)
                        pe.wait_ge(sem("kv_KT_a"), n * 2 + 2)
                        pe.wait_ge(sem("kv_KT_v"), n * 2 + 2)
                        pe.wait_ge(sem("null_ready"), (n + 1) * 4)
                        pe.wait_ge(sem("kv_v"), n * 4 + 4)
                    if s >= SLOTS:
                        pe.wait_ge(sem("ca_exp"), n * STEPS + s - SLOTS + 1)
                    elif not first:
                        pe.wait_ge(sem("ca_exp"), n * STEPS - (STEPS - 1 - max(t for t in range(STEPS - SLOTS, STEPS) if t % SLOTS == s)))
                    g, j = s // CA_N, s % CA_N
                    keys = [nkc[:, par, p:p + 1] if is_null(s) else KT[:, par, p, 128 * j:128 * j + 128] for p in range(2)]
                    scores(psS[:, s % SLOTS, :], 1 if is_null(s) else 128, keys, QT[:, par, g * QCOL:(g + 1) * QCOL]).then_inc(sem("ca_qk"), 1)
                step = at(s - AHEAD, core, back)
                if step is None:
                    return
                t, n, par = step
                g, j = t // CA_N, t % CA_N
                bank, here = psO[:, g % 2, :], slot(t, par, HSLOTS)
                if j == 0 and (g >= 2 or not isinstance(n, int) or n > 0):
                    pe.wait_ge(sem("ca_o"), n * H + GH * (g - 1))
                if is_null(t):
                    pe.wait_ge(sem("ca_exp"), n * STEPS + t + 1)
                    ins = mm(bank, nv[:, par], Pn[:], start=False, stop=True)
                else:
                    pe.wait_ge(sem("p_hi"), n * TILES + tile(t) + 1)
                    mm(bank, V[:, par, j, :], PH[:, here, :], start=(j == 0), stop=False)
                    mm(bank[0:DH, :], VL[:, par, j, :], PH[:, here, :], start=False, stop=False)
                    pe.wait_ge(sem("p_lo"), n * TILES + tile(t) + 1)
                    ins = mm(bank, V[:, par, j, :], PL[:, here, :], start=False, stop=False)
                ins.then_inc(sem("ca_pv"), 1)

            def weights(a, b):
                return W[:, a:b]

            def f_proj_sa(n, par):
                pe.wait_ge(sem("w_front"), (n // B + 1) * 32)
                pe.wait_ge(sem("sa_xnT"), n + 1)
                mm(psL[:, 1, 0:128], front.xnT[:], weights(W_SAKV, W_SAKV + 128), start=True, stop=True).then_inc(sem("sa_proj"), 1)
                mm(psL[:, 0, :], front.xnT[:], weights(W_SAQ, W_SAQ + 512), start=True, stop=True).then_inc(sem("sa_proj"), 1)

            def f_proj_sa2(n, par):
                pe.wait_ge(sem("sa_raw"), n * 3 + 1)
                mm(psL[:, 1, :], front.xnT[:], weights(W_SAQ + 512, W_SAQ + 1024), start=True, stop=True).then_inc(sem("sa_proj"), 1)

            def f_turn_k_sa(n, par):
                pe.wait_ge(sem("sa_QT"), n * 2 + 1)
                for i in range(2):
                    ins = nc.tensor.transpose(psLh[0][:, i, :], ks_self[:, DH * i:DH * i + 128], ident16[:])
                ins.then_inc(sem("sa_kT"), 1)

            def self_key(g):
                def stage(n, par):
                    pe.wait_ge(sem("sa_QT"), n * 2 + 2)
                    pe.wait_ge(sem("sa_KT"), n + 1)
                    if g >= 2:
                        pe.wait_ge(sem("sa_o"), n * H + GH * (g - 1))
                    scores(psL[:, g % 2, :], 128, [KTs[:, p, :] for p in range(2)], QTs[:, g * QCOL:(g + 1) * QCOL]).then_inc(sem("sa_qk"), 1)
                return stage

            def self_null(g):
                def stage(n, par):
                    pe.wait_ge(sem("null_ready"), (n + 1) * 4)
                    pe.wait_ge(sem("sa_exp"), n * NG + g + 1)
                    scores(psL[:, g % 2, :], 1, [nkcs[:, p:p + 1] for p in range(2)], QTs[:, g * QCOL:(g + 1) * QCOL]).then_inc(sem("sa_nqk"), 1)
                return stage

            def self_sum(g):
                def stage(n, par):
                    pe.wait_ge(sem("sa_p"), n * NG + g + 1)
                    pe.wait_ge(sem("sa_np"), n * NG + g + 1)
                    mm(psL[:, g % 2, :], Vs[:], Ps[:, g % 2, :], start=True, stop=False)
                    mm(psL[:, g % 2, :], nvs[:], Psn[:, g % 2, :], start=False, stop=True).then_inc(sem("sa_pv"), 1)
                return stage

            def project_out(bank, o, tag, done, w):
                def stage(n, par):
                    if tag == "ca":
                        pe.wait_ge(sem("w_back"), (n // B + 1) * 32)
                    pe.wait_ge(sem(tag + "_o"), (n + 1) * H)
                    for c in range(H // 2):
                        ins = mm(bank[:, 0:D], o[:, c, :], weights(w + c * D, w + (c + 1) * D), start=(c == 0), stop=(c == H // 2 - 1))
                    ins.then_inc(sem(done), 1)
                return stage

            def f_proj_ca(n, par):
                pe.wait_ge(sem("ca_xnT"), n + 1)
                for i in range(2):
                    mm(psL[:, i, :], front.xnT[:], weights(W_CAQ + 512 * i, W_CAQ + 512 * i + 512), start=True, stop=True).then_inc(sem("ca_proj"), 1)

            def f_kv(t):
                def stage(n, par):
                    pe.wait_ge(sem("ctx_in"), n * 16 + 16)
                    if t >= 2:
                        pe.wait_ge(sem("kv_raw"), n * 4 + t - 1)
                    else:
                        pe.wait_ge(sem("sa_raw"), n * 3 + 2 + t)
                    for a in range(4):
                        k = 4 * t + a
                        ins = mm(psL[:, t % 2, a * 128:(a + 1) * 128], ctx_sb[:, k * 128:(k + 1) * 128],
                                 weights(W_CAKV, W_CAKV + 128), start=True, stop=True)
                    ins.then_inc(sem("kv_proj"), 1)
                return stage

            def f_turn_q_sa(n, par):
                pe.wait_ge(sem("kv_raw"), n * 4 + 4)
                turn_q("sa")(n, par)

            def f_turn_q_ca(n, par):
                pe.wait_ge(sem("kv_KT_a"), n * 2 + 2)
                pe.wait_ge(sem("kv_KT_v"), n * 2 + 2)
                turn_q("ca")(n, par)

            def f_turn_k(part):
                def stage(n, par):
                    pe.wait_ge(sem("kv_lo"), n + 1)
                    for i in range(2):
                        if part == 1:
                            pe.wait_ge(sem("kv_KT_a" if i == 0 else "kv_KT_v"), n * 2 + 1)
                        else:
                            pe.wait_ge(sem("ca_raw"), n * 2 + i + 1)
                        for t in range(8):
                            ins = nc.tensor.transpose(psLh[i][:, t, :], ks[:, 8 * i + t, part:part + 2, :].rearrange("p a d -> p (a d)"), ident16[:])
                        ins.then_inc(sem("kv_T"), 1)
                return stage

            def b_gate(n, par):
                pe.wait_ge(sem("ff_xnT"), n + 1)
                mm(psA[:], back.xnT[:], weights(W_FF1 + 512, W_FF1 + 1024), start=True, stop=True).then_inc(sem("ff_gate"), 1)

            def b_up(n, par):
                pe.wait_ge(sem("ff_silu"), n + 1)
                mm(psA[:], back.xnT[:], weights(W_FF1, W_FF1 + 512), start=True, stop=True).then_inc(sem("ff_up"), 1)

            def b_turn_h(n, par):
                pe.wait_ge(sem("ff_act"), n + 1)
                for c in range(4):
                    ins = nc.tensor.transpose(psA[:, c * 128:(c + 1) * 128], hu[:, c * 128:(c + 1) * 128], ident)
                ins.then_inc(sem("ff_hT"), 1)

            def b_down(n, par):
                pe.wait_ge(sem("ff_hT_sb"), n + 1)
                for c in range(4):
                    ins = mm(psA[:, 0:D], hT[:, c * 128:(c + 1) * 128], weights(W_FF2 + c * D, W_FF2 + (c + 1) * D),
                             start=(c == 0), stop=(c == 3))
                ins.then_inc(sem("ff_w2"), 1)

            stages = {
                "f_turn_sa": lambda n, par: turn_x(front, "sa", psL[:, 0, :], n), "f_proj_sa": f_proj_sa, "f_proj_sa2": f_proj_sa2,
                "f_turn_q_sa": f_turn_q_sa, "f_turn_k_sa": f_turn_k_sa,
                "f_wo": project_out(psL[:, 0, :], oTs, "sa", "sao_wo", W_SAO),
                "f_turn_ca": lambda n, par: turn_x(front, "ca", psL[:, 0, :], n), "f_proj_ca": f_proj_ca, "f_turn_q_ca": f_turn_q_ca,
                "b_wo": project_out(psA[:], oT, "ca", "cao_wo", W_CAO),
                "b_turn": lambda n, par: turn_x(back, "ff", psA[:], n),
                "b_gate": b_gate, "b_up": b_up, "b_turn_h": b_turn_h, "b_down": b_down,
            }
            for g in range(NG):
                stages[f"f_sk{g}"] = self_key(g)
                stages[f"f_sn{g}"] = self_null(g)
                stages[f"f_sv{g}"] = self_sum(g)
                stages[f"f_kv{g}"] = f_kv(g)
            for part in range(2):
                stages[f"f_turn_k{part}"] = f_turn_k(part)
            drive(pe, PLAN_PE, stages, core_step)

            def tail_w(k):
                return TW[:, k, :]

            pe.wait_ge(sem("tail_in"), 48)

            def proj(t, b):
                pe.wait_ge(sem("fin_xnT"), b + 1)
                mm(t.banks[1][:, 0:D], t.rows.xnT[:], tail_w(T_PROJ), start=True, stop=True).then_inc(sem("fin_proj"), 1)

            def qkv(t, b):
                pe.wait_ge(sem("y2_xnT"), b + 1)
                mm(t.banks[1][:, 0:128], tail_w(T_Q), t.rows.xnT[:], start=True, stop=True)
                mm(t.banks[1][:, 128:256], tail_w(T_K), t.rows.xnT[:], start=True, stop=True)
                mm(t.banks[1][:, 256:384], t.rows.xnT[:], tail_w(T_V), start=True, stop=True).then_inc(sem("t_qkv"), 1)

            def tail_scores(t, b):
                pe.wait_ge(sem("t_km"), b + 1)
                for c in range(4):
                    ins = mm(t.banks[c], t.q, t.km[:, 4 * c:4 * c + 4, :].rearrange("p h t -> p (h t)"), start=True, stop=True)
                ins.then_inc(sem("t_s"), 1)

            def turn_probs(t, b):
                pe.wait_ge(sem("t_exp"), b + 1)
                for c in range(4):
                    for h in range(4 * c, 4 * c + 4):
                        ins = nc.tensor.transpose(t.banks[c][:, (h % 4) * 128:(h % 4) * 128 + 128], t.s[:, h, :], ident)
                    ins.then_inc(sem("t_pT"), 1)

            def tail_sums(t, b):
                pe.wait_ge(sem("t_pT_a"), b * 2 + 2)
                pe.wait_ge(sem("t_pT_v"), b * 2 + 2)
                for h in range(H):
                    ins = mm(t.banks[0][:, 8 * h:8 * h + 8], t.km[:, h, :], t.v[:, 8 * h:8 * h + 8], start=True, stop=True)
                ins.then_inc(sem("t_pv"), 1)

            def turn_out(t, b):
                pe.wait_ge(sem("t_o"), b + 1)
                nc.tensor.transpose(t.banks[1][:, 0:128], t.rows.xn[:], ident).then_inc(sem("t_oT"), 1)

            def project_tail(t, b):
                pe.wait_ge(sem("t_oT_sb"), b + 1)
                mm(t.banks[0][:, 0:D], t.rows.xnT[:], tail_w(T_O), start=True, stop=True).then_inc(sem("t_wo"), 1)

            with pe.Fori(0, B // 2) as pair:
                for stage in (lambda t, b: turn_x(t.rows, "fin", t.banks[0], b), proj,
                              lambda t, b: turn_x(t.rows, "y2", t.banks[0], b), qkv, tail_scores, turn_probs, tail_sums,
                              turn_out, project_tail, lambda t, b: turn_x(t.rows, "z", t.banks[0], b)):
                    for k, t in enumerate(tails):
                        stage(t, pair * 2 + k)
            pe.wait_ge(sem("dve_tail"), B * TAIL_LINKS)
            for t in range(B):
                pe.wait_ge(sem("c_ready"), t + 1)
                if t > 0:
                    pe.wait_ge(sem("gate_g"), t)
                for k, (w, u) in enumerate(((T_WF, T_UF), (T_WI, T_UI), (T_WC, T_UC))):
                    mm(psA[:, 128 * k:128 * k + 128], tail_w(w), zT[:, t, :], start=True, stop=False)
                    ins = mm(psA[:, 128 * k:128 * k + 128], tail_w(u), cT, start=False, stop=True)
                ins.then_inc(sem("gates"), 1)
            pe.wait_ge(sem("c_ready"), B + 1)
            for t in range(B):
                mm(psFour[t][:, 0:128], zT[:, t, :], tail_w(T_WO), start=True, stop=False)
                mm(psFour[t][:, 0:128], cT, tail_w(T_UO), start=False, stop=False)
                mm(psFour[t][:, 0:128], ones[:], bo_row[:], start=False, stop=True).then_inc(sem("y_mm"), 1)


_OUTS = [((4, 128, 128), 'float32')]


def constants(np):
    c = np.zeros((128, C_END), np.float32)
    c[:, 0:128] = np.eye(128)
    c[:, 128:256] = np.eye(128)[::-1]
    c[:, 256:384] = np.where(np.arange(128)[None, :] > np.arange(128)[:, None], -3.0e38, 0.0)
    neg = np.arange(N)
    safe = np.maximum(neg, 1).astype(np.float32)
    large = 16 + (np.log(safe / np.float32(16)) / np.float32(np.log(128 / 16)) * np.float32(16)).astype(np.int32)
    bucket = np.where(neg < 16, neg, np.minimum(large, NBUCK - 1))
    c[bucket, 384 + neg] = 1.0
    inv = (1.0 / 10000.0 ** (np.arange(0, ROT, 2, dtype=np.float32) / ROT)).astype(np.float32)
    f = np.arange(N, dtype=np.float32)[:, None] * inv[None, :]
    c[:, 512:544] = np.repeat(np.cos(f), 2, axis=-1)
    c[:, 544:576] = np.stack((-np.sin(f), np.sin(f)), -1).reshape(N, ROT)
    c[:, 576:592] = np.arange(128)[:, None] // 8 == np.arange(16)[None, :]
    return c


def kernel(**inputs):
    import numpy as np
    import concourse.bacc as _bacc
    from concourse.bass_utils import run_bass_kernel_spmd as _run

    t = {k: np.asarray(v) for k, v in inputs.items()}
    xa = {k[9:]: v for k, v in t.items() if k.startswith("L0_xattn_")}
    at = {k[8:]: v for k, v in t.items() if k.startswith("L0_attn_")}
    ff = {k[7:]: v for k, v in t.items() if k.startswith("L0_ffn_")}

    def rows(w, c):
        return w.reshape(L, c, 128, -1).transpose(0, 2, 1, 3).reshape(L, 128, -1)

    def heads(w):
        return w.transpose(1, 0, 2).reshape(128, 128)

    arrays = {
        "x": t["x"],
        "ctxT": t["ctx_1024"].transpose(0, 2, 1),
        "wpack": np.concatenate([xa["sa_wq"], xa["sa_wkv"], rows(xa["sa_wo"], 8), xa["ca_wq"], xa["ca_wkv"],
                                 rows(xa["ca_wo"], 8), xa["ff_w1"], rows(xa["ff_w2"], 4)], axis=2),
        "gcols": np.stack([xa["sa_norm_g"], xa["ca_norm_g"], xa["ff_norm_g"]], 1).transpose(2, 0, 1),
        "gout": np.stack([xa["sa_out_g"], xa["ca_out_g"]], 1),
        "null_k": np.concatenate([xa["sa_null_kv"][:, 0], xa["ca_null_kv"][:, 0]], 0),
        "null_v": np.concatenate([xa["sa_null_kv"][:, 1], xa["ca_null_kv"][:, 1]], 0)[None],
        "tail_w": np.stack([xa["proj_w"], heads(at["wq"]), heads(at["wk"]), heads(at["wv"]), at["wo"],
                            ff["wf"].T, ff["wi"].T, ff["wc"].T, ff["uf"].T, ff["ui"].T, ff["uc"].T,
                            ff["wo"].T, ff["uo"].T], 1),
        "tail_cols": np.stack([xa["final_g"], at["ln_w"], at["ln_b"], ff["bf"], ff["bi"], ff["bc"], ff["in_c"]], 1),
        "bo": ff["bo"][None],
        "emb": xa["rel_pos_emb"],
        "c_pack": constants(np),
    }
    arrays = {k: np.ascontiguousarray(v) for k, v in arrays.items()}
    nc = _bacc.Bacc("TRN2", target_bir_lowering=False, num_devices=1)
    args = [nc.dram_tensor(k, v.shape, mybir.dt.from_np(v.dtype), kind="ExternalInput").ap() for k, v in arrays.items()]
    outs = [nc.dram_tensor(f"out_{i}", shape, mybir.dt.from_np(np.dtype(d)), kind="ExternalOutput").ap()
            for i, (shape, d) in enumerate(_OUTS)]
    build(nc, *args, *outs)
    r = _run(nc, [arrays], core_ids=[0])
    return r.results[0]["out_0"]
```
